# Optimizing a Trainium2 kernel written in Bass

```python
import numpy as np
import jax
import jax.numpy as jnp

def _softmax(x, axis=-1):
    return jax.nn.softmax(x, axis=axis)

def _gelu(x):
    return jax.nn.gelu(x, approximate=True)

def _silu(x):
    return jax.nn.silu(x)

def _sigmoid(x):
    return jax.nn.sigmoid(x)

def _layernorm(x, axis=-1, eps=1e-05):
    m = jnp.mean(x, axis=axis, keepdims=True)
    v = jnp.var(x, axis=axis, keepdims=True)
    return (x - m) / jnp.sqrt(v + eps)

def _scatter_add(tgt, idx, src, axis=0):
    return tgt.at[idx].add(src)

def _segment_sum(src, seg, n):
    return jax.ops.segment_sum(src, seg, n)
kernel_name = 'mk_seq_postln_d2_jaxref_r4_39dff5'

def setup_inputs(seed: int=0):
    np.random.seed(seed)
    _w = jnp.asarray

    def _L0_attn_setup():
        import jax, jax.numpy as jnp
        import numpy as np
        B, S, DIN, DIM = (1, 1024, 256, 256)
        NH, NKV = (16, 4)
        HD = DIM // NH
        GS = NH // NKV
        key = jax.random.key(seed)
        ks = jax.random.split(key, 5)

        def w(k, shape, fan_in):
            return jax.random.normal(k, shape, jnp.float32) * fan_in ** (-0.5)
        return {'x': jax.random.normal(ks[0], (B, S, DIN), jnp.float32), 'wq': w(ks[1], (DIM, DIN), DIN), 'wk': w(ks[2], (NKV * HD, DIN), DIN), 'wv': w(ks[3], (NKV * HD, DIN), DIN), 'wo': w(ks[4], (DIM, DIM), DIM)}
    _L0_attn_in = _L0_attn_setup()

    def _L0_ffn_setup():
        import jax, jax.numpy as jnp
        import numpy as np
        B, T, C = (8, 512, 256)
        H = 1024
        E = 8
        K = 2
        LOAD_FACTOR = 1.2
        N_LAYER = 12

        def _get_expert_inputs(x, logits, expert_capacity):
            Tt = logits.shape[0]
            Cc = x.shape[1]
            top_k_logits, expert_indices = jax.lax.top_k(logits, K)
            expert_probs = jax.nn.softmax(top_k_logits, axis=-1)
            ei = jnp.swapaxes(expert_indices, 0, 1).ravel()
            one_hot = jax.nn.one_hot(ei, E, dtype=jnp.int32)
            pos = jnp.cumsum(one_hot, axis=0) * one_hot - 1
            pos = pos.reshape(-1, Tt, E)
            pos = jnp.swapaxes(pos, 0, 1)
            pos = jnp.max(pos, axis=2)
            ei = jnp.swapaxes(ei.reshape(-1, Tt), 0, 1)
            buf = jnp.zeros((E, expert_capacity, Cc), x.dtype)
            xr = jnp.repeat(x, K, axis=0)
            expert_inputs = buf.at[ei.ravel(), pos.ravel()].add(xr)
            return (expert_probs, pos, ei, expert_inputs)
        key = jax.random.key(seed)
        ks = jax.random.split(key, 9)
        std = 0.02
        proj_std = 0.02 * (2 * N_LAYER) ** (-0.5)
        return {'x': jax.random.normal(ks[0], (B, T, C), jnp.float32), 'router_w': jax.random.normal(ks[1], (C, E), jnp.float32) * std, 'router_b': jnp.zeros((E,), jnp.float32), 'w_c_fc': jax.random.normal(ks[2], (E, C, H), jnp.float32) * std, 'b_c_fc': jnp.zeros((E, 1, H), jnp.float32), 'w_gate': jax.random.normal(ks[3], (E, C, H), jnp.float32) * std, 'b_gate': jnp.zeros((E, 1, H), jnp.float32), 'w_c_proj': jax.random.normal(ks[4], (E, H, C), jnp.float32) * proj_std, 'b_c_proj': jnp.zeros((E, 1, C), jnp.float32)}
    _L0_ffn_in = _L0_ffn_setup()

    def _L1_attn_setup():
        import jax, jax.numpy as jnp
        import numpy as np
        N_HEAD = 16
        PAGE_SIZE = 64
        ROPE_THETA = 10000.0

        def _rope_tables(T, D, dtype):
            inv = 1.0 / ROPE_THETA ** (np.arange(0, D, 2, dtype=np.float32) / D)
            ang = np.outer(np.arange(T, dtype=np.float32), inv)
            return (jnp.asarray(np.cos(ang), dtype), jnp.asarray(np.sin(ang), dtype))

        def _apply_rope(x, cos, sin):
            x1 = x[..., 0::2]
            x2 = x[..., 1::2]
            c = cos[None, :, None, :]
            s = sin[None, :, None, :]
            out = jnp.stack([x1 * c - x2 * s, x1 * s + x2 * c], axis=-1)
            return out.reshape(x.shape)
        key = jax.random.key(seed)
        ks = jax.random.split(key, 6)
        B, T, E = (2, 512, 256)
        L = E // 2
        sc = lambda fan: 1.0 / np.sqrt(fan)
        return {'x': jax.random.normal(ks[0], (B, T, E), jnp.float32), 'wq': jax.random.normal(ks[1], (E, E), jnp.float32) * sc(E), 'w_down': jax.random.normal(ks[2], (E, L), jnp.float32) * sc(E), 'wk_up': jax.random.normal(ks[3], (L, E), jnp.float32) * sc(L), 'wv_up': jax.random.normal(ks[4], (L, E), jnp.float32) * sc(L), 'wo': jax.random.normal(ks[5], (E, E), jnp.float32) * sc(E)}
    _L1_attn_in = _L1_attn_setup()

    def _L1_ffn_setup():
        import jax, jax.numpy as jnp
        import numpy as np
        DIM = 256
        DEPTH = 2
        HEADS = 8
        DIM_HEAD = 64
        WINDOW = 128
        INNER = HEADS * DIM_HEAD
        HID = int(DIM * 4 * 2 / 3)
        B, N = (2, 2048)
        QK_SCALE = 8.0

        def shift_token(t):
            t1, t2 = jnp.split(t, 2, axis=-1)
            t2 = jnp.pad(t2, ((0, 0), (1, 0), (0, 0)))[:, :-1]
            return jnp.concatenate([t1, t2], axis=-1)

        def l2norm(t):
            return t / jnp.clip(jnp.linalg.norm(t, axis=-1, keepdims=True), 1e-12)

        def rotate_half(x):
            x1, x2 = jnp.split(x, 2, axis=-1)
            return jnp.concatenate([-x2, x1], axis=-1)

        def rotary_xpos(q, k):
            n = q.shape[-2]
            half_idx = jnp.arange(0, DIM_HEAD, 2, dtype=jnp.float32)
            inv_freq = 1.0 / 10000.0 ** (half_idx / DIM_HEAD)
            t = jnp.arange(n, dtype=jnp.float32)
            freqs = t[:, None] * inv_freq[None, :]
            freqs = jnp.concatenate([freqs, freqs], axis=-1)
            base = (half_idx + 0.4 * DIM_HEAD) / (1.4 * DIM_HEAD)
            power = (t - n // 2) / float(WINDOW // 2)
            scale = base[None, :] ** power[:, None]
            scale = jnp.concatenate([scale, scale], axis=-1)
            cos, sin = (jnp.cos(freqs), jnp.sin(freqs))
            q = q * cos * scale + rotate_half(q) * sin * scale
            k = k * cos / scale + rotate_half(k) * sin / scale
            return (q, k)

        def local_attention(q, k, v):
            b, h, n, d = q.shape
            w = n // WINDOW
            bq = q.reshape(b, h, w, WINDOW, d) * QK_SCALE
            bk = k.reshape(b, h, w, WINDOW, d)
            bv = v.reshape(b, h, w, WINDOW, d)

            def look_around(t):
                p = jnp.pad(t, ((0, 0), (0, 0), (1, 0), (0, 0), (0, 0)))
                return jnp.concatenate([p[:, :, :w], p[:, :, 1:]], axis=3)
            bk, bv = (look_around(bk), look_around(bv))
            bt = jnp.arange(n).reshape(w, WINDOW)
            btp = jnp.pad(bt, ((1, 0), (0, 0)), constant_values=-1)
            btk = jnp.concatenate([btp[:w], btp[1:]], axis=1)
            sim = jnp.einsum('bhwid,bhwjd->bhwij', bq, bk)
            i = bt[:, :, None]
            j = btk[:, None, :]
            mask = (i < j) | (i > j + WINDOW) | (j == -1)
            sim = jnp.where(mask, -jnp.finfo(sim.dtype).max, sim)
            attn = jax.nn.softmax(sim, axis=-1)
            out = jnp.einsum('bhwij,bhwjd->bhwid', attn, bv)
            return out.reshape(b, h, n, d)

        def _layer(x, wqkv, qs, ksc, wo, lg, lb, w1, b1, w2, b2):
            b, n, _ = x.shape
            h = shift_token(x)
            qkv = h @ wqkv
            q, k, v = jnp.split(qkv, 3, axis=-1)
            to_heads = lambda t: t.reshape(b, n, HEADS, DIM_HEAD).transpose(0, 2, 1, 3)
            q, k, v = (to_heads(q), to_heads(k), to_heads(v))
            q = l2norm(q) * qs
            k = l2norm(k) * ksc
            q, k = rotary_xpos(q, k)
            o = local_attention(q, k, v)
            o = o.transpose(0, 2, 1, 3).reshape(b, n, INNER)
            x = x + o @ wo
            h = shift_token(x)
            mu = h.mean(-1, keepdims=True)
            var = h.var(-1, keepdims=True)
            h = (h - mu) / jnp.sqrt(var + 1e-05) * lg + lb
            h = h @ w1 + b1
            a, g = jnp.split(h, 2, axis=-1)
            h = a * jax.nn.gelu(g, approximate=False)
            x = x + h @ w2 + b2
            return x
        key = jax.random.key(seed)
        ks = jax.random.split(key, 6)
        return {'x': jax.random.normal(ks[0], (B, N, DIM), jnp.float32), 'wqkv': jax.random.normal(ks[1], (DEPTH, DIM, 3 * INNER), jnp.float32) * 0.02, 'q_scale': jnp.ones((DEPTH, DIM_HEAD), jnp.float32), 'k_scale': jnp.ones((DEPTH, DIM_HEAD), jnp.float32), 'wo': jax.random.normal(ks[2], (DEPTH, INNER, DIM), jnp.float32) * 0.02, 'ln_g': jnp.ones((DEPTH, DIM), jnp.float32), 'ln_b': jnp.zeros((DEPTH, DIM), jnp.float32), 'w1': jax.random.normal(ks[3], (DEPTH, DIM, 2 * HID), jnp.float32) * 0.02, 'b1': jnp.zeros((DEPTH, 2 * HID), jnp.float32), 'w2': jax.random.normal(ks[4], (DEPTH, HID, DIM), jnp.float32) * 0.02, 'b2': jnp.zeros((DEPTH, DIM), jnp.float32)}
    _L1_ffn_in = _L1_ffn_setup()
    _d = {'L0_attn_x': _L0_attn_in['x'], 'L0_attn_wq': _L0_attn_in['wq'], 'L0_attn_wk': _L0_attn_in['wk'], 'L0_attn_wv': _L0_attn_in['wv'], 'L0_attn_wo': _L0_attn_in['wo'], 'L0_ffn_router_w': _L0_ffn_in['router_w'], 'L0_ffn_router_b': _L0_ffn_in['router_b'], 'L0_ffn_w_c_fc': _L0_ffn_in['w_c_fc'], 'L0_ffn_b_c_fc': _L0_ffn_in['b_c_fc'], 'L0_ffn_w_gate': _L0_ffn_in['w_gate'], 'L0_ffn_b_gate': _L0_ffn_in['b_gate'], 'L0_ffn_w_c_proj': _L0_ffn_in['w_c_proj'], 'L0_ffn_b_c_proj': _L0_ffn_in['b_c_proj'], 'L1_attn_wq': _L1_attn_in['wq'], 'L1_attn_w_down': _L1_attn_in['w_down'], 'L1_attn_wk_up': _L1_attn_in['wk_up'], 'L1_attn_wv_up': _L1_attn_in['wv_up'], 'L1_attn_wo': _L1_attn_in['wo'], 'L1_ffn_wqkv': _L1_ffn_in['wqkv'], 'L1_ffn_q_scale': _L1_ffn_in['q_scale'], 'L1_ffn_k_scale': _L1_ffn_in['k_scale'], 'L1_ffn_wo': _L1_ffn_in['wo'], 'L1_ffn_ln_g': _L1_ffn_in['ln_g'], 'L1_ffn_ln_b': _L1_ffn_in['ln_b'], 'L1_ffn_w1': _L1_ffn_in['w1'], 'L1_ffn_b1': _L1_ffn_in['b1'], 'L1_ffn_w2': _L1_ffn_in['w2'], 'L1_ffn_b2': _L1_ffn_in['b2']}
    _x0 = _d['L0_attn_x']
    _d['L0_attn_x'] = jax.random.normal(jax.random.fold_in(jax.random.key(seed), 1), (2, 2048, 256), dtype=_x0.dtype)
    del _x0
    return _d

def reference(L0_attn_x, L0_attn_wq, L0_attn_wk, L0_attn_wv, L0_attn_wo, L0_ffn_router_w, L0_ffn_router_b, L0_ffn_w_c_fc, L0_ffn_b_c_fc, L0_ffn_w_gate, L0_ffn_b_gate, L0_ffn_w_c_proj, L0_ffn_b_c_proj, L1_attn_wq, L1_attn_w_down, L1_attn_wk_up, L1_attn_wv_up, L1_attn_wo, L1_ffn_wqkv, L1_ffn_q_scale, L1_ffn_k_scale, L1_ffn_wo, L1_ffn_ln_g, L1_ffn_ln_b, L1_ffn_w1, L1_ffn_b1, L1_ffn_w2, L1_ffn_b2):

    def _L0_attn_ref(x, wq, wk, wv, wo):
        import jax, jax.numpy as jnp
        import numpy as np
        B, S, DIN, DIM = (1, 1024, 256, 256)
        NH, NKV = (16, 4)
        HD = DIM // NH
        GS = NH // NKV
        b, s, _ = x.shape
        q = (x @ wq.T).reshape(b, s, NKV, GS, HD)
        k = (x @ wk.T).reshape(b, s, NKV, HD)
        v = (x @ wv.T).reshape(b, s, NKV, HD)
        scale = jnp.asarray(HD ** 0.5, x.dtype)
        att = jnp.einsum('bsgmd,btgd->bgmst', q, k) / scale
        causal = jnp.triu(jnp.ones((s, s), bool), 1)
        att = jnp.where(causal, -jnp.inf, att)
        att = jax.nn.softmax(att, axis=-1)
        ctx = jnp.einsum('bgmst,btgd->bsgmd', att, v).reshape(b, s, DIM)
        return ctx @ wo.T

    def _L0_ffn_ref(x, router_w, router_b, w_c_fc, b_c_fc, w_gate, b_gate, w_c_proj, b_c_proj):
        import jax, jax.numpy as jnp
        import numpy as np
        B, T, C = (8, 512, 256)
        H = 1024
        E = 8
        K = 2
        LOAD_FACTOR = 1.2
        N_LAYER = 12

        def _get_expert_inputs(x, logits, expert_capacity):
            Tt = logits.shape[0]
            Cc = x.shape[1]
            top_k_logits, expert_indices = jax.lax.top_k(logits, K)
            expert_probs = jax.nn.softmax(top_k_logits, axis=-1)
            ei = jnp.swapaxes(expert_indices, 0, 1).ravel()
            one_hot = jax.nn.one_hot(ei, E, dtype=jnp.int32)
            pos = jnp.cumsum(one_hot, axis=0) * one_hot - 1
            pos = pos.reshape(-1, Tt, E)
            pos = jnp.swapaxes(pos, 0, 1)
            pos = jnp.max(pos, axis=2)
            ei = jnp.swapaxes(ei.reshape(-1, Tt), 0, 1)
            buf = jnp.zeros((E, expert_capacity, Cc), x.dtype)
            xr = jnp.repeat(x, K, axis=0)
            expert_inputs = buf.at[ei.ravel(), pos.ravel()].add(xr)
            return (expert_probs, pos, ei, expert_inputs)
        Bb, Tt, Cc = x.shape
        logits = jnp.einsum('btc,ce->bte', x, router_w) + router_b
        cap = int(LOAD_FACTOR * K * Tt // E)
        probs, pos, idx, einp = jax.vmap(lambda xb, lb: _get_expert_inputs(xb, lb, cap))(x, logits)
        if Bb % E == 0:
            t = einp.reshape(E, Bb // E, E, cap, Cc)
            t = jnp.swapaxes(t, 0, 2)
        else:
            t = jnp.swapaxes(einp, 0, 1)
        einp2 = t.reshape(E, Bb * cap, Cc)
        h = jnp.einsum('eti,eih->eth', einp2, w_c_fc) + b_c_fc
        g = jnp.einsum('eti,eih->eth', einp2, w_gate) + b_gate
        o = jnp.einsum('eth,eho->eto', jax.nn.silu(h * g), w_c_proj) + b_c_proj
        if Bb % E == 0:
            o = o.reshape(E, Bb // E, E, cap, Cc)
            o = jnp.swapaxes(o, 0, 2)
            o = o.reshape(Bb, E, cap, Cc)
        else:
            o = o.reshape(E, Bb, cap, Cc)
            o = jnp.swapaxes(o, 0, 1)

        def collect(eo, i, p, pr):
            sel = eo[i, p]
            return jnp.sum(pr[..., None] * sel, axis=1)
        return jax.vmap(collect)(o, idx, pos, probs)

    def _L1_attn_ref(x, wq, w_down, wk_up, wv_up, wo):
        import jax, jax.numpy as jnp
        import numpy as np
        N_HEAD = 16
        PAGE_SIZE = 64
        ROPE_THETA = 10000.0

        def _rope_tables(T, D, dtype):
            inv = 1.0 / ROPE_THETA ** (np.arange(0, D, 2, dtype=np.float32) / D)
            ang = np.outer(np.arange(T, dtype=np.float32), inv)
            return (jnp.asarray(np.cos(ang), dtype), jnp.asarray(np.sin(ang), dtype))

        def _apply_rope(x, cos, sin):
            x1 = x[..., 0::2]
            x2 = x[..., 1::2]
            c = cos[None, :, None, :]
            s = sin[None, :, None, :]
            out = jnp.stack([x1 * c - x2 * s, x1 * s + x2 * c], axis=-1)
            return out.reshape(x.shape)
        B, T, E = x.shape
        H = N_HEAD
        D = E // H
        q = (x @ wq).reshape(B, T, H, D)
        lat = x @ w_down
        k = (lat @ wk_up).reshape(B, T, H, D)
        v = (lat @ wv_up).reshape(B, T, H, D)
        cos, sin = _rope_tables(T, D, x.dtype)
        q = _apply_rope(q, cos, sin)
        k = _apply_rope(k, cos, sin)
        scale = 1.0 / jnp.sqrt(jnp.asarray(D, x.dtype))
        scores = jnp.einsum('bqhd,bkhd->bhqk', q, k) * scale
        pages = jnp.arange(T) // PAGE_SIZE
        allowed = pages[None, :] <= pages[:, None]
        scores = jnp.where(allowed[None, None], scores, jnp.finfo(scores.dtype).min)
        attn = jax.nn.softmax(scores, axis=-1)
        out = jnp.einsum('bhqk,bkhd->bqhd', attn, v).reshape(B, T, E)
        return out @ wo

    def _L1_ffn_ref(x, wqkv, q_scale, k_scale, wo, ln_g, ln_b, w1, b1, w2, b2):
        import jax, jax.numpy as jnp
        import numpy as np
        DIM = 256
        DEPTH = 2
        HEADS = 8
        DIM_HEAD = 64
        WINDOW = 128
        INNER = HEADS * DIM_HEAD
        HID = int(DIM * 4 * 2 / 3)
        B, N = (2, 2048)
        QK_SCALE = 8.0

        def shift_token(t):
            t1, t2 = jnp.split(t, 2, axis=-1)
            t2 = jnp.pad(t2, ((0, 0), (1, 0), (0, 0)))[:, :-1]
            return jnp.concatenate([t1, t2], axis=-1)

        def l2norm(t):
            return t / jnp.clip(jnp.linalg.norm(t, axis=-1, keepdims=True), 1e-12)

        def rotate_half(x):
            x1, x2 = jnp.split(x, 2, axis=-1)
            return jnp.concatenate([-x2, x1], axis=-1)

        def rotary_xpos(q, k):
            n = q.shape[-2]
            half_idx = jnp.arange(0, DIM_HEAD, 2, dtype=jnp.float32)
            inv_freq = 1.0 / 10000.0 ** (half_idx / DIM_HEAD)
            t = jnp.arange(n, dtype=jnp.float32)
            freqs = t[:, None] * inv_freq[None, :]
            freqs = jnp.concatenate([freqs, freqs], axis=-1)
            base = (half_idx + 0.4 * DIM_HEAD) / (1.4 * DIM_HEAD)
            power = (t - n // 2) / float(WINDOW // 2)
            scale = base[None, :] ** power[:, None]
            scale = jnp.concatenate([scale, scale], axis=-1)
            cos, sin = (jnp.cos(freqs), jnp.sin(freqs))
            q = q * cos * scale + rotate_half(q) * sin * scale
            k = k * cos / scale + rotate_half(k) * sin / scale
            return (q, k)

        def local_attention(q, k, v):
            b, h, n, d = q.shape
            w = n // WINDOW
            bq = q.reshape(b, h, w, WINDOW, d) * QK_SCALE
            bk = k.reshape(b, h, w, WINDOW, d)
            bv = v.reshape(b, h, w, WINDOW, d)

            def look_around(t):
                p = jnp.pad(t, ((0, 0), (0, 0), (1, 0), (0, 0), (0, 0)))
                return jnp.concatenate([p[:, :, :w], p[:, :, 1:]], axis=3)
            bk, bv = (look_around(bk), look_around(bv))
            bt = jnp.arange(n).reshape(w, WINDOW)
            btp = jnp.pad(bt, ((1, 0), (0, 0)), constant_values=-1)
            btk = jnp.concatenate([btp[:w], btp[1:]], axis=1)
            sim = jnp.einsum('bhwid,bhwjd->bhwij', bq, bk)
            i = bt[:, :, None]
            j = btk[:, None, :]
            mask = (i < j) | (i > j + WINDOW) | (j == -1)
            sim = jnp.where(mask, -jnp.finfo(sim.dtype).max, sim)
            attn = jax.nn.softmax(sim, axis=-1)
            out = jnp.einsum('bhwij,bhwjd->bhwid', attn, bv)
            return out.reshape(b, h, n, d)

        def _layer(x, wqkv, qs, ksc, wo, lg, lb, w1, b1, w2, b2):
            b, n, _ = x.shape
            h = shift_token(x)
            qkv = h @ wqkv
            q, k, v = jnp.split(qkv, 3, axis=-1)
            to_heads = lambda t: t.reshape(b, n, HEADS, DIM_HEAD).transpose(0, 2, 1, 3)
            q, k, v = (to_heads(q), to_heads(k), to_heads(v))
            q = l2norm(q) * qs
            k = l2norm(k) * ksc
            q, k = rotary_xpos(q, k)
            o = local_attention(q, k, v)
            o = o.transpose(0, 2, 1, 3).reshape(b, n, INNER)
            x = x + o @ wo
            h = shift_token(x)
            mu = h.mean(-1, keepdims=True)
            var = h.var(-1, keepdims=True)
            h = (h - mu) / jnp.sqrt(var + 1e-05) * lg + lb
            h = h @ w1 + b1
            a, g = jnp.split(h, 2, axis=-1)
            h = a * jax.nn.gelu(g, approximate=False)
            x = x + h @ w2 + b2
            return x
        for l in range(DEPTH):
            x = _layer(x, wqkv[l], q_scale[l], k_scale[l], wo[l], ln_g[l], ln_b[l], w1[l], b1[l], w2[l], b2[l])
        return x
    x = L0_attn_x
    x = _layernorm(x + _L0_attn_ref(x, L0_attn_wq, L0_attn_wk, L0_attn_wv, L0_attn_wo), axis=-1)
    x = _layernorm(x + _L0_ffn_ref(x, L0_ffn_router_w, L0_ffn_router_b, L0_ffn_w_c_fc, L0_ffn_b_c_fc, L0_ffn_w_gate, L0_ffn_b_gate, L0_ffn_w_c_proj, L0_ffn_b_c_proj), axis=-1)
    x = _layernorm(x + _L1_attn_ref(x, L1_attn_wq, L1_attn_w_down, L1_attn_wk_up, L1_attn_wv_up, L1_attn_wo), axis=-1)
    x = _layernorm(x + _L1_ffn_ref(x, L1_ffn_wqkv, L1_ffn_q_scale, L1_ffn_k_scale, L1_ffn_wo, L1_ffn_ln_g, L1_ffn_ln_b, L1_ffn_w1, L1_ffn_b1, L1_ffn_w2, L1_ffn_b2), axis=-1)
    return x

_drawn_inputs = setup_inputs


def setup_inputs(seed=0):
    import zlib

    import numpy as np

    out = dict(_drawn_inputs(seed))
    spreads = {'L0_ffn_router_b': (0.0, 0.1),
     'L0_ffn_b_c_fc': (0.0, 0.8),
     'L0_ffn_b_gate': (0.0, 0.8),
     'L0_ffn_b_c_proj': (0.0, 0.322),
     'L1_ffn_q_scale': (1.0, 0.6),
     'L1_ffn_k_scale': (1.0, 0.6),
     'L1_ffn_ln_g': (1.0, 0.6),
     'L1_ffn_ln_b': (0.0, 0.8),
     'L1_ffn_b1': (0.0, 0.8),
     'L1_ffn_b2': (0.0, 0.1)}
    factors = {'L0_ffn_w_c_fc': 8.0,
     'L0_ffn_w_gate': 8.0,
     'L0_ffn_w_c_proj': 8.0,
     'L1_ffn_wqkv': 2.759,
     'L1_ffn_wo': 2.759}
    for name, (base, spread) in spreads.items():
        noise = np.random.default_rng([zlib.crc32(name.encode()), seed]).standard_normal(out[name].shape)
        drawn = base * np.exp(spread * noise) if base else spread * noise
        out[name] = jnp.asarray(drawn.astype(out[name].dtype))
    for name, factor in factors.items():
        out[name] = (out[name] * factor).astype(out[name].dtype)
    return out
```

```python
from contextlib import ExitStack

import numpy as np
import concourse.bass as bass
from concourse import mybir

F32 = mybir.dt.float32
F32R = mybir.dt.float32r
BF16 = mybir.dt.bfloat16
U32 = mybir.dt.uint32
ALU = mybir.AluOpType
ACT = mybir.ActivationFunctionType
AX = mybir.AxisListType.X
ds = bass.ds

P = 128
B, S, D = 2, 2048, 256
TOK = B * S
NT = TOK // P
KC = D // P
CH = 512
CPB = S // CH
SUB = CH // P
NH, HD = 16, 16
GRP = 4
NG = NH // GRP
NIT = B * NG
NKV = 4
VW = 2 * HD
PAGE = 64
NEG = -1e30
EPS = 1e-5


def wait_apart(eng, semaphore, value, fence):
    eng.wait_ge(semaphore, value)
    eng.sem_inc(fence, 1)


def layer0_projections(nc, sem, xT, wqT, wkT, wvT, qh, ql, kh, kl, vs):
    NKD = NKV * HD
    STORES = 2 * KC + 2 + SUB
    with ExitStack() as ctx:
        sb = lambda n, s, t: ctx.enter_context(nc.sbuf_tensor("A_" + n, s, t))
        x = sb("x", [P, 2, KC, CH], F32)
        wq = sb("wq", [P, KC, D], F32)
        wk = sb("wk", [P, KC, NKD], F32)
        wv = sb("wv", [P, KC, NKD], F32)
        qhi = sb("qhi", [P, 2, KC, CH], F32R)
        qlo = sb("qlo", [P, 2, KC, CH], F32R)
        khi = sb("khi", [NKD, 2, CH], F32R)
        klo = sb("klo", [NKD, 2, CH], F32R)
        v = sb("v", [P, 2, SUB, NKV, VW], F32)
        bank = [ctx.enter_context(nc.psum_tensor(f"A_b{i}", [P, CH], F32)) for i in range(8)]
        w_in, x_in = sem("A_w_in"), [sem(f"A_x_in{u}") for u in range(2)]
        x_used, banks_used = sem("A_x_used"), sem("A_banks_used")
        stored = [sem(f"A_stored{u}") for u in range(2)]
        fence = sem("A_fence")
        mm_done, hi_done, lo_done, ones_set = sem("A_mm"), sem("A_hi"), sem("A_lo"), sem("A_ones")
        block = ctx.enter_context(nc.Block())
        xT_v = xT.rearrange("(kc p) t -> p kc t", p=P)

        @block.gpsimd
        def _(pool):
            for w, src in ((wq, wqT), (wk, wkT), (wv, wvT)):
                pool.dma_start(w[:], src.rearrange("(kc p) n -> p kc n", p=P)).then_inc(w_in, 16)
            with pool.Fori(0, TOK // CH // 2) as pair:
                for u in range(2):
                    wait_apart(pool, x_used, pair * 2 + u + 1, fence)
                    pool.dma_start(x[:, u], xT_v[:, :, ds(pair * (2 * CH) + u * CH, CH)]).then_inc(x_in[u], 16)

        @block.tensor
        def _(pe):
            pe.sem_inc(x_used, 2)
            pe.wait_ge(w_in, 48)
            with pe.Fori(0, TOK // CH // 2) as pair:
                for u in range(2):
                    n = pair * 2 + u
                    pe.wait_ge(x_in[u], pair * 16 + 16)
                    pe.wait_ge(banks_used, n + 1)
                    for m in range(KC):
                        for c in range(KC):
                            pe.matmul(bank[4 * u + m][:], wq[:, c, m * P:(m + 1) * P], x[:, u, c],
                                      start=c == 0, stop=c == KC - 1)
                    for c in range(KC):
                        pe.matmul(bank[4 * u + 2][0:NKD], wk[:, c], x[:, u, c], start=c == 0, stop=c == KC - 1)
                    for s in range(SUB):
                        for c in range(KC):
                            last = pe.matmul(bank[4 * u + 3][:, s * NKD:(s + 1) * NKD], x[:, u, c, s * P:(s + 1) * P],
                                             wv[:, c], start=c == 0, stop=c == KC - 1)
                    last.then_inc(mm_done, 1)
                    pe.drain().then_inc(x_used, 1)

        @block.scalar
        def _(act):
            act.wait_ge(ones_set, 1)
            with act.Fori(0, TOK // CH // 2) as pair:
                for u in range(2):
                    n = pair * 2 + u
                    act.wait_ge(mm_done, n + 1)
                    act.wait_ge(stored[u], pair * (16 * STORES))
                    for s in range(SUB):
                        act.activation(v[:, u, s, :, 0:HD],
                                       bank[4 * u + 3][:, s * NKD:(s + 1) * NKD].rearrange("p (g e) -> p g e", e=HD),
                                       ACT.Copy)
                    act.activation(khi[:, u], bank[4 * u + 2][0:NKD], ACT.Copy)
                    for m in range(KC):
                        last = act.activation(qhi[:, u, m], bank[4 * u + m][:], ACT.Copy)
                    last.then_inc(hi_done, 1)

        @block.vector
        def _(dve):
            dve.sem_inc(banks_used, 2)
            dve.memset(v[:], 1.0).then_inc(ones_set, 1)
            with dve.Fori(0, TOK // CH // 2) as pair:
                for u in range(2):
                    n = pair * 2 + u
                    dve.wait_ge(hi_done, n + 1)
                    dve.tensor_tensor(klo[:, u], bank[4 * u + 2][0:NKD], khi[:, u].bitcast(F32), ALU.subtract)
                    for m in range(KC):
                        last = dve.tensor_tensor(qlo[:, u, m], bank[4 * u + m][:], qhi[:, u, m].bitcast(F32),
                                                 ALU.subtract)
                    last.then_inc(lo_done, 1)
                    dve.drain().then_inc(banks_used, 1)

        @block.sync
        def _(sp):
            with sp.Fori(0, B) as b:
                with sp.Fori(0, CPB // 2) as pair:
                    for u in range(2):
                        n = b * CPB + pair * 2 + u
                        col = pair * (2 * CH) + u * CH
                        sp.wait_ge(lo_done, n + 1)
                        for m in range(KC):
                            for dst, src in ((qh, qhi), (ql, qlo)):
                                sp.dma_start(dst[ds(b * D + m * P, P), ds(col, CH)], src[:, u, m].bitcast(F32)).then_inc(stored[u], 16)
                        for dst, src in ((kh, khi), (kl, klo)):
                            sp.dma_start(dst[ds(b * NKD, NKD), ds(col, CH)], src[:, u].bitcast(F32)).then_inc(stored[u], 16)
                        vs_v = vs.rearrange("(bb g t) e -> bb t g e", bb=B, g=NG)
                        for s in range(SUB):
                            sp.dma_start(vs_v[ds(b, 1), ds(col + s * P, P)].rearrange("o t g e -> (o t) g e"),
                                         v[:, u, s]).then_inc(stored[u], 16)
            for u in range(2):
                sp.wait_ge(stored[u], 16 * STORES * (TOK // CH // 2))


def attention(nc, sem, tag, nk, qh, ql, kh, kl, vs, mask_qk, mask_kq, ident_bf, ident, m_rows, ot):
    R = 4 * HD
    NQ = S // P
    SC = 1.0 / HD ** 0.5

    pieces = []
    for qb in range(NQ):
        full, rest = divmod((qb + 1) * P, CH)
        for kc in range(full):
            pieces += [(qb, kc, CH, [h]) for h in range(GRP)]
        if rest:
            per = CH // rest
            pieces += [(qb, full, rest, list(range(h, h + per))) for h in range(0, GRP, per)]
    NP = len(pieces)
    steps = [(qc, kb) for qc in range(NQ * P // CH) for kb in range(SUB * (qc + 1))]
    NS = len(steps)
    cut = [NP * i // NS for i in range(NS + 1)]

    with ExitStack() as ctx:
        sb = lambda n, s, t: ctx.enter_context(nc.sbuf_tensor(tag + n, s, t))
        qs = [sb(f"qs{i}", [R + 2, GRP, S], F32R) for i in range(2)]
        ks = [sb(f"ks{i}", [R + 2, nk, S], F32R) for i in range(2)]
        v = [sb(f"v{i}", [P, NQ, nk, VW], F32) for i in range(2)]
        p = sb("p", [P, 2, GRP, CH], F32)
        o = sb("o", [P, 2, CH], F32)
        mpart = sb("mpart", [P, GRP, NQ, 4], F32)
        m = sb("m", [P, P], F32)
        mhi = sb("mhi", [GRP * NQ, P], F32R)
        mlo = sb("mlo", [GRP * NQ, P], F32R)
        mqk = sb("mqk", [P, P], BF16)
        mkq = sb("mkq", [P, P], BF16)
        idb = sb("idb", [P, P], BF16)
        idf = sb("idf", [P, P], F32)
        psc = ctx.enter_context(nc.psum_tensor(tag + "psc", [P, GRP, CH], F32))
        po = [ctx.enter_context(nc.psum_tensor(f"{tag}po{i}", [P, CH], F32)) for i in range(2)]
        pm = [ctx.enter_context(nc.psum_tensor(f"{tag}pm{i}", [P, CH], F32)) for i in range(2)]
        c_in, ready = sem(tag + "c_in"), sem(tag + "ready")
        q_in, ld_free = [sem(f"{tag}q_in{i}") for i in range(2)], sem(tag + "ld_free")
        s_max, max_done = sem(tag + "s_max"), sem(tag + "max_done")
        m_all, mt_done = sem(tag + "m_all"), sem(tag + "mt_done")
        mh_done, ml_done = sem(tag + "mh_done"), sem(tag + "ml_done")
        m_out, m_in, fence = sem(tag + "m_out"), sem(tag + "m_in"), sem(tag + "fence")
        s_done, pv_done = sem(tag + "s_done"), sem(tag + "pv_done")
        e_done = [sem(f"{tag}e_done{i}") for i in range(2)]
        o_done, o_out = sem(tag + "o_done"), [sem(f"{tag}o_out{i}") for i in range(2)]
        block = ctx.enter_context(nc.Block())

        LOADS = 8 + 1
        NC4 = S // CH

        @block.gpsimd
        def _(pool):
            for dst, src in ((mqk, mask_qk), (mkq, mask_kq), (idb, ident_bf)):
                pool.dma_start(dst[:], src).then_inc(c_in, 16)
            pool.dma_start(idf[:], ident).then_inc(c_in, 16)

            def load(i, s):
                for r, (a, c) in enumerate(((qh, kh), (qh, kl), (ql, kh), (ql, kl))):
                    pool.dma_start(qs[s][r * HD:(r + 1) * HD, :, :].bitcast(F32),
                                   a[ds(i * (GRP * HD), GRP * HD), :].rearrange("(h e) t -> e h t", e=HD)
                                   ).then_inc(q_in[s], 16)
                    pool.dma_start(ks[s][r * HD:(r + 1) * HD, :, :].bitcast(F32),
                                   c[ds(i * (nk * HD), nk * HD), :].rearrange("(h e) t -> e h t", e=HD)
                                   ).then_inc(q_in[s], 16)
                pool.dma_start(v[s][:], vs[ds(i * S, S), :].rearrange("(kb p) (h e) -> p kb h e", p=P, e=VW)
                               ).then_inc(q_in[s], 16)

            load(0, 0)
            load(1, 1)
            with pool.Fori(0, NIT // 2 - 1) as pair:
                for s in range(2):
                    wait_apart(pool, ld_free, pair * 2 + s + 1, fence)
                    load(pair * 2 + s + 2, s)

        @block.sync
        def _(sp):
            def m_step(i, s):
                sp.wait_ge(ml_done, i + 1)
                sp.dma_start(m_rows[0:1].rearrange("o (a t) -> (o a) t", t=P), mhi[:].bitcast(F32)).then_inc(m_out, 16)
                sp.dma_start(m_rows[1:2].rearrange("o (a t) -> (o a) t", t=P), mlo[:].bitcast(F32)).then_inc(m_out, 16)
                sp.wait_ge(m_out, (i + 1) * 32)
                sp.dma_start(qs[s][R:R + 2, :, :].bitcast(F32).rearrange("r h t -> r (h t)"), m_rows).then_inc(m_in, 16)

            def outs(i):
                for c in range(NC4):
                    sp.wait_ge(o_done, i * NC4 + c + 2)
                    sp.dma_start(ot[ds(i * P, P), c * CH:(c + 1) * CH], o[:, c % 2]).then_inc(o_out[c % 2], 16)

            m_step(0, 0)
            with sp.Fori(0, NIT // 2 - 1) as pair:
                for s in range(2):
                    outs(pair * 2 + s)
                    m_step(pair * 2 + s + 1, (s + 1) % 2)
            outs(NIT - 2)
            m_step(NIT - 1, 1)
            outs(NIT - 1)
            for c in range(2):
                sp.wait_ge(o_out[c], 16 * (NC4 // 2 * NIT))

        @block.tensor
        def _(pe):
            def maxima(i, s, a, z):
                for j in range(a, z):
                    qb, kc, w, heads = pieces[j]
                    t = pm[j % 2]
                    pe.wait_ge(max_done, i * NP + j + 1)
                    diag = kc * CH + w == (qb + 1) * P
                    for n, h in enumerate(heads):
                        last = pe.matmul(t[:, n * w:(n + 1) * w], qs[s][0:R, h, qb * P:(qb + 1) * P],
                                         ks[s][0:R, h % nk, kc * CH:kc * CH + w], start=True, stop=True)
                        if diag:
                            last = pe.matmul(t[:, (n + 1) * w - P:(n + 1) * w], idb[:], mqk[:], start=False,
                                             stop=True, skip_group_check=True)
                    last.then_inc(s_max, 1)

            def turn(i):
                pe.wait_ge(m_all, i + 1)
                pe.transpose(pm[0][:, 0:P], m[:], idf[:]).then_inc(mt_done, 1)

            def weigh(i, s, t):
                qc, kb = steps[t]
                off = max(0, kb - SUB * qc) * P
                for pr in range(2):
                    pe.wait_ge(e_done[pr], i * NS + t + 1)
                if kb == 0:
                    pe.wait_ge(o_done, i * NC4 + qc)
                for h in range(GRP):
                    last = pe.matmul(po[qc % 2][VW * h:VW * (h + 1), off:CH], v[s][:, kb, h % nk],
                                     p[:, t % 2, h, off:CH], start=kb == 0, stop=kb == SUB * (qc + 1) - 1,
                                     skip_group_check=True)
                last.then_inc(pv_done, 1)

            def step(i, s, nxt):
                pe.wait_ge(m_in, (i + 1) * 16)
                for t, (qc, kb) in enumerate(steps):
                    diag = kb - SUB * qc
                    off = max(0, diag) * P
                    for pr in range(2):
                        pe.wait_ge(e_done[pr], i * NS + t)
                        for h in (2 * pr, 2 * pr + 1):
                            last = pe.matmul(psc[:, h, off:CH], ks[s][0:R + 2, h % nk, kb * P:(kb + 1) * P],
                                             qs[s][0:R + 2, h, qc * CH + off:(qc + 1) * CH],
                                             start=True, stop=True)
                            if diag >= 0:
                                last = pe.matmul(psc[:, h, off:off + P], idb[:], mkq[:], start=False, stop=True,
                                                 skip_group_check=True)
                        last.then_inc(s_done, 1)
                    if t:
                        weigh(i, s, t - 1)
                    if nxt:
                        maxima(i + 1, 1 - s, cut[t], cut[t + 1])
                weigh(i, s, NS - 1)
                pe.drain().then_inc(ld_free, 1)
                if nxt:
                    turn(i + 1)

            pe.wait_ge(c_in, 64)
            pe.wait_ge(ready, 1)
            pe.wait_ge(q_in[0], 16 * LOADS)
            maxima(0, 0, 0, NP)
            turn(0)
            with pe.Fori(0, NIT // 2 - 1) as pair:
                for s in range(2):
                    pe.wait_ge(q_in[1 - s], (pair + s + 1) * (16 * LOADS))
                    step(pair * 2 + s, s, True)
            pe.wait_ge(q_in[1], NIT // 2 * 16 * LOADS)
            step(NIT - 2, 0, True)
            step(NIT - 1, 1, False)

        @block.scalar
        def _(act):
            def m_hi(i):
                act.wait_ge(mt_done, i + 1)
                act.wait_ge(m_in, i * 16)
                act.activation(mhi[:], pm[0][0:GRP * NQ, 0:P], ACT.Copy, scale=-1.0).then_inc(mh_done, 1)

            def step(i):
                for t, (qc, kb) in enumerate(steps):
                    off = max(0, kb - SUB * qc) * P
                    for pr in range(2):
                        act.wait_ge(s_done, (i * NS + t) * 2 + pr + 1)
                        act.wait_ge(pv_done, i * NS + t + 1)
                        act.activation(p[:, t % 2, 2 * pr:2 * pr + 2, off:CH], psc[:, 2 * pr:2 * pr + 2, off:CH],
                                       ACT.Exp, scale=SC).then_inc(e_done[pr], 1)

            m_hi(0)
            with act.Fori(0, NIT // 2 - 1) as pair:
                for s in range(2):
                    step(pair * 2 + s)
                    m_hi(pair * 2 + s + 1)
            step(NIT - 2)
            m_hi(NIT - 1)
            step(NIT - 1)

        @block.vector
        def _(dve):
            def maxima(i, a, z):
                for j in range(a, z):
                    qb, kc, w, heads = pieces[j]
                    dve.wait_ge(s_max, i * NP + j + 1)
                    dve.tensor_reduce(mpart[:, heads[0]:heads[-1] + 1, qb, kc],
                                      pm[j % 2][:, 0:len(heads) * w].rearrange("p (h k) -> p h k", k=w),
                                      AX, ALU.max).then_inc(max_done, 1)

            def fold(i):
                dve.wait_ge(max_done, (i + 1) * NP + 2)
                dve.wait_ge(mt_done, i)
                dve.tensor_reduce(m[:, 0:GRP * NQ], mpart[:].rearrange("p h q k -> p (h q) k"), AX, ALU.max).then_inc(m_all, 1)

            def m_lo(i):
                dve.wait_ge(mh_done, i + 1)
                dve.scalar_tensor_tensor(mlo[:], pm[0][0:GRP * NQ, 0:P], -1.0, mhi[:].bitcast(F32),
                                         ALU.mult, ALU.subtract).then_inc(ml_done, 1)

            def copy_out(i, qc):
                dve.wait_ge(pv_done, i * NS + 2 + sum(SUB * (c + 1) for c in range(qc + 1)))
                dve.wait_ge(o_out[qc % 2], i * (NC4 // 2 * 16) + qc // 2 * 16)
                dve.tensor_copy(o[:, qc % 2], po[qc % 2][:]).then_inc(o_done, 1)

            def step(i, nxt):
                for t, (qc, kb) in enumerate(steps):
                    if nxt:
                        maxima(i + 1, cut[t], cut[t + 1])
                    if kb == 0 and qc:
                        copy_out(i, qc - 1)
                copy_out(i, NC4 - 1)
                if nxt:
                    fold(i + 1)
                    m_lo(i + 1)

            dve.sem_inc(max_done, 2)
            dve.sem_inc(o_done, 1)
            dve.sem_inc(pv_done, 2)
            dve.memset(mpart[:], -3e38)
            dve.memset(m[:], 0.0)
            for s in range(2):
                last = dve.memset(ks[s][R:R + 2].bitcast(F32), 1.0)
            last.then_inc(ready, 1)
            maxima(0, 0, NP)
            fold(0)
            m_lo(0)
            with dve.Fori(0, NIT // 2 - 1) as pair:
                for s in range(2):
                    step(pair * 2 + s, True)
            step(NIT - 2, True)
            step(NIT - 1, False)


E_, HID_E = 8, 1024
TOPK = 2
CAP = int(1.2 * TOPK * S // E_)
ROWS = B * CAP


class Chain:

    def __init__(self, eng, semaphore, per):
        self.eng, self.sem, self.per, self.n, self.base = eng, semaphore, per, 0, 0

    def start(self, i):
        self.base, self.n = i * self.per, 0

    def link(self, ins):
        self.n += 1
        ins.then_inc(self.sem, 1)
        self.eng.wait_ge(self.sem, self.base + self.n)

    def end(self):
        assert self.n == self.per, self.n


def attention_output(nc, sem, tag, ot, woT, x_src, X, ident, router, xp):
    NLN = 2 + 1 + 2 + SUB
    with ExitStack() as ctx:
        sb = lambda n, s, t: ctx.enter_context(nc.sbuf_tensor(tag + n, s, t))
        num = sb("num", [P, 2, KC, CH], F32)
        den = sb("den", [P, 2, KC, CH], F32)
        rec = sb("rec", [P, KC, CH], F32)
        cx = sb("cx", [P, KC, CH], F32)
        wo = sb("wo", [P, KC, D], F32)
        y = sb("y", [P, SUB, D], F32)
        xn = sb("xn", [P, SUB, D], F32)
        xnT = sb("xnT", [P, KC, CH], F32)
        st = sb("st", [P, SUB, 6], F32)
        mv = sb("mv", [P, SUB, 2], F32)
        sd = sb("sd", [P, SUB], F32)
        rs = sb("rs", [P, SUB], F32)
        eps = sb("eps", [P, 1], F32)
        idf = sb("idf", [P, P], F32)
        rw = sb("rw", [P, KC, E_], F32)
        rb = sb("rb", [P, E_], F32)
        pb = [ctx.enter_context(nc.psum_tensor(f"{tag}pb{i}", [P, CH], F32)) for i in range(5)]
        w_in, a_in = sem(tag + "w_in"), [sem(f"{tag}a_in{u}") for u in range(2)]
        c_ready, mm_done = sem(tag + "c_ready"), sem(tag + "mm_done")
        var_done, sd_done, n_done = sem(tag + "var"), sem(tag + "sd"), sem(tag + "n_done")
        t_done, xt_done, lg_done, lg_out = sem(tag + "t"), sem(tag + "xt"), sem(tag + "lg"), sem(tag + "lgo")
        x_copied, st_done, dch, fence = sem(tag + "xc"), sem(tag + "st"), sem(tag + "dch"), sem(tag + "fence")
        block = ctx.enter_context(nc.Block())
        eps_set = sem(tag + "eps")
        wcount = 2 + (2 if router else 0) + (1 if x_src is not None else 0)

        def chunks(eng, body):
            with eng.Fori(0, B) as b:
                with eng.Fori(0, CPB // 2) as pair:
                    for u in range(2):
                        body(b * CPB + pair * 2 + u, b, pair, u)

        @block.gpsimd
        def _(pool):
            pool.dma_start(wo[:], woT.rearrange("(kc p) n -> p kc n", p=P)).then_inc(w_in, 16)
            pool.dma_start(idf[:], ident).then_inc(w_in, 16)
            pool.memset(eps[:], EPS).then_inc(eps_set, 1)
            if router:
                pool.dma_start(rw[:], router[0].rearrange("(kc p) n -> p kc n", p=P)).then_inc(w_in, 16)
                pool.dma_start(rb[:], router[1]).then_inc(w_in, 16)
            if x_src is not None:
                pool.dma_start(X[:], x_src.rearrange("(t p) c -> p t c", p=P)).then_inc(w_in, 16)

            def body(n, b, pair, u):
                wait_apart(pool, c_ready, n, fence)
                for m in range(KC):
                    o = ot[ds(b * (NH * VW) + m * (NH * VW // KC), NH * VW // KC),
                           ds(pair * (2 * CH) + u * CH, CH)].rearrange("(h r) t -> h r t", r=VW)
                    pool.dma_start(num[:, u, m], o[:, 0:HD]).then_inc(a_in[u], 16)
                    pool.dma_start(den[:, u, m], o[:, HD:VW]).then_inc(a_in[u], 16)
            chunks(pool, body)

        @block.tensor
        def _(pe):
            pe.wait_ge(w_in, wcount * 16)

            def body(n, b, pair, u):
                pe.wait_ge(c_ready, n + 2)
                for s in range(SUB):
                    for c in range(KC):
                        last = pe.matmul(pb[s // 2][:, s % 2 * D:(s % 2 + 1) * D], cx[:, c, s * P:(s + 1) * P],
                                         wo[:, c], start=c == 0, stop=c == KC - 1)
                last.then_inc(mm_done, 1)
                if router:
                    pe.wait_ge(n_done, n + 1)
                    for c in range(KC):
                        for s in range(SUB):
                            last = pe.transpose(pb[2 + c][:, s * P:(s + 1) * P], xn[:, s, c * P:(c + 1) * P], idf[:])
                    last.then_inc(t_done, 1)
                    pe.wait_ge(xt_done, n + 1)
                    for s in range(SUB):
                        for c in range(KC):
                            last = pe.matmul(pb[4][:, s * E_:(s + 1) * E_], xnT[:, c, s * P:(s + 1) * P], rw[:, c],
                                             start=c == 0, stop=c == KC - 1)
                    last.then_inc(lg_done, 1)
            chunks(pe, body)

        @block.scalar
        def _(act):
            act.wait_ge(eps_set, 1)

            def body(n, b, pair, u):
                act.wait_ge(var_done, n + 1)
                act.activation(sd[:], mv[:, :, 1], ACT.Sqrt, bias=eps[:]).then_inc(sd_done, 1)
                act.wait_ge(n_done, n + 1)
                act.activation(X[:, ds(n * SUB, SUB), :], xn[:], ACT.Copy).then_inc(x_copied, 1)
                if router:
                    act.wait_ge(t_done, n + 1)
                    for c in range(KC):
                        last = act.activation(xnT[:, c], pb[2 + c][:], ACT.Copy)
                    last.then_inc(xt_done, 1)
            chunks(act, body)

        @block.vector
        def _(dve):
            ch = Chain(dve, dch, 5 + SUB - 1 + (1 if router else 0))
            dve.wait_ge(w_in, wcount * 16)
            dve.sem_inc(c_ready, 1)

            def body(n, b, pair, u):
                ch.start(n)
                dve.wait_ge(a_in[u], b * (CPB // 2 * 64) + pair * 64 + 64)
                dve.wait_ge(mm_done, n)
                ch.link(dve.reciprocal(rec[:], den[:, u]))
                dve.tensor_tensor(cx[:], num[:, u], rec[:], ALU.mult).then_inc(c_ready, 1)
                dve.wait_ge(mm_done, n + 1)
                for k in range(2):
                    last = dve.tensor_tensor(y[:, 2 * k:2 * k + 2], pb[k][:].rearrange("p (s c) -> p s c", c=D),
                                             X[:, ds(n * SUB + 2 * k, 2), :], ALU.add)
                    ch.link(last)
                for s in range(SUB):
                    last = dve.bn_stats(st[:, s], y[:, s])
                ch.link(last)
                dve.sem_inc(fence, 1)
                for s in range(SUB):
                    last = dve.bn_aggr(mv[:, s], st[:, s])
                last.then_inc(var_done, 1)
                dve.wait_ge(sd_done, n + 1)
                ch.link(dve.reciprocal(rs[:], sd[:]))
                dve.wait_ge(x_copied, n)
                if router:
                    dve.wait_ge(t_done, n)
                if xp is not None:
                    dve.wait_ge(st_done, n * (16 * SUB))
                for s in range(SUB):
                    last = dve.tensor_scalar(xn[:, s], y[:, s], mv[:, s, 0:1], rs[:, s:s + 1], ALU.subtract, ALU.mult)
                    if s == SUB - 1:
                        last.then_inc(n_done, 1)
                    else:
                        ch.link(last)
                if router:
                    dve.wait_ge(lg_done, n + 1)
                    ch.link(dve.tensor_tensor(router[2][:, ds(n * SUB, SUB), :],
                                              pb[4][:, 0:SUB * E_].rearrange("p (s e) -> p s e", e=E_),
                                              rb[:].unsqueeze(1).to_broadcast([P, SUB, E_]), ALU.add))
                ch.end()
            chunks(dve, body)
            dve.wait_ge(x_copied, TOK // CH)

        @block.sync
        def _(sp):
            if xp is not None:
                def body(n, b, pair, u):
                    sp.wait_ge(n_done, n + 1)
                    for s in range(SUB):
                        sp.dma_start(xp[ds(b * (S + 1) + pair * (2 * CH) + u * CH + s * P + 1, P), :], xn[:, s]
                                     ).then_inc(st_done, 16)
                chunks(sp, body)
                sp.wait_ge(st_done, 16 * SUB * (TOK // CH))


def route(nc, sem, LG, tri, iota8, ones, slot_s, slot_g, prob):
    NK = TOPK
    QT = S // P
    SEQ = NK * QT
    with ExitStack() as ctx:
        sb = lambda n, s, t: ctx.enter_context(nc.sbuf_tensor("D_" + n, s, t))
        m8 = sb("m8", [P, NT, 8], F32)
        i8 = sb("i8", [P, NT, 8], U32)
        ixf = sb("ixf", [P, NK, NT], F32)
        oh = sb("oh", [P, B, NK, QT, E_], F32)
        trs = sb("trs", [P, P], F32)
        on = sb("on", [P, P], F32)
        io = sb("io", [P, E_], F32)
        ca = sb("ca", [P, B, SEQ, E_], F32)
        cb = sb("cb", [P, B, SEQ, E_], F32)
        pos = sb("pos", [P, B, SEQ, E_], F32)
        pf = sb("pf", [P, B, NK, QT], F32)
        base = sb("base", [P, B, NK, QT], F32)
        of = sb("of", [P, B, NK, QT], F32)
        g = sb("g", [P, B, NK, QT], F32)
        dif = sb("dif", [P, NT], F32)
        e2 = sb("e2", [P, NT], F32)
        den = sb("den", [P, NT], F32)
        pc = ctx.enter_context(nc.psum_tensor("D_pc", [P, CH], F32))
        pt = ctx.enter_context(nc.psum_tensor("D_pt", [P, CH], F32))
        c_in, dch, oh_done, cum_done = sem("D_c_in"), sem("D_dch"), sem("D_oh"), sem("D_cum")
        dif_done, e2_done = sem("D_dif"), sem("D_e2")
        block = ctx.enter_context(nc.Block())

        @block.sync
        def _(sp):
            for dst, src in ((trs, tri), (on, ones), (io, iota8)):
                sp.dma_start(dst[:], src).then_inc(c_in, 16)

        @block.tensor
        def _(pe):
            pe.wait_ge(c_in, 48)
            pe.wait_ge(oh_done, 1)
            flat = oh[:].rearrange("p b k t e -> p (b k t e)")
            pe.matmul(pc[:], trs[:], flat, start=True, stop=True)
            pe.matmul(pt[:], on[:], flat, start=True, stop=True).then_inc(cum_done, 1)

        @block.scalar
        def _(act):
            act.wait_ge(dif_done, 1)
            act.activation(e2[:], dif[:], ACT.Exp).then_inc(e2_done, 1)

        @block.vector
        def _(dve):
            n = [0]

            def link(ins):
                n[0] += 1
                ins.then_inc(dch, 1)
                dve.wait_ge(dch, n[0])

            dve.wait_ge(c_in, 48)
            for t in range(NT):
                last = dve.max(m8[:, t], LG[:, t])
            link(last)
            for t in range(NT):
                last = dve.max_index(i8[:, t], m8[:, t], LG[:, t])
            link(last)
            dve.tensor_tensor(dif[:], m8[:, :, 1], m8[:, :, 0], ALU.subtract).then_inc(dif_done, 1)
            for k in range(NK):
                last = dve.tensor_copy(ixf[:, k], i8[:, :, k])
            link(last)
            for b in range(B):
                for k in range(NK):
                    last = dve.tensor_tensor(
                        oh[:, b, k], io[:].unsqueeze(1).to_broadcast([P, QT, E_]),
                        ixf[:, k, b * QT:(b + 1) * QT].unsqueeze(2).to_broadcast([P, QT, E_]), ALU.is_equal)
            last.then_inc(oh_done, 1)
            dve.wait_ge(cum_done, 1)
            tot = pt[:].rearrange("p (b s e) -> p b s e", b=B, e=E_)
            link(dve.memset(ca[:, :, 0:1], 0.0))
            link(dve.tensor_copy(ca[:, :, 1:SEQ], tot[:, :, 0:SEQ - 1]))
            a, c, step = ca, cb, 1
            while step < SEQ:
                dve.tensor_copy(c[:, :, 0:step], a[:, :, 0:step])
                link(dve.tensor_tensor(c[:, :, step:SEQ], a[:, :, step:SEQ], a[:, :, 0:SEQ - step], ALU.add))
                a, c, step = c, a, step * 2
            link(dve.tensor_tensor(pos[:], pc[:].rearrange("p (b s e) -> p b s e", b=B, e=E_), a[:], ALU.add))
            link(dve.tensor_tensor(c[:], pos[:], oh[:].rearrange("p b k t e -> p b (k t) e"), ALU.mult))
            link(dve.tensor_reduce(pf[:].rearrange("p b k t -> p b (k t)"), c[:], AX, ALU.add))
            for b in range(B):
                for k in range(NK):
                    last = dve.tensor_scalar(base[:, b, k], ixf[:, k, b * QT:(b + 1) * QT], float(ROWS),
                                             float(b * CAP - 1), ALU.mult, ALU.add)
            link(last)
            link(dve.tensor_scalar(of[:], pf[:], float(CAP), float(E_ * ROWS), ALU.is_gt, ALU.mult))
            link(dve.tensor_scalar(g[:], pf[:], float(CAP), None, ALU.min))
            link(dve.tensor_tensor(of[:], of[:], pf[:], ALU.add))
            dve.tensor_tensor(slot_s[:], of[:], base[:], ALU.add)
            dve.tensor_tensor(slot_g[:], g[:], base[:], ALU.add)
            dve.wait_ge(e2_done, 1)
            link(dve.tensor_scalar(den[:], e2[:], 1.0, None, ALU.add))
            link(dve.reciprocal(prob[:, 0], den[:]))
            link(dve.tensor_tensor(prob[:, 1], e2[:], prob[:, 0], ALU.mult))


HT = HID_E // P
XT = -(-ROWS // P)
LAST = ROWS - (XT - 1) * P


def experts(nc, sem, X, slot_s, ein, eout, wfc, bfc, wgate, bgate, wproj, bproj, ident):
    chunks = [(t, min(SUB, XT - t)) for t in range(0, XT, SUB)]
    NCH = len(chunks)
    assert NCH * 2 % 2 == 0

    def width(t, k):
        return min(ROWS, (t + k) * P) - t * P

    with ExitStack() as ctx:
        sb = lambda n, s, t: ctx.enter_context(nc.sbuf_tensor("E_" + n, s, t))
        wf = sb("wf", [P, 2, KC, HID_E], F32)
        wg = sb("wg", [P, 2, KC, HID_E], F32)
        wp = sb("wp", [P, 2, HT, D], F32)
        bf = sb("bf", [P, 2, HT], F32)
        bg = sb("bg", [P, 2, HT], F32)
        bp = sb("bp", [P, 2, D], F32)
        xin = sb("xin", [P, 2, XT, D], F32)
        xT = sb("xT", [P, 2, KC, CH], F32)
        hs = sb("hs", [P, 2, CH], F32)
        z = sb("z", [P, 2, CH], F32)
        a = sb("a", [P, HT, CH], F32)
        ob = sb("ob", [P, SUB, D], F32)
        idf = sb("idf", [P, P], F32)
        pT = [ctx.enter_context(nc.psum_tensor(f"E_pT{i}", [P, CH], F32)) for i in range(2)]
        pH = [ctx.enter_context(nc.psum_tensor(f"E_pH{i}", [P, CH], F32)) for i in range(2)]
        pG = [ctx.enter_context(nc.psum_tensor(f"E_pG{i}", [P, CH], F32)) for i in range(2)]
        pO = [ctx.enter_context(nc.psum_tensor(f"E_pO{i}", [P, CH], F32)) for i in range(2)]
        c_in, sent, e_in, e_used = sem("E_c_in"), sem("E_sent"), [sem(f"E_in{i}") for i in range(2)], sem("E_used")
        t_done, xt_done, hg_done, hs_done = sem("E_t"), sem("E_xt"), sem("E_hg"), sem("E_hs")
        fence = sem("E_fence")
        z_done, a_done, o_mm, o_done, o_out = sem("E_z"), sem("E_a"), sem("E_omm"), sem("E_od"), sem("E_out")
        block = ctx.enter_context(nc.Block())
        LOADS = 8

        @block.gpsimd
        def _(pool):
            for b in range(B):
                for k in range(TOPK):
                    for q in range(S // P):
                        pool.indirect_dma_start(ein, bass.IndirectOffsetOnAxis(slot_s[:, b, k, q:q + 1], 0),
                                                X[:, b * (S // P) + q], None, bounds_check=E_ * ROWS - 1,
                                                oob_is_err=False).then_inc(sent, 16)
            pool.wait_ge(sent, 16 * B * TOPK * (S // P))

            def load(e, s):
                rows = e * ROWS
                pool.dma_start(xin[:, s, 0:XT - 1], ein[ds(rows, (XT - 1) * P), :].rearrange("(t p) c -> p t c", p=P)
                               ).then_inc(e_in[s], 16)
                pool.dma_start(xin[0:LAST, s, XT - 1], ein[ds(rows + (XT - 1) * P, LAST), :]).then_inc(e_in[s], 16)
                for w, src, kc in ((wf, wfc, KC), (wg, wgate, KC), (wp, wproj, HT)):
                    pool.dma_start(w[:, s], src[ds(e * kc * P, kc * P), :].rearrange("(k p) n -> p k n", p=P)
                                   ).then_inc(e_in[s], 16)
                pool.dma_start(bf[:, s], bfc[ds(e * P, P), :]).then_inc(e_in[s], 16)
                pool.dma_start(bg[:, s], bgate[ds(e * P, P), :]).then_inc(e_in[s], 16)
                pool.dma_start(bp[:, s], bproj[ds(e, 1), :].to_broadcast([P, D])).then_inc(e_in[s], 16)

            with pool.Fori(0, E_ // 2) as pair:
                for s in range(2):
                    wait_apart(pool, e_used, pair * 2 + s + 1, fence)
                    load(pair * 2 + s, s)

        def every(eng, body):
            with eng.Fori(0, E_ // 2) as pair:
                for s in range(2):
                    e = pair * 2 + s
                    for c, (t, k) in enumerate(chunks):
                        body(pair, e, s, c, t, k, width(t, k), e * NCH + c, (s * NCH + c) % 2)

        @block.tensor
        def _(pe):
            pe.sem_inc(e_used, 2)
            pe.wait_ge(c_in, 16)

            def body(pair, e, s, c, t, k, w, q, par):
                if c == 0:
                    pe.wait_ge(e_in[s], (pair + 1) * (16 * LOADS))
                pe.wait_ge(xt_done, q)
                for h in range(KC):
                    for j in range(k):
                        r = min(P, ROWS - (t + j) * P)
                        last = pe.transpose(pT[h][:, j * P:j * P + r], xin[0:r, s, t + j, h * P:(h + 1) * P],
                                            idf[0:r, 0:r])
                last.then_inc(t_done, 1)
                pe.wait_ge(xt_done, q + 1)
                for ht in range(HT):
                    pe.wait_ge(z_done, q * HT + ht + 1)
                    for bank, wt in ((pH, wf), (pG, wg)):
                        for kc in range(KC):
                            last = pe.matmul(bank[ht % 2][:, 0:w], wt[:, s, kc, ht * P:(ht + 1) * P],
                                             xT[:, par, kc, 0:w], start=kc == 0, stop=kc == KC - 1)
                    last.then_inc(hg_done, 1)
                pe.wait_ge(a_done, (q + 1) * HT + 2)
                pe.wait_ge(o_done, q)
                for j in range(k):
                    r = min(P, ROWS - (t + j) * P)
                    for ht in range(HT):
                        last = pe.matmul(pO[j // 2][0:r, j % 2 * D:(j % 2 + 1) * D], a[:, ht, j * P:j * P + r],
                                         wp[:, s, ht], start=ht == 0, stop=ht == HT - 1)
                last.then_inc(o_mm, 1)
                if c == NCH - 1:
                    pe.wait_ge(o_done, q + 1)
                    pe.sem_inc(e_used, 1)
            every(pe, body)

        @block.scalar
        def _(act):
            def silu(q, ht, w):
                act.wait_ge(z_done, q * HT + ht + 3)
                act.activation(a[:, ht, 0:w], z[:, ht % 2, 0:w], ACT.Silu).then_inc(a_done, 1)

            def body(pair, e, s, c, t, k, w, q, par):
                act.wait_ge(t_done, q + 1)
                for h in range(KC):
                    last = act.activation(xT[:, par, h, 0:w], pT[h][:, 0:w], ACT.Copy)
                last.then_inc(xt_done, 1)
                for ht in range(HT):
                    act.wait_ge(hg_done, q * HT + ht + 1)
                    act.activation(hs[:, ht % 2, 0:w], pH[ht % 2][:, 0:w], ACT.Identity, bias=bf[:, s, ht:ht + 1]
                                   ).then_inc(hs_done, 1)
                    if ht == 0:
                        act.wait_ge(o_mm, q)
                    else:
                        silu(q, ht - 1, w)
                silu(q, HT - 1, w)
            every(act, body)

        @block.vector
        def _(dve):
            dve.sem_inc(z_done, 2)
            dve.sem_inc(a_done, 2)

            def body(pair, e, s, c, t, k, w, q, par):
                for ht in range(HT):
                    dve.wait_ge(hs_done, q * HT + ht + 1)
                    dve.wait_ge(a_done, q * HT + ht + 1)
                    dve.scalar_tensor_tensor(z[:, ht % 2, 0:w], pG[ht % 2][:, 0:w], bg[:, s, ht:ht + 1],
                                             hs[:, ht % 2, 0:w], ALU.add, ALU.mult).then_inc(z_done, 1)
                dve.wait_ge(o_mm, q + 1)
                dve.wait_ge(o_out, e * (16 * (NCH + 1)) + 16 * c)
                for j in range(k):
                    r = min(P, ROWS - (t + j) * P)
                    last = dve.tensor_tensor(ob[0:r, j], pO[j // 2][0:r, j % 2 * D:(j % 2 + 1) * D], bp[0:r, s], ALU.add)
                last.then_inc(o_done, 1)
            every(dve, body)

        @block.sync
        def _(sp):
            sp.dma_start(idf[:], ident).then_inc(c_in, 16)

            def body(pair, e, s, c, t, k, w, q, par):
                sp.wait_ge(o_done, q + 1)
                rows = e * ROWS + t * P
                whole = k if w == k * P else k - 1
                sp.dma_start(eout[ds(rows, whole * P), :].rearrange("(t p) c -> p t c", p=P), ob[:, 0:whole]
                             ).then_inc(o_out, 16)
                if whole < k:
                    sp.dma_start(eout[ds(rows + whole * P, LAST), :], ob[0:LAST, whole]).then_inc(o_out, 16)
            every(sp, body)
            sp.wait_ge(o_out, 16 * (NCH + 1) * E_)


def combine_and_project(nc, sem, X, eout, slot_g, prob, cos, sin, wq, wqs, wdown, wk, wks, wv, ident,
                        qh, ql, kh, kl, vs):
    LAT = wdown.shape[1]
    QT = S // P
    RJ = 2 * KC
    PER = 1 + (SUB - 1) + 2 * RJ + 3
    STORES = 2 * RJ + SUB
    with ExitStack() as ctx:
        sb = lambda n, s, t: ctx.enter_context(nc.sbuf_tensor("F_" + n, s, t))
        Y = sb("Y", [P, NT, TOPK, D], F32)
        y = sb("y", [P, SUB, D], F32)
        xn = sb("xn", [P, SUB, D], F32)
        xnT = sb("xnT", [P, KC, CH], F32)
        lat = sb("lat", [LAT, CH], F32)
        st = sb("st", [P, SUB, 6], F32)
        mv = sb("mv", [P, SUB, 2], F32)
        sd = sb("sd", [P, SUB], F32)
        rs = sb("rs", [P, SUB], F32)
        eps = sb("eps", [P, 1], F32)
        idf = sb("idf", [P, P], F32)
        wt = {n: sb("w" + n, [P, KC, D], F32) for n in ("q", "qs")}
        wd = sb("wd", [P, KC, LAT], F32)
        wkt = {n: sb("w" + n, [LAT, D], F32) for n in ("k", "ks", "v")}
        co = sb("co", [P, S], F32)
        si = sb("si", [P, S], F32)
        t1 = sb("t1", [P, CH], F32)
        t2 = sb("t2", [P, CH], F32)
        r = sb("r", [P, 2, CH], F32)
        hi = sb("hi", [P, RJ, CH], F32R)
        lo = sb("lo", [P, RJ, CH], F32R)
        v = sb("v", [P, SUB, NH, VW], F32)
        pb = [ctx.enter_context(nc.psum_tensor(f"F_pb{i}", [P, CH], F32)) for i in range(8)]
        c_in, got, eps_set = sem("F_c_in"), sem("F_got"), sem("F_eps")
        var_done, sd_done, n_done, x_copied = sem("F_var"), sem("F_sd"), sem("F_n"), sem("F_xc")
        t_done, xt_done, l_done, lat_done = sem("F_t"), sem("F_xt"), sem("F_l"), sem("F_lat")
        r_mm, r_read, r_done, hi_done, lo_done = sem("F_rmm"), sem("F_rr"), sem("F_r"), sem("F_hi"), sem("F_lo")
        v_mm, v_done, stored, dch, fence = sem("F_vmm"), sem("F_v"), sem("F_st"), sem("F_dch"), sem("F_fence")
        block = ctx.enter_context(nc.Block())

        def chunks(eng, body):
            with eng.Fori(0, B) as b:
                with eng.Fori(0, CPB) as c:
                    body(b * CPB + c, b, c)

        @block.gpsimd
        def _(pool):
            pool.memset(eps[:], EPS).then_inc(eps_set, 1)
            pool.memset(v[:], 1.0).then_inc(eps_set, 1)
            for b in range(B):
                for q in range(QT):
                    for k in range(TOPK):
                        pool.indirect_dma_start(Y[:, b * QT + q, k], None, eout,
                                                bass.IndirectOffsetOnAxis(slot_g[:, b, k, q:q + 1], 0),
                                                bounds_check=E_ * ROWS - 1, oob_is_err=False).then_inc(got, 16)

        @block.tensor
        def _(pe):
            pe.wait_ge(c_in, 16 * 9)

            def body(n, b, c):
                pe.wait_ge(n_done, n + 1)
                for kc in range(KC):
                    for s in range(SUB):
                        last = pe.transpose(pb[kc][:, s * P:(s + 1) * P], xn[:, s, kc * P:(kc + 1) * P], idf[:])
                last.then_inc(t_done, 1)
                pe.wait_ge(xt_done, n + 1)
                pe.wait_ge(v_done, n)
                for kc in range(KC):
                    last = pe.matmul(pb[2][0:LAT], wd[:, kc], xnT[:, kc], start=kc == 0, stop=kc == KC - 1)
                last.then_inc(l_done, 1)
                for j in range(RJ):
                    pe.wait_ge(r_read, n * RJ + j + 1)
                    m = j % KC
                    if j == KC:
                        pe.wait_ge(lat_done, n + 1)
                    for i, name in enumerate(("q", "qs") if j < KC else ("k", "ks")):
                        bank = pb[3 + 2 * (j % 2) + i]
                        if j < KC:
                            for kc in range(KC):
                                last = pe.matmul(bank[:], wt[name][:, kc, m * P:(m + 1) * P], xnT[:, kc],
                                                 start=kc == 0, stop=kc == KC - 1)
                        else:
                            last = pe.matmul(bank[:], wkt[name][:, m * P:(m + 1) * P], lat[:], start=True, stop=True)
                    last.then_inc(r_mm, 1)
                for s in range(SUB):
                    last = pe.matmul(pb[(7, 2)[s // 2]][:, s % 2 * D:(s % 2 + 1) * D], lat[:, s * P:(s + 1) * P],
                                     wkt["v"][:], start=True, stop=True)
                last.then_inc(v_mm, 1)
            chunks(pe, body)

        @block.scalar
        def _(act):
            act.wait_ge(eps_set, 2)

            def body(n, b, c):
                act.wait_ge(var_done, n + 1)
                act.activation(sd[:], mv[:, :, 1], ACT.Sqrt, bias=eps[:]).then_inc(sd_done, 1)
                act.wait_ge(n_done, n + 1)
                act.activation(X[:, ds(n * SUB, SUB), :], xn[:], ACT.Copy).then_inc(x_copied, 1)
                act.wait_ge(t_done, n + 1)
                act.wait_ge(v_mm, n)
                for kc in range(KC):
                    last = act.activation(xnT[:, kc], pb[kc][:], ACT.Copy)
                last.then_inc(xt_done, 1)
                act.wait_ge(l_done, n + 1)
                act.activation(lat[:], pb[2][0:LAT], ACT.Copy).then_inc(lat_done, 1)
                act.wait_ge(stored, n * (16 * STORES))
                for j in range(RJ):
                    act.wait_ge(r_done, n * RJ + j + 1)
                    act.activation(hi[:, j], r[:, j % 2], ACT.Copy).then_inc(hi_done, 1)
                act.wait_ge(v_mm, n + 1)
                for s in range(SUB):
                    last = act.activation(v[:, s, :, 0:HD], pb[(7, 2)[s // 2]][:, s % 2 * D:(s % 2 + 1) * D].rearrange(
                        "p (h e) -> p h e", e=HD), ACT.Copy)
                last.then_inc(v_done, 1)
            chunks(act, body)

        @block.vector
        def _(dve):
            ch = Chain(dve, dch, 2 * SUB + 2 + SUB - 1 + RJ - 1)
            dve.wait_ge(c_in, 16 * 9)
            dve.wait_ge(got, 16 * NT * TOPK)
            dve.sem_inc(r_read, 2)

            def body(n, b, c):
                ch.start(n)
                for s in range(SUB):
                    tile = n * SUB + s
                    t0 = Y[:, ds(tile, 1), 0, :].rearrange("p o c -> p (o c)")
                    ch.link(dve.scalar_tensor_tensor(y[:, s], t0, prob[:, 0, ds(tile, 1)],
                                                     X[:, ds(tile, 1), :].rearrange("p o c -> p (o c)"),
                                                     ALU.mult, ALU.add))
                for s in range(SUB):
                    tile = n * SUB + s
                    t0 = Y[:, ds(tile, 1), 1, :].rearrange("p o c -> p (o c)")
                    ch.link(dve.scalar_tensor_tensor(y[:, s], t0, prob[:, 1, ds(tile, 1)], y[:, s],
                                                     ALU.mult, ALU.add))
                for s in range(SUB):
                    last = dve.bn_stats(st[:, s], y[:, s])
                ch.link(last)
                dve.sem_inc(fence, 1)
                for s in range(SUB):
                    last = dve.bn_aggr(mv[:, s], st[:, s])
                last.then_inc(var_done, 1)
                dve.wait_ge(sd_done, n + 1)
                ch.link(dve.reciprocal(rs[:], sd[:]))
                dve.wait_ge(x_copied, n)
                dve.wait_ge(t_done, n)
                for s in range(SUB):
                    last = dve.tensor_scalar(xn[:, s], y[:, s], mv[:, s, 0:1], rs[:, s:s + 1], ALU.subtract, ALU.mult)
                    if s == SUB - 1:
                        last.then_inc(n_done, 1)
                    else:
                        ch.link(last)
                for j in range(RJ):
                    dve.wait_ge(r_mm, n * RJ + j + 1)
                    main, swap = pb[3 + 2 * (j % 2)], pb[4 + 2 * (j % 2)]
                    dve.tensor_tensor(t1[:], main[:], co[:, ds(c * CH, CH)], ALU.mult)
                    last = dve.tensor_tensor(t2[:], swap[:], si[:, ds(c * CH, CH)], ALU.mult)
                    last.then_inc(r_read, 1)
                    dve.wait_ge(r_read, n * RJ + j + 3)
                    dve.tensor_tensor(r[:, j % 2], t1[:], t2[:], ALU.add).then_inc(r_done, 1)
                    dve.wait_ge(hi_done, n * RJ + j + 1)
                    last = dve.tensor_tensor(lo[:, j], r[:, j % 2], hi[:, j].bitcast(F32), ALU.subtract)
                    if j == RJ - 1:
                        last.then_inc(lo_done, 1)
                    else:
                        ch.link(last)
                ch.end()
            chunks(dve, body)
            dve.wait_ge(x_copied, TOK // CH)

        @block.sync
        def _(sp):
            sp.dma_start(idf[:], ident).then_inc(c_in, 16)
            for n, src in (("q", wq), ("qs", wqs)):
                sp.dma_start(wt[n][:], src.rearrange("(kc p) n -> p kc n", p=P)).then_inc(c_in, 16)
            sp.dma_start(wd[:], wdown.rearrange("(kc p) n -> p kc n", p=P)).then_inc(c_in, 16)
            for n, src in (("k", wk), ("ks", wks), ("v", wv)):
                sp.dma_start(wkt[n][:], src).then_inc(c_in, 16)
            sp.dma_start(co[:], cos).then_inc(c_in, 16)
            sp.dma_start(si[:], sin).then_inc(c_in, 16)
            vs_v = vs.rearrange("(bb g t) e -> bb t g e", bb=B, g=NG)

            def body(n, b, c):
                sp.wait_ge(lo_done, n + 1)
                for j in range(RJ):
                    for dst, src in (((qh, hi), (ql, lo)) if j < KC else ((kh, hi), (kl, lo))):
                        sp.dma_start(dst[ds(b * D + j % KC * P, P), ds(c * CH, CH)], src[:, j].bitcast(F32)
                                     ).then_inc(stored, 16)
                sp.wait_ge(v_done, n + 1)
                for s in range(SUB):
                    sp.dma_start(vs_v[ds(b, 1), ds(c * CH + s * P, P)].rearrange("o t g e -> (o t) g e"),
                                 v[:, s]).then_inc(stored, 16)
            chunks(sp, body)
            sp.wait_ge(stored, 16 * STORES * (TOK // CH))


LH, LD = 8, 64
INNER = LH * LD
WIN = S // P
VE = LD + 1
HIDF = int(D * 4 * 2 / 3)
FT = -(-HIDF // P)
FLAST = HIDF - (FT - 1) * P
PADS = S + 1
PADW = S + P
PAIRS = INNER // P


def tiles(eng, body):
    with eng.Fori(0, B) as b:
        with eng.Fori(0, WIN // 2) as pair:
            for u in range(2):
                body(b * WIN + pair * 2 + u, b, pair * 2 + u, b * (WIN // 2) + pair, u)


def local_projections(nc, sem, tag, xp, wqkv, tab, scales, ident, qT, kT, ve):
    W2 = 2 * INNER
    NB = 2 * LH
    with ExitStack() as ctx:
        sb = lambda n, s, t: ctx.enter_context(nc.sbuf_tensor(tag + n, s, t))
        w = sb("w", [P, KC, 3 * INNER], F32)
        h = sb("h", [P, 2, D], F32)
        hT = sb("hT", [P, 2, KC, P], F32)
        tb = sb("tb", [P, 4, WIN, LD], F32)
        sc = sb("sc", [P, 2, LD], F32)
        A = sb("A", [P, 2, WIN, LD], F32)
        R = sb("R", [P, 2, WIN, LD], F32)
        sq = sb("sq", [P, 2, W2], F32)
        ss = sb("ss", [P, 2, NB], F32)
        nr = sb("nr", [P, 2, NB], F32)
        rn = sb("rn", [P, 2, NB], F32)
        qn = sb("qn", [P, 2, 2, LH, LD], F32)
        t1 = sb("t1", [P, 2, 2, LH, LD], F32)
        t2 = sb("t2", [P, 2, 2, LH, LD], F32)
        v = sb("v", [P, 2, LH, VE], F32)
        tT = sb("tT", [P, 2, 2, PAIRS, P], F32)
        idf = sb("idf", [P, P], F32)
        pqk = [ctx.enter_context(nc.psum_tensor(f"{tag}pqk{u}", [P, 2, CH], F32)) for u in range(2)]
        pv = [ctx.enter_context(nc.psum_tensor(f"{tag}pv{u}", [P, CH], F32)) for u in range(2)]
        ph = [ctx.enter_context(nc.psum_tensor(f"{tag}ph{u}", [P, CH], F32)) for u in range(2)]
        c_in, h_in, v_set = sem(tag + "c_in"), [sem(f"{tag}h_in{u}") for u in range(2)], sem(tag + "vs")
        t_done, ht_done, qk_mm, v_mm = sem(tag + "t"), sem(tag + "ht"), sem(tag + "qkmm"), sem(tag + "vmm")
        sq_done, ss_done, nr_done, qn_done = sem(tag + "sq"), sem(tag + "ss"), sem(tag + "nr"), sem(tag + "qn")
        t2_done, r_done, qt_done, ev_done = sem(tag + "t2"), sem(tag + "r"), sem(tag + "qt"), sem(tag + "ev")
        v_done, stored, dch = sem(tag + "v"), [sem(f"{tag}st{u}") for u in range(2)], sem(tag + "dch")
        pch, tabs = sem(tag + "pch"), sem(tag + "tabs")
        block = ctx.enter_context(nc.Block())
        NST = 3

        def pairs(eng, body):
            with eng.Fori(0, B) as b:
                with eng.Fori(0, WIN // 2) as pair:
                    body(b * (WIN // 2) + pair, b, pair)

        @block.sync
        def _(sp):
            sp.dma_start(w[:], wqkv.rearrange("(kc p) n -> p kc n", p=P)).then_inc(c_in, 16)
            sp.dma_start(tb[:], tab.rearrange("(k w p) d -> p k w d", p=P, w=WIN)).then_inc(c_in, 16)
            sp.dma_start(sc[:].rearrange("p k d -> p (k d)"), scales.to_broadcast([P, 2 * LD])).then_inc(c_in, 16)
            sp.dma_start(idf[:], ident).then_inc(c_in, 16)

            def body(m, b, pair):
                for u in range(2):
                    sp.wait_ge(t_done, m * 2 + u)
                    row = b * PADS + pair * (2 * P) + u * P
                    sp.dma_start(h[:, u, 0:P], xp[ds(row + 1, P), 0:P]).then_inc(h_in[u], 16)
                    sp.dma_start(h[:, u, P:D], xp[ds(row, P), P:D]).then_inc(h_in[u], 16)
                for u in range(2):
                    sp.wait_ge(ev_done, m * 2 + u + 1)
                    col = P + pair * (2 * P) + u * P
                    sp.dma_start(qT[ds(b * INNER, INNER), ds(pair * (2 * P) + u * P, P)].rearrange(
                        "(g p) t -> p g t", p=P), tT[:, u, 0]).then_inc(stored[u], 16)
                    sp.dma_start(kT[ds(b * INNER, INNER), ds(col, P)].rearrange("(g p) t -> p g t", p=P), tT[:, u, 1]
                                 ).then_inc(stored[u], 16)
                    sp.dma_start(ve[ds(b * PADW + col, P), :], v[:, u].rearrange("p h e -> p (h e)")
                                 ).then_inc(stored[u], 16)
            pairs(sp, body)
            for u in range(2):
                sp.wait_ge(stored[u], 16 * NST * (NT // 2))

        @block.tensor
        def _(pe):
            pe.wait_ge(c_in, 64)

            def body(m, b, pair):
                for u in range(2):
                    pe.wait_ge(h_in[u], m * 32 + 32)
                    pe.wait_ge(ht_done, m * 2 + u)
                    for kc in range(KC):
                        last = pe.transpose(ph[u][:, kc * P:(kc + 1) * P], h[:, u, kc * P:(kc + 1) * P], idf[:])
                    last.then_inc(t_done, 1)
                for u in range(2):
                    pe.wait_ge(ht_done, m * 2 + u + 1)
                    pe.wait_ge(ev_done, m * 2)
                    for j in range(3):
                        for kc in range(KC):
                            last = pe.matmul(pqk[u][:, j] if j < 2 else pv[u][:], hT[:, u, kc],
                                             w[:, kc, j * INNER:(j + 1) * INNER], start=kc == 0, stop=kc == KC - 1)
                        if j == 1:
                            last.then_inc(qk_mm, 1)
                    last.then_inc(v_mm, 1)
                for u in range(2):
                    pe.wait_ge(r_done, m * 2 + u + 1)
                    for j in range(2):
                        for g in range(PAIRS):
                            last = pe.transpose(pqk[u][:, j, g * P:(g + 1) * P],
                                                t1[:, u, j].rearrange("p h e -> p (h e)")[:, g * P:(g + 1) * P], idf[:])
                    last.then_inc(qt_done, 1)
            pairs(pe, body)

        @block.scalar
        def _(act):
            act.wait_ge(v_set, 1)

            def body(m, b, pair):
                for u in range(2):
                    act.wait_ge(t_done, m * 2 + u + 1)
                    act.activation(hT[:, u].rearrange("p k t -> p (k t)"), ph[u][:, 0:D], ACT.Copy).then_inc(ht_done, 1)
                for u in range(2):
                    act.wait_ge(qk_mm, m * 2 + u + 1)
                    act.activation(sq[:, u], pqk[u][:].rearrange("p j c -> p (j c)"), ACT.Square).then_inc(sq_done, 1)
                    act.wait_ge(ss_done, m * 2 + u + 1)
                    act.activation(nr[:, u], ss[:, u], ACT.Sqrt).then_inc(nr_done, 1)
                    act.wait_ge(v_mm, m * 2 + u + 1)
                    act.wait_ge(stored[u], m * (16 * NST))
                    act.activation(v[:, u, :, 0:LD], pv[u][:].rearrange("p (h e) -> p h e", e=LD), ACT.Copy
                                   ).then_inc(v_done, 1)
                for u in range(2):
                    act.wait_ge(qt_done, m * 2 + u + 1)
                    act.activation(tT[:, u].rearrange("p j g t -> p j (g t)"), pqk[u][:], ACT.Copy).then_inc(ev_done, 1)
            pairs(act, body)

        @block.gpsimd
        def _(pool):
            pool.wait_ge(tabs, 1)

            def body(m, b, pair):
                for u in range(2):
                    pool.wait_ge(qn_done, m * 2 + u + 1)
                    H = LD // 2
                    for a, z in ((0, H), (H, 0)):
                        last = pool.tensor_tensor(
                            t2[:, u, :, :, a:a + H], qn[:, u, :, :, z:z + H],
                            R[:, :, ds(pair * 2 + u, 1), a:a + H].to_broadcast([P, 2, LH, H]), ALU.mult)
                    last.then_inc(t2_done, 1)
            pairs(pool, body)

        @block.vector
        def _(dve):
            H = LD // 2
            dve.wait_ge(c_in, 64)
            dve.memset(v[:], 1.0).then_inc(v_set, 1)
            for j in range(2):
                dve.tensor_tensor(A[:, j], tb[:, 2 * j], sc[:, j:j + 1].to_broadcast([P, WIN, LD]), ALU.mult)
                for a, z in ((0, H), (H, 0)):
                    last = dve.tensor_tensor(R[:, j, :, a:a + H], tb[:, 2 * j + 1, :, a:a + H],
                                             sc[:, j:j + 1, z:z + H].to_broadcast([P, WIN, H]), ALU.mult)
            last.then_inc(tabs, 1)
            dve.wait_ge(tabs, 1)
            ch = Chain(dve, dch, 6)

            def body(m, b, pair):
                ch.start(m)
                for u in range(2):
                    dve.wait_ge(sq_done, m * 2 + u + 1)
                    dve.tensor_reduce(ss[:, u], sq[:, u].rearrange("p (n e) -> p n e", e=LD), AX, ALU.add
                                      ).then_inc(ss_done, 1)
                    dve.wait_ge(nr_done, m * 2 + u + 1)
                    ch.link(dve.tensor_scalar(nr[:, u], nr[:, u], 1e-12, None, ALU.max))
                    ch.link(dve.reciprocal(rn[:, u], nr[:, u]))
                    dve.wait_ge(t2_done, m * 2 + u)
                    dve.tensor_tensor(qn[:, u].rearrange("p j h e -> p (j h) e"),
                                      pqk[u][:].rearrange("p j (h e) -> p (j h) e", e=LD),
                                      rn[:, u].unsqueeze(2).to_broadcast([P, NB, LD]), ALU.mult).then_inc(qn_done, 1)
                    dve.wait_ge(qn_done, m * 2 + u + 1)
                    dve.wait_ge(qt_done, m * 2)
                    ch.link(dve.tensor_tensor(t1[:, u], qn[:, u],
                                              A[:, :, ds(pair * 2 + u, 1), :].to_broadcast([P, 2, LH, LD]), ALU.mult))
                    dve.wait_ge(t2_done, m * 2 + u + 1)
                    dve.tensor_tensor(t1[:, u], t1[:, u], t2[:, u], ALU.add).then_inc(r_done, 1)
            pairs(dve, body)


def local_attention(nc, sem, tag, qT, kT, ve, wo, masks, ident_bf, ident, X, xp):
    def pos(h):
        return h % 2 * (LH // 2) + h // 2

    HB = LH // 2
    with ExitStack() as ctx:
        sb = lambda n, s, t: ctx.enter_context(nc.sbuf_tensor(tag + n, s, t))
        q = sb("q", [P, 2, PAIRS, P], F32)
        k = sb("k", [P, 2, PAIRS, 2 * P], F32)
        v = sb("v", [P, 2, 2, LH * VE], F32)
        pr = sb("pr", [P, LH, 2 * P], F32)
        pT = sb("pT", [P, 4, 2, 2, P], F32)
        mx = sb("mx", [P, 2, LH], F32)
        nm = sb("nm", [P, 2, LH], F32)
        rc = sb("rc", [P, LH], F32)
        cx = sb("cx", [P, LH, LD], F32)
        cT = sb("cT", [P, PAIRS, P], F32)
        xn = sb("xn", [P, 2, D], F32)
        w = sb("w", [P, PAIRS, D], F32)
        mk = sb("mk", [P, NT, 2 * P], BF16)
        idb = sb("idb", [P, P], BF16)
        idf = sb("idf", [P, P], F32)
        pS = ctx.enter_context(nc.psum_tensor(tag + "pS", [P, LH, 2 * P], F32))
        pP = [ctx.enter_context(nc.psum_tensor(f"{tag}pP{i}", [P, CH], F32)) for i in range(2)]
        pO = [ctx.enter_context(nc.psum_tensor(f"{tag}pO{i}", [P, CH], F32)) for i in range(2)]
        c_in, in_, used = sem(tag + "c_in"), [sem(f"{tag}in{u}") for u in range(2)], sem(tag + "used")
        s_done, m_done, nm_done, e_done = sem(tag + "s"), sem(tag + "m"), sem(tag + "nm"), sem(tag + "e")
        t_done, te_done, o_mm, cx_done = sem(tag + "t"), [sem(f"{tag}te{i}") for i in range(2)], sem(tag + "omm"), sem(tag + "cx")
        ct_mm, ct_done, w_mm, x_done = sem(tag + "ctm"), sem(tag + "ct"), sem(tag + "wmm"), sem(tag + "x")
        fence = sem(tag + "fence")
        x_out, xc, dch = [sem(f"{tag}xo{u}") for u in range(2)], sem(tag + "xc"), sem(tag + "dch")
        block = ctx.enter_context(nc.Block())

        def skewed(eng, first, body):
            first(0, 0)
            with eng.Fori(0, NT // 2 - 1) as m:
                for u in range(2):
                    body(m * 2 + u, m, u, True)
            body(NT - 2, NT // 2 - 1, 0, True)
            body(NT - 1, NT // 2 - 1, 1, False)

        @block.gpsimd
        def _(pool):
            for dst, src in ((w[:], wo.rearrange("(g p) n -> p g n", p=P)), (idb[:], ident_bf), (idf[:], ident),
                             (mk[:], masks.rearrange("(w p) k -> p w k", p=P))):
                pool.dma_start(dst, src).then_inc(c_in, 16)

            def body(n, b, win, m, u):
                wait_apart(pool, used, n + 1, fence)
                pool.dma_start(q[:, u], qT[ds(b * INNER, INNER), ds(win * P, P)].rearrange("(g p) t -> p g t", p=P)
                               ).then_inc(in_[u], 16)
                pool.dma_start(k[:, u], kT[ds(b * INNER, INNER), ds(win * P, 2 * P)].rearrange(
                    "(g p) t -> p g t", p=P)).then_inc(in_[u], 16)
                pool.dma_start(v[:, u], ve[ds(b * PADW + win * P, 2 * P), :].rearrange("(s p) e -> p s e", p=P)
                               ).then_inc(in_[u], 16)
            tiles(pool, body)

        @block.tensor
        def _(pe):
            pe.sem_inc(used, 2)
            pe.wait_ge(c_in, 64)

            def scores(n, u, m):
                pe.wait_ge(in_[u], m * 48 + 48)
                pe.wait_ge(e_done, n)
                for i in range(4):
                    pe.matmul(pS[:, 2 * i:2 * i + 2, :], idb[:], mk[:, ds(n, 1), :].to_broadcast([P, 2, 2 * P]),
                              start=True, stop=False, skip_group_check=True)
                for h in sorted(range(LH), key=pos):
                    a = h % 2 * LD
                    last = pe.matmul(pS[:, pos(h), :], q[a:a + LD, u, h // 2], k[a:a + LD, u, h // 2],
                                     start=False, stop=True, skip_group_check=True)
                last.then_inc(s_done, 1)

            def rest(n, m, u):
                pe.wait_ge(x_done, n)
                pe.wait_ge(e_done, n + 1)
                for r in range(4):
                    if r >= 2:
                        pe.wait_ge(te_done[r % 2], n * 2 + 1)
                    for i in range(2):
                        for s in range(2):
                            last = pe.transpose(pP[r % 2][:, (2 * i + s) * P:(2 * i + s + 1) * P],
                                                pr[:, 2 * r + i, s * P:(s + 1) * P], idf[:])
                    last.then_inc(t_done, 1)
                for r in range(4):
                    pe.wait_ge(te_done[r % 2], n * 2 + r // 2 + 1)
                    for i in range(2):
                        p_ = 2 * r + i
                        h = next(h for h in range(LH) if pos(h) == p_)
                        for s in range(2):
                            last = pe.matmul(pO[h // HB][:, h % HB * VE:(h % HB + 1) * VE], pT[:, r, i, s],
                                             v[:, u, s, h * VE:(h + 1) * VE], start=s == 0, stop=s == 1)
                last.then_inc(o_mm, 1)
                pe.drain().then_inc(used, 1)
                pe.wait_ge(cx_done, n + 1)
                for g in range(PAIRS):
                    last = pe.transpose(pP[0][:, g * P:(g + 1) * P],
                                        cx[:].rearrange("p h e -> p (h e)")[:, g * P:(g + 1) * P], idf[:])
                last.then_inc(ct_mm, 1)
                pe.wait_ge(ct_done, n + 1)
                for g in range(PAIRS):
                    last = pe.matmul(pP[1][:, 0:D], cT[:, g], w[:, g], start=g == 0, stop=g == PAIRS - 1)
                last.then_inc(w_mm, 1)

            def both(n, m, u, nxt):
                if nxt:
                    scores(n + 1, 1 - u, m + u)
                rest(n, m, u)
            skewed(pe, lambda n, m: scores(0, 0, 0), both)

        @block.scalar
        def _(act):
            def exps(n, u):
                act.wait_ge(nm_done, n + 1)
                act.wait_ge(t_done, n * 4)
                for p_ in range(LH):
                    last = act.activation(pr[:, p_], pS[:, p_, :], ACT.Exp, bias=nm[:, u, p_:p_ + 1], scale=8.0)
                last.then_inc(e_done, 1)

            def both(n, m, u, nxt):
                for r in (0, 2):
                    act.wait_ge(t_done, n * 4 + r + 1)
                    act.activation(pT[:, r].rearrange("p i s t -> p (i s t)"), pP[0][:], ACT.Copy
                                   ).then_inc(te_done[0], 1)
                if nxt:
                    exps(n + 1, 1 - u)
                act.wait_ge(ct_mm, n + 1)
                act.activation(cT[:].rearrange("p g t -> p (g t)"), pP[0][:], ACT.Copy).then_inc(ct_done, 1)
                act.wait_ge(x_done, n + 1)
                act.activation(X[:, ds(n, 1), :], xn[:, u:u + 1], ACT.Copy).then_inc(xc, 1)
            skewed(act, lambda n, m: exps(0, 0), both)

        @block.vector
        def _(dve):
            ch = Chain(dve, dch, 1)

            def maxima(n, u):
                dve.wait_ge(s_done, n + 1)
                dve.tensor_reduce(mx[:, u], pS[:], AX, ALU.max).then_inc(m_done, 1)
                dve.wait_ge(m_done, n + 1)
                dve.tensor_scalar(nm[:, u], mx[:, u], -8.0, None, ALU.mult).then_inc(nm_done, 1)

            def both(n, m, u, nxt):
                ch.start(n)
                for r in (1, 3):
                    dve.wait_ge(t_done, n * 4 + r + 1)
                    dve.tensor_copy(pT[:, r].rearrange("p i s t -> p (i s t)"), pP[1][:]).then_inc(te_done[1], 1)
                if nxt:
                    maxima(n + 1, 1 - u)
                dve.wait_ge(o_mm, n + 1)
                o = [pO[i][:, 0:HB * VE].rearrange("p (h e) -> p h e", e=VE) for i in range(2)]
                for i in range(2):
                    last = dve.reciprocal(rc[:, i * HB:(i + 1) * HB], o[i][:, :, LD])
                ch.link(last)
                for i in range(2):
                    last = dve.tensor_tensor(cx[:, i * HB:(i + 1) * HB], o[i][:, :, 0:LD],
                                             rc[:, i * HB:(i + 1) * HB].unsqueeze(2).to_broadcast([P, HB, LD]),
                                             ALU.mult)
                last.then_inc(cx_done, 1)
                dve.wait_ge(w_mm, n + 1)
                dve.wait_ge(x_out[u], m * 16)
                dve.wait_ge(xc, n)
                dve.tensor_tensor(xn[:, u:u + 1], pP[1][:, 0:D].unsqueeze(1), X[:, ds(n, 1), :], ALU.add
                                  ).then_inc(x_done, 1)
            skewed(dve, lambda n, m: maxima(0, 0), both)
            dve.wait_ge(xc, NT)

        @block.sync
        def _(sp):
            def body(n, b, win, m, u):
                sp.wait_ge(x_done, n + 1)
                sp.dma_start(xp[ds(b * PADS + win * P + 1, P), :], xn[:, u]).then_inc(x_out[u], 16)
            tiles(sp, body)
            for u in range(2):
                sp.wait_ge(x_out[u], 16 * (NT // 2))


def gated_unit(nc, sem, tag, xp, lng, lnb, w1, b1a, b1g, w2, b2, ident, X, xp_out, xp_first, out):
    NCK = TOK // CH
    final = out is not None
    with ExitStack() as ctx:
        sb = lambda n, s, t: ctx.enter_context(nc.sbuf_tensor(tag + n, s, t))
        W1 = sb("W1", [P, KC, 2 * HIDF], F32)
        W2 = sb("W2", [P, FT, D], F32)
        g_ = sb("g_", [P, KC], F32)
        b_ = sb("b_", [P, KC], F32)
        ba = sb("ba", [P, FT], F32)
        bg = sb("bg", [P, FT], F32)
        bb = sb("bb", [P, D], F32)
        h = sb("h", [P, 2, SUB, D], F32)
        hn = sb("hn", [P, SUB, D], F32)
        hT = sb("hT", [P, 2, KC, CH], F32)
        gl = sb("gl", [P, 2, CH], F32)
        hid = sb("hid", [P, FT, CH], F32)
        y = sb("y", [P, SUB, D], F32)
        y2 = sb("y2", [P, 2, SUB, D], F32)
        x0 = sb("x0", [P, 2, SUB, D], F32)
        st = sb("st", [P, SUB, 6], F32)
        mv = sb("mv", [P, SUB, 2], F32)
        sd = sb("sd", [P, SUB], F32)
        rs = sb("rs", [P, SUB], F32)
        st2 = sb("st2", [P, SUB, 6], F32)
        mv2 = sb("mv2", [P, SUB, 2], F32)
        sd2 = sb("sd2", [P, SUB], F32)
        rs2 = sb("rs2", [P, SUB], F32)
        eps = sb("eps", [P, 1], F32)
        idf = sb("idf", [P, P], F32)
        pT = [ctx.enter_context(nc.psum_tensor(f"{tag}pT{i}", [P, CH], F32)) for i in range(2)]
        pA = [ctx.enter_context(nc.psum_tensor(f"{tag}pA{i}", [P, CH], F32)) for i in range(2)]
        pG = [ctx.enter_context(nc.psum_tensor(f"{tag}pG{i}", [P, CH], F32)) for i in range(2)]
        pO = [ctx.enter_context(nc.psum_tensor(f"{tag}pO{i}", [P, CH], F32)) for i in range(2)]
        c_in, h_in = sem(tag + "c_in"), [sem(f"{tag}h_in{u}") for u in range(2)]
        var, sdd, n_done, t_done = sem(tag + "var"), sem(tag + "sdd"), sem(tag + "n"), sem(tag + "t")
        xt_done, ag_mm, gl_done, hid_done = sem(tag + "xt"), sem(tag + "ag"), sem(tag + "gl"), sem(tag + "hid")
        o_mm, y_done, x_done, xc = sem(tag + "omm"), sem(tag + "y"), sem(tag + "x"), sem(tag + "xc")
        var2, sdd2, eps_set = sem(tag + "var2"), sem(tag + "sdd2"), sem(tag + "eps")
        fence = sem(tag + "fence")
        dch, och, x_out = sem(tag + "dch"), sem(tag + "och"), [sem(f"{tag}xo{u}") for u in range(2)]
        block = ctx.enter_context(nc.Block())
        x0_in, x_free = [sem(f"{tag}x0{u}") for u in range(2)], sem(tag + "xf")
        NC_IN = 9

        def skewed(eng, first, body):
            first(0)
            with eng.Fori(0, NCK // 2 - 1) as m:
                for u in range(2):
                    body(m * 2 + u, m, u, True)
            body(NCK - 2, NCK // 2 - 1, 0, True)
            body(NCK - 1, NCK // 2 - 1, 1, False)

        def chunks(eng, body):
            with eng.Fori(0, B) as b:
                with eng.Fori(0, CPB // 2) as pair:
                    for u in range(2):
                        body(b * CPB + pair * 2 + u, b, pair * 2 + u, b * (CPB // 2) + pair, u)

        def rows(j):
            return P if j < FT - 1 else FLAST

        @block.gpsimd
        def _(pool):
            pool.memset(eps[:], EPS).then_inc(eps_set, 1)
            for dst, src in ((W1[:], w1.rearrange("(kc p) n -> p kc n", p=P)),
                             (W2[:, 0:FT - 1], w2[0:(FT - 1) * P, :].rearrange("(k p) n -> p k n", p=P)),
                             (W2[0:FLAST, FT - 1], w2[(FT - 1) * P:HIDF, :]), (g_[:], lng), (b_[:], lnb),
                             (ba[:], b1a), (bg[:], b1g), (bb[:], b2.to_broadcast([P, D])), (idf[:], ident)):
                pool.dma_start(dst, src).then_inc(c_in, 16)

            def body(n, b, c, m, u):
                wait_apart(pool, n_done, n, fence)
                row = b * PADS + c * CH
                pool.dma_start(h[:, u, :, 0:P], xp[ds(row + 1, CH), 0:P].rearrange("(s p) c -> p s c", p=P)
                               ).then_inc(h_in[u], 16)
                pool.dma_start(h[:, u, :, P:D], xp[ds(row, CH), P:D].rearrange("(s p) c -> p s c", p=P)
                               ).then_inc(h_in[u], 16)
                if final:
                    wait_apart(pool, x_free, n + 1, fence)
                    pool.dma_start(x0[:, u], xp_first[ds(row + 1, CH), :].rearrange("(s p) c -> p s c", p=P)
                                   ).then_inc(x0_in[u], 16)
            chunks(pool, body)

        @block.tensor
        def _(pe):
            pe.wait_ge(c_in, 16 * NC_IN)

            def turn(n):
                pe.wait_ge(n_done, n + 2)
                pe.wait_ge(xt_done, n)
                for kc in range(KC):
                    for s in range(SUB):
                        last = pe.transpose(pT[kc][:, s * P:(s + 1) * P], hn[:, s, kc * P:(kc + 1) * P], idf[:])
                last.then_inc(t_done, 1)

            def body(n, m, u, nxt):
                pe.wait_ge(xt_done, n + 1)
                for j in range(FT):
                    pe.wait_ge(hid_done, n * FT + j + 1)
                    r = rows(j)
                    for bank, off in ((pG, HIDF), (pA, 0)):
                        for kc in range(KC):
                            last = pe.matmul(bank[j % 2][0:r, :], W1[:, kc, off + j * P:off + j * P + r], hT[:, u, kc],
                                             start=kc == 0, stop=kc == KC - 1)
                    last.then_inc(ag_mm, 1)
                if nxt:
                    turn(n + 1)
                pe.wait_ge(hid_done, (n + 1) * FT + 2)
                pe.wait_ge(y_done, n)
                for s in range(SUB):
                    for j in range(FT):
                        r = rows(j)
                        last = pe.matmul(pO[s // 2][:, s % 2 * D:(s % 2 + 1) * D], hid[0:r, j, s * P:(s + 1) * P],
                                         W2[0:r, j], start=j == 0, stop=j == FT - 1)
                last.then_inc(o_mm, 1)
            skewed(pe, turn, body)

        @block.scalar
        def _(act):
            act.wait_ge(c_in, 16 * NC_IN)
            act.wait_ge(eps_set, 1)

            def norm(n, u):
                act.wait_ge(var, n + 1)
                act.activation(sd[:], mv[:, :, 1], ACT.Sqrt, bias=eps[:]).then_inc(sdd, 1)
                act.wait_ge(t_done, n + 1)
                for kc in range(KC):
                    last = act.activation(hT[:, u, kc], pT[kc][:], ACT.Identity, bias=b_[:, kc:kc + 1],
                                          scale=g_[:, kc:kc + 1])
                last.then_inc(xt_done, 1)

            def body(n, m, u, nxt):
                for j in range(FT):
                    r = rows(j)
                    act.wait_ge(ag_mm, n * FT + j + 1)
                    act.wait_ge(hid_done, n * FT + j + 1)
                    act.activation(gl[0:r, j % 2], pG[j % 2][0:r, :], ACT.Gelu, bias=bg[0:r, j:j + 1]
                                   ).then_inc(gl_done, 1)
                if nxt:
                    norm(n + 1, 1 - u)
                if final:
                    act.wait_ge(var2, n + 1)
                    act.activation(sd2[:], mv2[:, :, 1], ACT.Sqrt, bias=eps[:]).then_inc(sdd2, 1)
                else:
                    act.wait_ge(x_done, n + 1)
                    act.activation(X[:, ds(n * SUB, SUB), :], y2[:, u], ACT.Copy).then_inc(xc, 1)
            skewed(act, lambda n: norm(0, 0), body)

        @block.vector
        def _(dve):
            NL, OL = 2, (4 if final else 0)
            cn, co = Chain(dve, dch, NL), Chain(dve, och, OL)
            dve.wait_ge(c_in, 16 * NC_IN)
            dve.sem_inc(n_done, 1)
            if final:
                dve.sem_inc(x_free, 2)
            dve.sem_inc(hid_done, 2)

            def norm(n, m, u):
                cn.start(n)
                dve.wait_ge(h_in[u], m * 32 + 32)
                for s in range(SUB):
                    last = dve.bn_stats(st[:, s], h[:, u, s])
                cn.link(last)
                dve.sem_inc(fence, 1)
                for s in range(SUB):
                    last = dve.bn_aggr(mv[:, s], st[:, s])
                last.then_inc(var, 1)
                dve.wait_ge(sdd, n + 1)
                cn.link(dve.reciprocal(rs[:], sd[:]))
                dve.wait_ge(t_done, n)
                for s in range(SUB):
                    last = dve.tensor_scalar(hn[:, s], h[:, u, s], mv[:, s, 0:1], rs[:, s:s + 1], ALU.subtract, ALU.mult)
                last.then_inc(n_done, 1)
                cn.end()

            def body(n, m, u, nxt):
                for j in range(FT):
                    r = rows(j)
                    dve.wait_ge(gl_done, n * FT + j + 1)
                    if j == 0:
                        dve.wait_ge(o_mm, n)
                    dve.scalar_tensor_tensor(hid[0:r, j], pA[j % 2][0:r, :], ba[0:r, j:j + 1], gl[0:r, j % 2],
                                             ALU.add, ALU.mult).then_inc(hid_done, 1)
                if nxt:
                    norm(n + 1, m + u, 1 - u)
                co.start(n)
                dve.wait_ge(o_mm, n + 1)
                for k in range(2):
                    last = dve.tensor_tensor(y[:, 2 * k:2 * k + 2], pO[k][:].rearrange("p (s c) -> p s c", c=D),
                                             bb[:].unsqueeze(1).to_broadcast([P, 2, D]), ALU.add)
                last.then_inc(y_done, 1)
                dve.wait_ge(y_done, n + 1)
                dve.wait_ge(x_out[u], m * 16)
                if final:
                    co.link(dve.tensor_tensor(y[:], y[:], X[:, ds(n * SUB, SUB), :], ALU.add))
                    dve.wait_ge(x0_in[u], m * 16 + 16)
                    co.link(dve.tensor_tensor(y[:], y[:], x0[:, u], ALU.add))
                    for s in range(SUB):
                        last = dve.bn_stats(st2[:, s], y[:, s])
                    co.link(last)
                    dve.sem_inc(fence, 1)
                    for s in range(SUB):
                        last = dve.bn_aggr(mv2[:, s], st2[:, s])
                    last.then_inc(var2, 1)
                    dve.wait_ge(sdd2, n + 1)
                    co.link(dve.reciprocal(rs2[:], sd2[:]))
                    for s in range(SUB):
                        last = dve.tensor_scalar(y2[:, u, s], y[:, s], mv2[:, s, 0:1], rs2[:, s:s + 1], ALU.subtract,
                                                 ALU.mult)
                    last.then_inc(x_done, 1)
                    dve.drain().then_inc(x_free, 1)
                else:
                    dve.wait_ge(xc, n)
                    dve.tensor_tensor(y2[:, u], y[:], X[:, ds(n * SUB, SUB), :], ALU.add).then_inc(x_done, 1)
                    co.end()
            skewed(dve, lambda n: norm(0, 0, 0), body)
            if not final:
                dve.wait_ge(xc, NCK)

        @block.sync
        def _(sp):
            def body(n, b, c, m, u):
                sp.wait_ge(x_done, n + 1)
                if final:
                    dst = out[ds(n * CH, CH), :]
                else:
                    dst = xp_out[ds(b * PADS + c * CH + 1, CH), :]
                sp.dma_start(dst.rearrange("(s p) c -> p s c", p=P), y2[:, u]).then_inc(x_out[u], 16)
            chunks(sp, body)
            for u in range(2):
                sp.wait_ge(x_out[u], 16 * (NCK // 2))


def clear_buffers(nc, sem, ein, xps, kT, ve):
    WIDTH = E_ * ROWS * D // P
    CUT = 8
    with ExitStack() as ctx:
        z = ctx.enter_context(nc.sbuf_tensor("Z_z", [P, WIDTH // CUT], F32))
        zeroed, cleared = sem("Z_zeroed"), sem("Z_cleared")
        block = ctx.enter_context(nc.Block())

        @block.vector
        def _(dve):
            dve.memset(z[:], 0.0).then_inc(zeroed, 1)

        @block.sync
        def _(sp):
            sp.wait_ge(zeroed, 1)
            flat = ein.rearrange("r c -> (r c)").rearrange("(p w) -> p w", p=P)
            n = 0
            for i in range(CUT):
                sp.dma_start(flat[:, i * (WIDTH // CUT):(i + 1) * (WIDTH // CUT)], z[:]).then_inc(cleared, 16)
                n += 1
            for b in range(B):
                for xp in xps:
                    sp.dma_start(xp[b * PADS:b * PADS + 1, :], z[0:1, 0:D]).then_inc(cleared, 16)
                    n += 1
                sp.dma_start(ve[b * PADW:b * PADW + P, :], z[:, 0:LH * VE]).then_inc(cleared, 16)
                sp.dma_start(kT[b * INNER:(b + 1) * INNER, 0:P].rearrange("(g p) t -> p g t", p=P),
                             z[:, 0:PAIRS * P].rearrange("p (g t) -> p g t", g=PAIRS)).then_inc(cleared, 16)
                n += 2
            sp.wait_ge(cleared, 16 * n)


def build(nc, d, out):
    with ExitStack() as ctx:
        taken = []

        def sem(name):
            taken.append(nc.alloc_semaphore(name))
            return taken[-1]

        def clear_semaphores():
            nc.all_engine_barrier()
            nc.clear_and_free_semaphores(taken)
            nc.all_engine_barrier()
            taken.clear()

        keep = lambda n, s, t=F32: ctx.enter_context(nc.sbuf_tensor(n, s, t))
        scratch = lambda n, s: nc.dram_tensor(n, s, F32).ap()
        X = keep("X", [P, NT, D])
        LG = keep("LG", [P, NT, E_])
        slot_s = keep("slot_s", [P, B, TOPK, S // P], U32)
        slot_g = keep("slot_g", [P, B, TOPK, S // P], U32)
        prob = keep("prob", [P, TOPK, NT])
        ein, eout = scratch("ein", (E_ * ROWS, D)), scratch("eout", (E_ * ROWS, D))
        xp = [scratch(f"xp{i}", (B * PADS, D)) for i in range(3)]
        lqT, lkT = scratch("lqT", (B * INNER, S)), scratch("lkT", (B * INNER, PADW))
        lve = scratch("lve", (B * PADW, LH * VE))
        m_rows = scratch("m_rows", (2, GRP * S))
        ot = scratch("ot", (NIT * P, S))

        clear_buffers(nc, sem, ein, xp, lkT, lve)
        qh, ql = scratch("qh0", (B * D, S)), scratch("ql0", (B * D, S))
        kh, kl = scratch("kh0", (B * NKV * HD, S)), scratch("kl0", (B * NKV * HD, S))
        vs = scratch("vs0", (NIT * S, VW))
        layer0_projections(nc, sem, d["xT"], d["a0_wqT"], d["a0_wkT"], d["a0_wvT"], qh, ql, kh, kl, vs)
        attention(nc, sem, "B_", 1, qh, ql, kh, kl, vs, d["causal"], d["causalT"], d["ident_bf"], d["ident"], m_rows, ot)
        attention_output(nc, sem, "C_", ot, d["a0_woT"], d["x"], X, d["ident"], (d["router_w"], d["router_b"], LG), None)
        clear_semaphores()
        route(nc, sem, LG, d["tri"], d["iota8"], d["ones"], slot_s, slot_g, prob)
        experts(nc, sem, X, slot_s, ein, eout, d["w_fc"], d["b_fc"], d["w_gate"], d["b_gate"], d["w_proj"], d["b_proj"],
                d["ident"])
        qh1, ql1 = scratch("qh1", (B * D, S)), scratch("ql1", (B * D, S))
        kh1, kl1 = scratch("kh1", (B * D, S)), scratch("kl1", (B * D, S))
        vs1 = scratch("vs1", (NIT * S, GRP * VW))
        combine_and_project(nc, sem, X, eout, slot_g, prob, d["rope_cos"], d["rope_sin"], d["a1_wq"], d["a1_wqs"],
                            d["a1_wd"], d["a1_wk"], d["a1_wks"], d["a1_wv"], d["ident"], qh1, ql1, kh1, kl1, vs1)
        clear_semaphores()
        attention(nc, sem, "G_", GRP, qh1, ql1, kh1, kl1, vs1, d["paged"], d["pagedT"], d["ident_bf"], d["ident"],
                  m_rows, ot)
        attention_output(nc, sem, "H_", ot, d["a1_wo"], None, X, d["ident"], None, xp[0])
        for l in range(2):
            clear_semaphores()
            local_projections(nc, sem, f"I{l}_", xp[0] if l == 0 else xp[2], d[f"l{l}_wqkv"], d["xpos"],
                              d[f"l{l}_scales"], d["ident"], lqT, lkT, lve)
            local_attention(nc, sem, f"J{l}_", lqT, lkT, lve, d[f"l{l}_wo"], d["windows"], d["ident_bf"], d["ident"],
                            X, xp[1])
            gated_unit(nc, sem, f"K{l}_", xp[1], d[f"l{l}_lng"], d[f"l{l}_lnb"], d[f"l{l}_w1"], d[f"l{l}_b1a"],
                       d[f"l{l}_b1g"], d[f"l{l}_w2"], d[f"l{l}_b2"], d["ident"], X, xp[2] if l == 0 else None,
                       xp[0], out if l else None)


def shape_constants():
    c = {}
    i = np.arange(P)
    c["ident"] = np.eye(P, dtype=np.float32)
    c["ones"] = np.ones((P, P), np.float32)
    c["tri"] = (i[:, None] <= i[None, :]).astype(np.float32)
    c["iota8"] = np.tile(np.arange(E_, dtype=np.float32), (P, 1))
    page = i // PAGE
    bf = mybir.dt.np(BF16)
    c["ident_bf"] = np.eye(P).astype(bf)
    causal = np.where(i[None, :] > i[:, None], NEG, 0.0)
    paged = np.where(page[None, :] > page[:, None], NEG, 0.0)
    for name, m in (("causal", causal), ("paged", paged)):
        c[name], c[name + "T"] = m.astype(bf), np.ascontiguousarray(m.T).astype(bf)
    before = np.where(i[None, :] < i[:, None], NEG, 0.0)
    c["windows"] = np.concatenate([np.concatenate([before if t % WIN else np.full((P, P), NEG), causal], 1)
                                   for t in range(NT)]).astype(bf)
    inv = 1.0 / 10000.0 ** (np.arange(0, HD, 2, dtype=np.float32) / HD)
    ang = np.outer(np.arange(S, dtype=np.float32), inv)
    pair = i % HD // 2
    c["rope_cos"] = np.ascontiguousarray(np.cos(ang).T[pair]).astype(np.float32)
    sign = np.where(i % 2 == 0, -1.0, 1.0)[:, None]
    c["rope_sin"] = (np.sin(ang).T[pair] * sign).astype(np.float32)
    half = np.arange(0, LD, 2, dtype=np.float32)
    freq = np.arange(S, dtype=np.float32)[:, None] * (1.0 / 10000.0 ** (half / LD)).astype(np.float32)[None, :]
    freq = np.concatenate([freq, freq], -1)
    base = (half + np.float32(0.4 * LD)) / np.float32(1.4 * LD)
    power = (np.arange(S, dtype=np.float32) - S // 2) / np.float32(P // 2)
    scale = base[None, :] ** power[:, None]
    scale = np.concatenate([scale, scale], -1)
    sign = np.where(np.arange(LD) < LD // 2, -1.0, 1.0)
    cos, sin = np.cos(freq), np.sin(freq) * sign
    c["xpos"] = np.concatenate([cos * scale, sin * scale, cos / scale, sin / scale]).astype(np.float32)
    return c


def laid_out(v):
    a = {k: np.asarray(x) for k, x in v.items()}
    x = a["L0_attn_x"].reshape(TOK, D)
    d = {"x": x, "xT": x.T}
    for n in ("wq", "wk", "wv", "wo"):
        d[f"a0_{n}T"] = a[f"L0_attn_{n}"].T
    cols = lambda w: w.reshape(-1, P).T
    d["router_w"] = a["L0_ffn_router_w"]
    d["router_b"] = np.broadcast_to(a["L0_ffn_router_b"], (P, E_))
    d["w_fc"] = a["L0_ffn_w_c_fc"].reshape(E_ * D, HID_E)
    d["w_gate"] = a["L0_ffn_w_gate"].reshape(E_ * D, HID_E)
    d["w_proj"] = a["L0_ffn_w_c_proj"].reshape(E_ * HID_E, D)
    for n in ("fc", "gate"):
        b = a["L0_ffn_b_c_fc" if n == "fc" else "L0_ffn_b_gate"]
        d[f"b_{n}"] = b.reshape(E_, HT, P).transpose(0, 2, 1).reshape(E_ * P, HT)
    d["b_proj"] = a["L0_ffn_b_c_proj"].reshape(E_, D)
    swap = np.arange(D) ^ 1
    d["a1_wq"], d["a1_wqs"] = a["L1_attn_wq"], a["L1_attn_wq"][:, swap]
    d["a1_wk"], d["a1_wks"] = a["L1_attn_wk_up"], a["L1_attn_wk_up"][:, swap]
    d["a1_wd"], d["a1_wv"], d["a1_wo"] = a["L1_attn_w_down"], a["L1_attn_wv_up"], a["L1_attn_wo"]
    for l in range(2):
        g = lambda n: a["L1_ffn_" + n][l]
        d[f"l{l}_wqkv"], d[f"l{l}_wo"], d[f"l{l}_w1"], d[f"l{l}_w2"] = g("wqkv"), g("wo"), g("w1"), g("w2")
        d[f"l{l}_scales"] = np.concatenate([g("q_scale"), g("k_scale")]).reshape(1, 2 * LD)
        d[f"l{l}_lng"], d[f"l{l}_lnb"] = cols(g("ln_g")), cols(g("ln_b"))
        b1 = np.zeros((2, FT * P), np.float32)
        b1[:, :HIDF] = g("b1").reshape(2, HIDF)
        d[f"l{l}_b1a"], d[f"l{l}_b1g"] = cols(b1[0]), cols(b1[1])
        d[f"l{l}_b2"] = g("b2").reshape(1, D)
    return d


def kernel(**inputs):
    import concourse.bacc as bacc
    from concourse.bass_utils import run_bass_kernel_spmd

    nc = bacc.Bacc("TRN2", target_bir_lowering=False, num_devices=1)
    arrays = {f"in_{k}": np.ascontiguousarray(v) for k, v in {**laid_out(inputs), **shape_constants()}.items()}
    d = {k[3:]: nc.dram_tensor(k, v.shape, mybir.dt.from_np(v.dtype), kind="ExternalInput").ap()
         for k, v in arrays.items()}
    out = nc.dram_tensor("out_0", (TOK, D), F32, kind="ExternalOutput").ap()
    build(nc, d, out)
    r = run_bass_kernel_spmd(nc, [arrays], core_ids=[0])
    return r.results[0]["out_0"].reshape(B, S, D)
```

```python
from contextlib import ExitStack

import numpy as np
import concourse.bass as bass
from concourse import mybir

F32 = mybir.dt.float32
F32R = mybir.dt.float32r
BF16 = mybir.dt.bfloat16
U32 = mybir.dt.uint32
ALU = mybir.AluOpType
ACT = mybir.ActivationFunctionType
AX = mybir.AxisListType.X
ds = bass.ds

P = 128
B, S, D = 2, 2048, 256
TOK = B * S
NT = TOK // P
KC = D // P
CH = 512
CPB = S // CH
SUB = CH // P
NH, HD = 16, 16
GRP = 4
NG = NH // GRP
NIT = B * NG
NKV = 4
VW = 2 * HD
PAGE = 64
NEG = -1e30
EPS = 1e-5


class Semaphores:

    def __init__(self, nc):
        self.nc, self.taken, self.new = nc, [], []

    def __call__(self, name, first=1):
        s = self.nc.alloc_semaphore(name)
        self.new.append((s, first))
        return s

    def start(self):
        for s, first in self.new:
            if first:
                self.nc.gpsimd.sem_inc(s, first)
            self.taken.append(s)
        self.nc.all_engine_barrier()
        self.new = []

    def clear(self):
        self.nc.all_engine_barrier()
        self.nc.clear_and_free_semaphores(self.taken)
        self.nc.all_engine_barrier()
        self.taken = []


def wait_apart(eng, semaphore, value, fence):
    eng.wait_ge(semaphore, value + 1)
    eng.sem_inc(fence, 1)


def layer0_projections(nc, sem, xT, wqT, wkT, wvT, qh, ql, kh, kl, vs):
    NKD = NKV * HD
    STORES = 2 * KC + 2 + SUB
    with ExitStack() as ctx:
        sb = lambda n, s, t: ctx.enter_context(nc.sbuf_tensor("A_" + n, s, t))
        x = sb("x", [P, 2, KC, CH], F32)
        wq = sb("wq", [P, KC, D], F32)
        wk = sb("wk", [P, KC, NKD], F32)
        wv = sb("wv", [P, KC, NKD], F32)
        qhi = sb("qhi", [P, 2, KC, CH], F32R)
        qlo = sb("qlo", [P, 2, KC, CH], F32R)
        khi = sb("khi", [NKD, 2, CH], F32R)
        klo = sb("klo", [NKD, 2, CH], F32R)
        v = sb("v", [P, 2, SUB, NKV, VW], F32)
        bank = [ctx.enter_context(nc.psum_tensor(f"A_b{i}", [P, CH], F32)) for i in range(8)]
        w_in, x_in = sem("A_w_in", 0), [sem(f"A_x_in{u}", 0) for u in range(2)]
        x_used, banks_used = sem("A_x_used"), sem("A_banks_used")
        stored = [sem(f"A_stored{u}") for u in range(2)]
        fence = sem("A_fence")
        mm_done, hi_done, lo_done, ones_set = sem("A_mm"), sem("A_hi"), sem("A_lo"), sem("A_ones")
        sem.start()
        block = ctx.enter_context(nc.Block())
        xT_v = xT.rearrange("(kc p) t -> p kc t", p=P)

        @block.gpsimd
        def _(pool):
            for w, src in ((wq, wqT), (wk, wkT), (wv, wvT)):
                pool.dma_start(w[:], src.rearrange("(kc p) n -> p kc n", p=P)).then_inc(w_in, 16)
            with pool.Fori(0, TOK // CH // 2) as pair:
                for u in range(2):
                    wait_apart(pool, x_used, pair * 2 + u + 1, fence)
                    pool.dma_start(x[:, u], xT_v[:, :, ds(pair * (2 * CH) + u * CH, CH)]).then_inc(x_in[u], 16)

        @block.tensor
        def _(pe):
            pe.sem_inc(x_used, 2)
            pe.wait_ge(w_in, 48)
            with pe.Fori(0, TOK // CH // 2) as pair:
                for u in range(2):
                    n = pair * 2 + u
                    pe.wait_ge(x_in[u], pair * 16 + 16)
                    pe.wait_ge(banks_used, n + 2)
                    for m in range(KC):
                        for c in range(KC):
                            pe.matmul(bank[4 * u + m][:], wq[:, c, m * P:(m + 1) * P], x[:, u, c],
                                      start=c == 0, stop=c == KC - 1)
                    for c in range(KC):
                        pe.matmul(bank[4 * u + 2][0:NKD], wk[:, c], x[:, u, c], start=c == 0, stop=c == KC - 1)
                    for s in range(SUB):
                        for c in range(KC):
                            last = pe.matmul(bank[4 * u + 3][:, s * NKD:(s + 1) * NKD], x[:, u, c, s * P:(s + 1) * P],
                                             wv[:, c], start=c == 0, stop=c == KC - 1)
                    last.then_inc(mm_done, 1)
                    pe.drain().then_inc(x_used, 1)

        @block.scalar
        def _(act):
            act.wait_ge(ones_set, 2)
            with act.Fori(0, TOK // CH // 2) as pair:
                for u in range(2):
                    n = pair * 2 + u
                    act.wait_ge(mm_done, n + 2)
                    act.wait_ge(stored[u], pair * (16 * STORES) + 1)
                    for s in range(SUB):
                        act.activation(v[:, u, s, :, 0:HD],
                                       bank[4 * u + 3][:, s * NKD:(s + 1) * NKD].rearrange("p (g e) -> p g e", e=HD),
                                       ACT.Copy)
                    act.activation(khi[:, u], bank[4 * u + 2][0:NKD], ACT.Copy)
                    for m in range(KC):
                        last = act.activation(qhi[:, u, m], bank[4 * u + m][:], ACT.Copy)
                    last.then_inc(hi_done, 1)

        @block.vector
        def _(dve):
            dve.sem_inc(banks_used, 2)
            dve.memset(v[:], 1.0).then_inc(ones_set, 1)
            with dve.Fori(0, TOK // CH // 2) as pair:
                for u in range(2):
                    n = pair * 2 + u
                    dve.wait_ge(hi_done, n + 2)
                    dve.tensor_tensor(klo[:, u], bank[4 * u + 2][0:NKD], khi[:, u].bitcast(F32), ALU.subtract)
                    for m in range(KC):
                        last = dve.tensor_tensor(qlo[:, u, m], bank[4 * u + m][:], qhi[:, u, m].bitcast(F32),
                                                 ALU.subtract)
                    last.then_inc(lo_done, 1)
                    dve.drain().then_inc(banks_used, 1)

        @block.sync
        def _(sp):
            with sp.Fori(0, B) as b:
                with sp.Fori(0, CPB // 2) as pair:
                    for u in range(2):
                        n = b * CPB + pair * 2 + u
                        col = pair * (2 * CH) + u * CH
                        sp.wait_ge(lo_done, n + 2)
                        for m in range(KC):
                            for dst, src in ((qh, qhi), (ql, qlo)):
                                sp.dma_start(dst[ds(b * D + m * P, P), ds(col, CH)], src[:, u, m].bitcast(F32)).then_inc(stored[u], 16)
                        for dst, src in ((kh, khi), (kl, klo)):
                            sp.dma_start(dst[ds(b * NKD, NKD), ds(col, CH)], src[:, u].bitcast(F32)).then_inc(stored[u], 16)
                        vs_v = vs.rearrange("(bb g t) e -> bb t g e", bb=B, g=NG)
                        for s in range(SUB):
                            sp.dma_start(vs_v[ds(b, 1), ds(col + s * P, P)].rearrange("o t g e -> (o t) g e"),
                                         v[:, u, s]).then_inc(stored[u], 16)
            for u in range(2):
                sp.wait_ge(stored[u], 16 * STORES * (TOK // CH // 2) + 1)


def attention(nc, sem, tag, nk, qh, ql, kh, kl, vs, mask_qk, mask_kq, ident_bf, ident, m_rows, ot):
    R = 4 * HD
    MR = 96
    NQ = S // P
    SC = 1.0 / HD ** 0.5

    pieces = []
    for qb in range(NQ):
        full, rest = divmod((qb + 1) * P, CH)
        for kc in range(full):
            pieces += [(qb, kc, CH, [h]) for h in range(GRP)]
        if rest:
            per = CH // rest
            pieces += [(qb, full, rest, list(range(h, h + per))) for h in range(0, GRP, per)]
    NP = len(pieces)
    steps = [(qc, kb) for qc in range(NQ * P // CH) for kb in range(SUB * (qc + 1))]
    NS = len(steps)
    cut = [NP * i // NS for i in range(NS + 1)]

    with ExitStack() as ctx:
        sb = lambda n, s, t: ctx.enter_context(nc.sbuf_tensor(tag + n, s, t))
        qs = [sb(f"qs{i}", [P, GRP, S], F32R) for i in range(2)]
        ks = [sb(f"ks{i}", [P, nk, S], F32R) for i in range(2)]
        v = [sb(f"v{i}", [P, NQ, nk, VW], F32) for i in range(2)]
        p = sb("p", [P, 2, GRP, CH], F32)
        o = sb("o", [P, 2, CH], F32)
        mpart = sb("mpart", [P, GRP, NQ, 4], F32)
        m = sb("m", [P, P], F32)
        mhi = sb("mhi", [GRP * NQ, P], F32R)
        mlo = sb("mlo", [GRP * NQ, P], F32R)
        mqk = sb("mqk", [P, P], BF16)
        mkq = sb("mkq", [P, P], BF16)
        idb = sb("idb", [P, P], BF16)
        idf = sb("idf", [P, P], F32)
        psc = ctx.enter_context(nc.psum_tensor(tag + "psc", [P, GRP, CH], F32))
        po = [ctx.enter_context(nc.psum_tensor(f"{tag}po{i}", [P, CH], F32)) for i in range(2)]
        pm = [ctx.enter_context(nc.psum_tensor(f"{tag}pm{i}", [P, CH], F32)) for i in range(2)]
        c_in, ready = sem(tag + "c_in", 0), sem(tag + "ready")
        q_in, ld_free = [sem(f"{tag}q_in{i}", 0) for i in range(2)], sem(tag + "ld_free")
        s_max, max_done = sem(tag + "s_max"), sem(tag + "max_done")
        m_all, mt_done = sem(tag + "m_all"), sem(tag + "mt_done")
        mh_done, ml_done = sem(tag + "mh_done"), sem(tag + "ml_done")
        m_out, m_in, fence = sem(tag + "m_out"), sem(tag + "m_in"), sem(tag + "fence")
        s_done, pv_done = sem(tag + "s_done"), sem(tag + "pv_done")
        e_done = [sem(f"{tag}e_done{i}") for i in range(2)]
        o_done, o_out = sem(tag + "o_done"), [sem(f"{tag}o_out{i}") for i in range(2)]
        sem.start()
        block = ctx.enter_context(nc.Block())

        LOADS = 8 + 1
        NC4 = S // CH

        @block.gpsimd
        def _(pool):
            for dst, src in ((mqk, mask_qk), (mkq, mask_kq), (idb, ident_bf)):
                pool.dma_start(dst[:], src).then_inc(c_in, 16)
            pool.dma_start(idf[:], ident).then_inc(c_in, 16)

            def load(i, s):
                for r, (a, c) in enumerate(((qh, kh), (qh, kl), (ql, kh), (ql, kl))):
                    pool.dma_start(qs[s][r * HD:(r + 1) * HD, :, :].bitcast(F32),
                                   a[ds(i * (GRP * HD), GRP * HD), :].rearrange("(h e) t -> e h t", e=HD)
                                   ).then_inc(q_in[s], 16)
                    pool.dma_start(ks[s][r * HD:(r + 1) * HD, :, :].bitcast(F32),
                                   c[ds(i * (nk * HD), nk * HD), :].rearrange("(h e) t -> e h t", e=HD)
                                   ).then_inc(q_in[s], 16)
                pool.dma_start(v[s][:], vs[ds(i * S, S), :].rearrange("(kb p) (h e) -> p kb h e", p=P, e=VW)
                               ).then_inc(q_in[s], 16)

            load(0, 0)
            load(1, 1)
            with pool.Fori(0, NIT // 2 - 1) as pair:
                for s in range(2):
                    wait_apart(pool, ld_free, pair * 2 + s + 1, fence)
                    load(pair * 2 + s + 2, s)

        @block.sync
        def _(sp):
            def m_step(i, s):
                sp.wait_ge(ml_done, i + 2)
                sp.dma_start(m_rows[0:1].rearrange("o (a t) -> (o a) t", t=P), mhi[:].bitcast(F32)).then_inc(m_out, 16)
                sp.dma_start(m_rows[1:2].rearrange("o (a t) -> (o a) t", t=P), mlo[:].bitcast(F32)).then_inc(m_out, 16)
                sp.wait_ge(m_out, (i + 1) * 32 + 1)
                sp.dma_start(qs[s][MR:MR + 2, :, :].bitcast(F32).rearrange("r h t -> r (h t)"), m_rows).then_inc(m_in, 16)

            def outs(i):
                for c in range(NC4):
                    sp.wait_ge(o_done, i * NC4 + c + 3)
                    sp.dma_start(ot[ds(i * P, P), c * CH:(c + 1) * CH], o[:, c % 2]).then_inc(o_out[c % 2], 16)

            m_step(0, 0)
            with sp.Fori(0, NIT // 2 - 1) as pair:
                for s in range(2):
                    outs(pair * 2 + s)
                    m_step(pair * 2 + s + 1, (s + 1) % 2)
            outs(NIT - 2)
            m_step(NIT - 1, 1)
            outs(NIT - 1)
            for c in range(2):
                sp.wait_ge(o_out[c], 16 * (NC4 // 2 * NIT) + 1)

        @block.tensor
        def _(pe):
            def maxima(i, s, a, z):
                for j in range(a, z):
                    qb, kc, w, heads = pieces[j]
                    t = pm[j % 2]
                    pe.wait_ge(max_done, i * NP + j + 2)
                    diag = kc * CH + w == (qb + 1) * P
                    for n, h in enumerate(heads):
                        last = pe.matmul(t[:, n * w:(n + 1) * w], qs[s][0:MR, h, qb * P:(qb + 1) * P],
                                         ks[s][0:MR, h % nk, kc * CH:kc * CH + w], start=True, stop=True)
                        if diag:
                            last = pe.matmul(t[:, (n + 1) * w - P:(n + 1) * w], idb[:], mqk[:], start=False,
                                             stop=True, skip_group_check=True)
                    last.then_inc(s_max, 1)

            def turn(i):
                pe.wait_ge(m_all, i + 2)
                pe.transpose(pm[0][:, 0:P], m[:], idf[:]).then_inc(mt_done, 1)

            def weigh(i, s, t):
                qc, kb = steps[t]
                off = max(0, kb - SUB * qc) * P
                for pr in range(2):
                    pe.wait_ge(e_done[pr], i * NS + t + 2)
                if kb == 0:
                    pe.wait_ge(o_done, i * NC4 + qc + 1)
                for h in range(GRP):
                    last = pe.matmul(po[qc % 2][VW * h:VW * (h + 1), off:CH], v[s][:, kb, h % nk],
                                     p[:, t % 2, h, off:CH], start=kb == 0, stop=kb == SUB * (qc + 1) - 1,
                                     skip_group_check=True)
                last.then_inc(pv_done, 1)

            def step(i, s, nxt):
                pe.wait_ge(m_in, (i + 1) * 16 + 1)
                for t, (qc, kb) in enumerate(steps):
                    diag = kb - SUB * qc
                    off = max(0, diag) * P
                    a, z = (cut[t], cut[t + 1]) if nxt else (0, 0)
                    spread = [a, min(a + 1, z), min(a + 2, z), z]
                    for pr in range(2):
                        pe.wait_ge(e_done[pr], i * NS + t + 1)
                        for h in (2 * pr, 2 * pr + 1):
                            last = pe.matmul(psc[:, h, off:CH], ks[s][:, h % nk, kb * P:(kb + 1) * P],
                                             qs[s][:, h, qc * CH + off:(qc + 1) * CH],
                                             start=True, stop=True)
                            if diag >= 0:
                                last = pe.matmul(psc[:, h, off:off + P], idb[:], mkq[:], start=False, stop=True,
                                                 skip_group_check=True)
                        last.then_inc(s_done, 1)
                        maxima(i + 1, 1 - s, spread[pr], spread[pr + 1])
                    if t:
                        weigh(i, s, t - 1)
                    maxima(i + 1, 1 - s, spread[2], spread[3])
                weigh(i, s, NS - 1)
                pe.drain().then_inc(ld_free, 1)
                if nxt:
                    turn(i + 1)

            pe.wait_ge(c_in, 64)
            pe.wait_ge(ready, 2)
            pe.wait_ge(q_in[0], 16 * LOADS)
            maxima(0, 0, 0, NP)
            turn(0)
            with pe.Fori(0, NIT // 2 - 1) as pair:
                for s in range(2):
                    pe.wait_ge(q_in[1 - s], (pair + s + 1) * (16 * LOADS))
                    step(pair * 2 + s, s, True)
            pe.wait_ge(q_in[1], NIT // 2 * 16 * LOADS)
            step(NIT - 2, 0, True)
            step(NIT - 1, 1, False)

        @block.scalar
        def _(act):
            def m_hi(i):
                act.wait_ge(mt_done, i + 2)
                act.wait_ge(m_in, i * 16 + 1)
                act.activation(mhi[:], pm[0][0:GRP * NQ, 0:P], ACT.Copy, scale=-1.0).then_inc(mh_done, 1)

            def step(i):
                for t, (qc, kb) in enumerate(steps):
                    off = max(0, kb - SUB * qc) * P
                    for pr in range(2):
                        act.wait_ge(s_done, (i * NS + t) * 2 + pr + 2)
                        act.wait_ge(pv_done, i * NS + t + 2)
                        act.activation(p[:, t % 2, 2 * pr:2 * pr + 2, off:CH], psc[:, 2 * pr:2 * pr + 2, off:CH],
                                       ACT.Exp, scale=SC).then_inc(e_done[pr], 1)

            m_hi(0)
            with act.Fori(0, NIT // 2 - 1) as pair:
                for s in range(2):
                    step(pair * 2 + s)
                    m_hi(pair * 2 + s + 1)
            step(NIT - 2)
            m_hi(NIT - 1)
            step(NIT - 1)

        @block.vector
        def _(dve):
            def maxima(i, a, z):
                for j in range(a, z):
                    qb, kc, w, heads = pieces[j]
                    dve.wait_ge(s_max, i * NP + j + 2)
                    dve.tensor_reduce(mpart[:, heads[0]:heads[-1] + 1, qb, kc],
                                      pm[j % 2][:, 0:len(heads) * w].rearrange("p (h k) -> p h k", k=w),
                                      AX, ALU.max).then_inc(max_done, 1)

            def fold(i):
                dve.wait_ge(max_done, (i + 1) * NP + 3)
                dve.wait_ge(mt_done, i + 1)
                dve.tensor_reduce(m[:, 0:GRP * NQ], mpart[:].rearrange("p h q k -> p (h q) k"), AX, ALU.max).then_inc(m_all, 1)

            def m_lo(i):
                dve.wait_ge(mh_done, i + 2)
                dve.scalar_tensor_tensor(mlo[:], pm[0][0:GRP * NQ, 0:P], -1.0, mhi[:].bitcast(F32),
                                         ALU.mult, ALU.subtract).then_inc(ml_done, 1)

            def copy_out(i, qc):
                dve.wait_ge(pv_done, i * NS + 2 + sum(SUB * (c + 1) for c in range(qc + 1)) + 1)
                dve.wait_ge(o_out[qc % 2], i * (NC4 // 2 * 16) + qc // 2 * 16 + 1)
                dve.tensor_copy(o[:, qc % 2], po[qc % 2][:]).then_inc(o_done, 1)

            def step(i, nxt):
                for t, (qc, kb) in enumerate(steps):
                    if nxt:
                        maxima(i + 1, cut[t], cut[t + 1])
                    if kb == 0 and qc:
                        copy_out(i, qc - 1)
                copy_out(i, NC4 - 1)
                if nxt:
                    fold(i + 1)
                    m_lo(i + 1)

            dve.sem_inc(max_done, 2)
            dve.sem_inc(o_done, 1)
            dve.sem_inc(pv_done, 2)
            dve.memset(mpart[:], -3e38)
            dve.memset(m[:], 0.0)
            for s in range(2):
                dve.memset(qs[s][R:P].bitcast(F32), 0.0)
                last = dve.memset(ks[s][R:P].bitcast(F32), 1.0)
            last.then_inc(ready, 1)
            maxima(0, 0, NP)
            fold(0)
            m_lo(0)
            with dve.Fori(0, NIT // 2 - 1) as pair:
                for s in range(2):
                    step(pair * 2 + s, True)
            step(NIT - 2, True)
            step(NIT - 1, False)


E_, HID_E = 8, 1024
TOPK = 2
CAP = int(1.2 * TOPK * S // E_)
ROWS = B * CAP


class Chain:

    def __init__(self, eng, semaphore, per):
        self.eng, self.sem, self.per, self.n, self.base = eng, semaphore, per, 0, 0

    def start(self, i):
        self.base, self.n = i * self.per, 0

    def link(self, ins):
        self.n += 1
        ins.then_inc(self.sem, 1)
        self.eng.wait_ge(self.sem, self.base + self.n + 1)

    def end(self):
        assert self.n == self.per, self.n


def attention_output(nc, sem, tag, ot, woT, x_src, X, ident, router, xp, inverse):
    with ExitStack() as ctx:
        sb = lambda n, s, t: ctx.enter_context(nc.sbuf_tensor(tag + n, s, t))
        num = sb("num", [P, 2, KC, CH], F32)
        den = sb("den", [P, 2, KC, CH], F32)
        sums = sb("sums", [P, CH], F32)
        inv = sb("inv", [P, CH], F32)
        cx = sb("cx", [P, 2, KC, CH], F32)
        wo = sb("wo", [P, KC, D], F32)
        y = sb("y", [P, SUB, D], F32)
        xn = sb("xn", [P, SUB, D], F32)
        xnT = sb("xnT", [P, KC, CH], F32)
        st = sb("st", [P, SUB, 6], F32)
        mv = sb("mv", [P, SUB, 2], F32)
        sd = sb("sd", [P, SUB], F32)
        rs = sb("rs", [P, SUB], F32)
        eps = sb("eps", [P, 1], F32)
        idf = sb("idf", [P, P], F32)
        rw = sb("rw", [P, KC, E_], F32)
        rb = sb("rb", [P, E_], F32)
        pb = [ctx.enter_context(nc.psum_tensor(f"{tag}pb{i}", [P, CH], F32)) for i in range(5)]
        w_in, a_in = sem(tag + "w_in", 0), [sem(f"{tag}a_in{u}", 0) for u in range(2)]
        c_ready, mm_done = sem(tag + "c_ready"), sem(tag + "mm_done")
        var_done, sd_done, n_done = sem(tag + "var"), sem(tag + "sd"), sem(tag + "n_done")
        t_done, xt_done, lg_done, lg_out = sem(tag + "t"), sem(tag + "xt"), sem(tag + "lg"), sem(tag + "lgo")
        x_copied, st_done, dch, fence = sem(tag + "xc"), sem(tag + "st"), sem(tag + "dch"), sem(tag + "fence")
        eps_set, sums_in, inv_done, inv_out = sem(tag + "eps"), sem(tag + "si", 0), sem(tag + "id"), sem(tag + "io")
        sem.start()
        block = ctx.enter_context(nc.Block())
        wcount = 2 + (2 if router else 0) + (1 if x_src is not None else 0)

        def chunks(eng, body):
            with eng.Fori(0, B) as b:
                with eng.Fori(0, CPB // 2) as pair:
                    for u in range(2):
                        body(b * CPB + pair * 2 + u, b, pair, u)

        @block.gpsimd
        def _(pool):
            pool.dma_start(wo[:], woT.rearrange("(kc p) n -> p kc n", p=P)).then_inc(w_in, 16)
            pool.dma_start(idf[:], ident).then_inc(w_in, 16)
            pool.memset(eps[:], EPS).then_inc(eps_set, 1)
            if router:
                pool.dma_start(rw[:], router[0].rearrange("(kc p) n -> p kc n", p=P)).then_inc(w_in, 16)
                pool.dma_start(rb[:], router[1]).then_inc(w_in, 16)
            if x_src is not None:
                pool.dma_start(X[:], x_src.rearrange("(t p) c -> p t c", p=P)).then_inc(w_in, 16)

            def body(n, b, pair, u):
                wait_apart(pool, a_in[u], b * (CPB // 2 * 64) + pair * 64 + 63, fence)
                wait_apart(pool, mm_done, n, fence)
                pool.tensor_tensor(cx[:, u], num[:, u], den[:, u], ALU.mult).then_inc(c_ready, 1)
            chunks(pool, body)

        @block.tensor
        def _(pe):
            pe.wait_ge(w_in, wcount * 16)

            def body(n, b, pair, u):
                pe.wait_ge(c_ready, n + 2)
                pe.wait_ge(var_done, n + 1)
                for s in range(SUB):
                    for c in range(KC):
                        last = pe.matmul(pb[s // 2][:, s % 2 * D:(s % 2 + 1) * D], cx[:, u, c, s * P:(s + 1) * P],
                                         wo[:, c], start=c == 0, stop=c == KC - 1)
                last.then_inc(mm_done, 1)
                if router:
                    pe.wait_ge(n_done, n + 2)
                    for c in range(KC):
                        for s in range(SUB):
                            last = pe.transpose(pb[2 + c][:, s * P:(s + 1) * P], xn[:, s, c * P:(c + 1) * P], idf[:])
                    last.then_inc(t_done, 1)
                    pe.wait_ge(xt_done, n + 2)
                    for s in range(SUB):
                        for c in range(KC):
                            last = pe.matmul(pb[4][:, s * E_:(s + 1) * E_], xnT[:, c, s * P:(s + 1) * P], rw[:, c],
                                             start=c == 0, stop=c == KC - 1)
                    last.then_inc(lg_done, 1)
            chunks(pe, body)

        @block.scalar
        def _(act):
            act.wait_ge(eps_set, 2)

            def body(n, b, pair, u):
                act.wait_ge(var_done, n + 2)
                act.activation(sd[:], mv[:, :, 1], ACT.Sqrt, bias=eps[:]).then_inc(sd_done, 1)
                act.wait_ge(n_done, n + 2)
                if xp is not None:
                    for s in range(SUB):
                        act.dma_start(xp[ds(b * (S + 1) + pair * (2 * CH) + u * CH + s * P + 1, P), :], xn[:, s]
                                      ).then_inc(st_done, 16)
                act.activation(X[:, ds(n * SUB, SUB), :], xn[:], ACT.Copy).then_inc(x_copied, 1)
                if router:
                    act.wait_ge(t_done, n + 2)
                    for c in range(KC):
                        last = act.activation(xnT[:, c], pb[2 + c][:], ACT.Copy)
                    last.then_inc(xt_done, 1)
            chunks(act, body)

        @block.vector
        def _(dve):
            ch = Chain(dve, dch, 4 + SUB - 1 + (1 if router else 0))
            dve.wait_ge(sums_in, 16)
            dve.reciprocal(inv[:], sums[:]).then_inc(inv_done, 1)
            dve.wait_ge(w_in, wcount * 16)
            def body(n, b, pair, u):
                ch.start(n)
                dve.wait_ge(mm_done, n + 2)
                for k in range(2):
                    last = dve.tensor_tensor(y[:, 2 * k:2 * k + 2], pb[k][:].rearrange("p (s c) -> p s c", c=D),
                                             X[:, ds(n * SUB + 2 * k, 2), :], ALU.add)
                    ch.link(last)
                for s in range(SUB):
                    last = dve.bn_stats(st[:, s], y[:, s])
                ch.link(last)
                dve.sem_inc(fence, 1)
                for s in range(SUB):
                    last = dve.bn_aggr(mv[:, s], st[:, s])
                last.then_inc(var_done, 1)
                dve.wait_ge(sd_done, n + 2)
                ch.link(dve.reciprocal(rs[:], sd[:]))
                dve.wait_ge(x_copied, n + 1)
                if router:
                    dve.wait_ge(t_done, n + 1)
                if xp is not None:
                    dve.wait_ge(st_done, n * (16 * SUB) + 1)
                for s in range(SUB):
                    last = dve.tensor_scalar(xn[:, s], y[:, s], mv[:, s, 0:1], rs[:, s:s + 1], ALU.subtract, ALU.mult)
                    if s == SUB - 1:
                        last.then_inc(n_done, 1)
                    else:
                        ch.link(last)
                if router:
                    dve.wait_ge(lg_done, n + 2)
                    ch.link(dve.tensor_tensor(router[2][:, ds(n * SUB, SUB), :],
                                              pb[4][:, 0:SUB * E_].rearrange("p (s e) -> p s e", e=E_),
                                              rb[:].unsqueeze(1).to_broadcast([P, SUB, E_]), ALU.add))
                ch.end()
            chunks(dve, body)
            dve.wait_ge(x_copied, TOK // CH + 1)

        @block.sync
        def _(sp):
            def body(n, b, pair, u):
                sp.wait_ge(c_ready, n)
                for m in range(KC):
                    cols = ds(pair * (2 * CH) + u * CH, CH)
                    o = ot[ds(b * (NH * VW) + m * (NH * VW // KC), NH * VW // KC), cols].rearrange(
                        "(h r) t -> h r t", r=VW)
                    sp.dma_start(num[:, u, m], o[:, 0:HD]).then_inc(a_in[u], 16)
                    sp.dma_start(den[:, u, m], inverse[ds(b * NH + m * (NH // KC), NH // KC), cols].unsqueeze(1)
                                 .to_broadcast([NH // KC, HD, CH])).then_inc(a_in[u], 16)

            heads = ot.rearrange("(g r) t -> g r t", r=VW)[:, HD]
            sp.dma_start(sums[:], heads.rearrange("g (q t) -> g q t", t=CH)).then_inc(sums_in, 16)
            sp.wait_ge(inv_done, 2)
            sp.dma_start(inverse.rearrange("g (q t) -> g q t", t=CH), inv[:]).then_inc(inv_out, 16)
            sp.wait_ge(inv_out, 17)
            chunks(sp, body)
            if xp is not None:
                sp.wait_ge(st_done, 16 * SUB * (TOK // CH) + 1)


def route(nc, sem, LG, tri, iota8, ones, slot_s, slot_g, prob):
    NK = TOPK
    QT = S // P
    SEQ = NK * QT
    with ExitStack() as ctx:
        sb = lambda n, s, t: ctx.enter_context(nc.sbuf_tensor("D_" + n, s, t))
        m8 = sb("m8", [P, NT, 8], F32)
        i8 = sb("i8", [P, NT, 8], U32)
        ixf = sb("ixf", [P, NK, NT], F32)
        oh = sb("oh", [P, B, NK, QT, E_], F32)
        trs = sb("trs", [P, P], F32)
        on = sb("on", [P, P], F32)
        io = sb("io", [P, E_], F32)
        ca = sb("ca", [P, B, SEQ, E_], F32)
        cb = sb("cb", [P, B, SEQ, E_], F32)
        pos = sb("pos", [P, B, SEQ, E_], F32)
        pf = sb("pf", [P, B, NK, QT], F32)
        base = sb("base", [P, B, NK, QT], F32)
        of = sb("of", [P, B, NK, QT], F32)
        g = sb("g", [P, B, NK, QT], F32)
        dif = sb("dif", [P, NT], F32)
        e2 = sb("e2", [P, NT], F32)
        den = sb("den", [P, NT], F32)
        pc = ctx.enter_context(nc.psum_tensor("D_pc", [P, CH], F32))
        pt = ctx.enter_context(nc.psum_tensor("D_pt", [P, CH], F32))
        c_in, dch, oh_done, cum_done = sem("D_c_in", 0), sem("D_dch"), sem("D_oh"), sem("D_cum")
        dif_done, e2_done = sem("D_dif"), sem("D_e2")
        sem.start()
        block = ctx.enter_context(nc.Block())

        @block.sync
        def _(sp):
            for dst, src in ((trs, tri), (on, ones), (io, iota8)):
                sp.dma_start(dst[:], src).then_inc(c_in, 16)

        @block.tensor
        def _(pe):
            pe.wait_ge(c_in, 48)
            pe.wait_ge(oh_done, 2)
            flat = oh[:].rearrange("p b k t e -> p (b k t e)")
            pe.matmul(pc[:], trs[:], flat, start=True, stop=True)
            pe.matmul(pt[:], on[:], flat, start=True, stop=True).then_inc(cum_done, 1)

        @block.scalar
        def _(act):
            act.wait_ge(dif_done, 2)
            act.activation(e2[:], dif[:], ACT.Exp).then_inc(e2_done, 1)

        @block.vector
        def _(dve):
            n = [0]

            def link(ins):
                n[0] += 1
                ins.then_inc(dch, 1)
                dve.wait_ge(dch, n[0] + 1)

            dve.wait_ge(c_in, 48)
            for t in range(NT):
                last = dve.max(m8[:, t], LG[:, t])
            link(last)
            for t in range(NT):
                last = dve.max_index(i8[:, t], m8[:, t], LG[:, t])
            link(last)
            dve.tensor_tensor(dif[:], m8[:, :, 1], m8[:, :, 0], ALU.subtract).then_inc(dif_done, 1)
            for k in range(NK):
                last = dve.tensor_copy(ixf[:, k], i8[:, :, k])
            link(last)
            for b in range(B):
                for k in range(NK):
                    last = dve.tensor_tensor(
                        oh[:, b, k], io[:].unsqueeze(1).to_broadcast([P, QT, E_]),
                        ixf[:, k, b * QT:(b + 1) * QT].unsqueeze(2).to_broadcast([P, QT, E_]), ALU.is_equal)
            last.then_inc(oh_done, 1)
            dve.wait_ge(cum_done, 2)
            tot = pt[:].rearrange("p (b s e) -> p b s e", b=B, e=E_)
            link(dve.memset(ca[:, :, 0:1], 0.0))
            link(dve.tensor_copy(ca[:, :, 1:SEQ], tot[:, :, 0:SEQ - 1]))
            a, c, step = ca, cb, 1
            while step < SEQ:
                dve.tensor_copy(c[:, :, 0:step], a[:, :, 0:step])
                link(dve.tensor_tensor(c[:, :, step:SEQ], a[:, :, step:SEQ], a[:, :, 0:SEQ - step], ALU.add))
                a, c, step = c, a, step * 2
            link(dve.tensor_tensor(pos[:], pc[:].rearrange("p (b s e) -> p b s e", b=B, e=E_), a[:], ALU.add))
            link(dve.tensor_tensor(c[:], pos[:], oh[:].rearrange("p b k t e -> p b (k t) e"), ALU.mult))
            link(dve.tensor_reduce(pf[:].rearrange("p b k t -> p b (k t)"), c[:], AX, ALU.add))
            for b in range(B):
                for k in range(NK):
                    last = dve.tensor_scalar(base[:, b, k], ixf[:, k, b * QT:(b + 1) * QT], float(ROWS),
                                             float(b * CAP - 1), ALU.mult, ALU.add)
            link(last)
            link(dve.tensor_scalar(of[:], pf[:], float(CAP), float(E_ * ROWS), ALU.is_gt, ALU.mult))
            link(dve.tensor_scalar(g[:], pf[:], float(CAP), None, ALU.min))
            link(dve.tensor_tensor(of[:], of[:], pf[:], ALU.add))
            dve.tensor_tensor(slot_s[:], of[:], base[:], ALU.add)
            dve.tensor_tensor(slot_g[:], g[:], base[:], ALU.add)
            dve.wait_ge(e2_done, 2)
            link(dve.tensor_scalar(den[:], e2[:], 1.0, None, ALU.add))
            link(dve.reciprocal(prob[:, 0], den[:]))
            link(dve.tensor_tensor(prob[:, 1], e2[:], prob[:, 0], ALU.mult))


HT = HID_E // P
XT = -(-ROWS // P)
LAST = ROWS - (XT - 1) * P


def experts(nc, sem, X, slot_s, ein, eout, wfc, bfc, wgate, bgate, wproj, bproj, ident):
    chunks = [(t, min(SUB, XT - t)) for t in range(0, XT, SUB)]
    NCH = len(chunks)
    assert NCH * 2 % 2 == 0

    def width(t, k):
        return min(ROWS, (t + k) * P) - t * P

    with ExitStack() as ctx:
        sb = lambda n, s, t: ctx.enter_context(nc.sbuf_tensor("E_" + n, s, t))
        wf = sb("wf", [P, 2, KC, HID_E], F32)
        wg = sb("wg", [P, 2, KC, HID_E], F32)
        wp = sb("wp", [P, 2, HT, D], F32)
        bf = sb("bf", [P, 2, HT], F32)
        bg = sb("bg", [P, 2, HT], F32)
        bp = sb("bp", [P, 2, D], F32)
        xin = sb("xin", [P, 2, XT, D], F32)
        xT = sb("xT", [P, 2, KC, CH], F32)
        hs = sb("hs", [P, 2, CH], F32)
        z = sb("z", [P, 2, CH], F32)
        a = sb("a", [P, HT, CH], F32)
        ob = sb("ob", [P, SUB, D], F32)
        idf = sb("idf", [P, P], F32)
        pT = [ctx.enter_context(nc.psum_tensor(f"E_pT{i}", [P, CH], F32)) for i in range(2)]
        pH = [ctx.enter_context(nc.psum_tensor(f"E_pH{i}", [P, CH], F32)) for i in range(2)]
        pG = [ctx.enter_context(nc.psum_tensor(f"E_pG{i}", [P, CH], F32)) for i in range(2)]
        pO = [ctx.enter_context(nc.psum_tensor(f"E_pO{i}", [P, CH], F32)) for i in range(2)]
        c_in, sent, e_in, e_used = sem("E_c_in", 0), sem("E_sent", 0), [sem(f"E_in{i}", 0) for i in range(2)], sem("E_used")
        t_done, xt_done, hg_done, hs_done = sem("E_t"), sem("E_xt"), sem("E_hg"), sem("E_hs")
        fence = sem("E_fence")
        z_done, a_done, o_mm, o_done, o_out = sem("E_z"), sem("E_a"), sem("E_omm"), sem("E_od"), sem("E_out")
        sem.start()
        block = ctx.enter_context(nc.Block())
        LOADS = 8

        @block.gpsimd
        def _(pool):
            for b in range(B):
                for k in range(TOPK):
                    for q in range(S // P):
                        pool.indirect_dma_start(ein, bass.IndirectOffsetOnAxis(slot_s[:, b, k, q:q + 1], 0),
                                                X[:, b * (S // P) + q], None, bounds_check=E_ * ROWS - 1,
                                                oob_is_err=False).then_inc(sent, 16)
            pool.wait_ge(sent, 16 * B * TOPK * (S // P))

            def load(e, s):
                rows = e * ROWS
                pool.dma_start(xin[:, s, 0:XT - 1], ein[ds(rows, (XT - 1) * P), :].rearrange("(t p) c -> p t c", p=P)
                               ).then_inc(e_in[s], 16)
                pool.dma_start(xin[0:LAST, s, XT - 1], ein[ds(rows + (XT - 1) * P, LAST), :]).then_inc(e_in[s], 16)
                for w, src, kc in ((wf, wfc, KC), (wg, wgate, KC), (wp, wproj, HT)):
                    pool.dma_start(w[:, s], src[ds(e * kc * P, kc * P), :].rearrange("(k p) n -> p k n", p=P)
                                   ).then_inc(e_in[s], 16)
                pool.dma_start(bf[:, s], bfc[ds(e * P, P), :]).then_inc(e_in[s], 16)
                pool.dma_start(bg[:, s], bgate[ds(e * P, P), :]).then_inc(e_in[s], 16)
                pool.dma_start(bp[:, s], bproj[ds(e, 1), :].to_broadcast([P, D])).then_inc(e_in[s], 16)

            with pool.Fori(0, E_ // 2) as pair:
                for s in range(2):
                    wait_apart(pool, e_used, pair * 2 + s + 1, fence)
                    load(pair * 2 + s, s)

        def every(eng, body):
            with eng.Fori(0, E_ // 2) as pair:
                for s in range(2):
                    e = pair * 2 + s
                    for c, (t, k) in enumerate(chunks):
                        body(pair, e, s, c, t, k, width(t, k), e * NCH + c, (s * NCH + c) % 2)

        @block.tensor
        def _(pe):
            pe.sem_inc(e_used, 2)
            pe.wait_ge(c_in, 16)

            def body(pair, e, s, c, t, k, w, q, par):
                if c == 0:
                    pe.wait_ge(e_in[s], (pair + 1) * (16 * LOADS))
                pe.wait_ge(xt_done, q + 1)
                for h in range(KC):
                    for j in range(k):
                        r = min(P, ROWS - (t + j) * P)
                        last = pe.transpose(pT[h][:, j * P:j * P + r], xin[0:r, s, t + j, h * P:(h + 1) * P],
                                            idf[0:r, 0:r])
                last.then_inc(t_done, 1)
                pe.wait_ge(xt_done, q + 2)
                for ht in range(HT):
                    pe.wait_ge(z_done, q * HT + ht + 2)
                    for bank, wt in ((pH, wf), (pG, wg)):
                        for kc in range(KC):
                            last = pe.matmul(bank[ht % 2][:, 0:w], wt[:, s, kc, ht * P:(ht + 1) * P],
                                             xT[:, par, kc, 0:w], start=kc == 0, stop=kc == KC - 1)
                    last.then_inc(hg_done, 1)
                pe.wait_ge(a_done, (q + 1) * HT + 3)
                pe.wait_ge(o_done, q + 1)
                for j in range(k):
                    r = min(P, ROWS - (t + j) * P)
                    for ht in range(HT):
                        last = pe.matmul(pO[j // 2][0:r, j % 2 * D:(j % 2 + 1) * D], a[:, ht, j * P:j * P + r],
                                         wp[:, s, ht], start=ht == 0, stop=ht == HT - 1)
                last.then_inc(o_mm, 1)
                if c == NCH - 1:
                    pe.wait_ge(o_done, q + 2)
                    pe.sem_inc(e_used, 1)
            every(pe, body)

        @block.scalar
        def _(act):
            def silu(q, ht, w):
                act.wait_ge(z_done, q * HT + ht + 4)
                act.activation(a[:, ht, 0:w], z[:, ht % 2, 0:w], ACT.Silu).then_inc(a_done, 1)

            def body(pair, e, s, c, t, k, w, q, par):
                act.wait_ge(t_done, q + 2)
                for h in range(KC):
                    last = act.activation(xT[:, par, h, 0:w], pT[h][:, 0:w], ACT.Copy)
                last.then_inc(xt_done, 1)
                for ht in range(HT):
                    act.wait_ge(hg_done, q * HT + ht + 2)
                    act.activation(hs[:, ht % 2, 0:w], pH[ht % 2][:, 0:w], ACT.Identity, bias=bf[:, s, ht:ht + 1]
                                   ).then_inc(hs_done, 1)
                    if ht == 0:
                        act.wait_ge(o_mm, q + 1)
                    else:
                        silu(q, ht - 1, w)
                silu(q, HT - 1, w)
            every(act, body)

        @block.vector
        def _(dve):
            dve.sem_inc(z_done, 2)
            dve.sem_inc(a_done, 2)

            def body(pair, e, s, c, t, k, w, q, par):
                for ht in range(HT):
                    dve.wait_ge(hs_done, q * HT + ht + 2)
                    dve.wait_ge(a_done, q * HT + ht + 2)
                    dve.scalar_tensor_tensor(z[:, ht % 2, 0:w], pG[ht % 2][:, 0:w], bg[:, s, ht:ht + 1],
                                             hs[:, ht % 2, 0:w], ALU.add, ALU.mult).then_inc(z_done, 1)
                dve.wait_ge(o_mm, q + 2)
                dve.wait_ge(o_out, e * (16 * (NCH + 1)) + 16 * c + 1)
                for j in range(k):
                    r = min(P, ROWS - (t + j) * P)
                    last = dve.tensor_tensor(ob[0:r, j], pO[j // 2][0:r, j % 2 * D:(j % 2 + 1) * D], bp[0:r, s], ALU.add)
                last.then_inc(o_done, 1)
            every(dve, body)

        @block.sync
        def _(sp):
            sp.dma_start(idf[:], ident).then_inc(c_in, 16)

            def body(pair, e, s, c, t, k, w, q, par):
                sp.wait_ge(o_done, q + 2)
                rows = e * ROWS + t * P
                whole = k if w == k * P else k - 1
                sp.dma_start(eout[ds(rows, whole * P), :].rearrange("(t p) c -> p t c", p=P), ob[:, 0:whole]
                             ).then_inc(o_out, 16)
                if whole < k:
                    sp.dma_start(eout[ds(rows + whole * P, LAST), :], ob[0:LAST, whole]).then_inc(o_out, 16)
            every(sp, body)
            sp.wait_ge(o_out, 16 * (NCH + 1) * E_ + 1)


def combine_and_project(nc, sem, X, eout, slot_g, prob, cos, sin, wq, wqs, wdown, wk, wks, wv, ident,
                        qh, ql, kh, kl, vs):
    LAT = wdown.shape[1]
    QT = S // P
    RJ = 2 * KC
    PER = 1 + (SUB - 1) + 2 * RJ + 3
    STORES = 2 * RJ + SUB
    with ExitStack() as ctx:
        sb = lambda n, s, t: ctx.enter_context(nc.sbuf_tensor("F_" + n, s, t))
        Y = sb("Y", [P, NT, TOPK, D], F32)
        y = sb("y", [P, SUB, D], F32)
        xn = sb("xn", [P, SUB, D], F32)
        xnT = sb("xnT", [P, KC, CH], F32)
        lat = sb("lat", [LAT, CH], F32)
        st = sb("st", [P, SUB, 6], F32)
        mv = sb("mv", [P, SUB, 2], F32)
        sd = sb("sd", [P, SUB], F32)
        rs = sb("rs", [P, SUB], F32)
        eps = sb("eps", [P, 1], F32)
        idf = sb("idf", [P, P], F32)
        wt = {n: sb("w" + n, [P, KC, D], F32) for n in ("q", "qs")}
        wd = sb("wd", [P, KC, LAT], F32)
        wkt = {n: sb("w" + n, [LAT, D], F32) for n in ("k", "ks", "v")}
        co = sb("co", [P, S], F32)
        si = sb("si", [P, S], F32)
        t1 = sb("t1", [P, CH], F32)
        t2 = sb("t2", [P, CH], F32)
        r = sb("r", [P, 2, CH], F32)
        hi = sb("hi", [P, RJ, CH], F32R)
        lo = sb("lo", [P, RJ, CH], F32R)
        v = sb("v", [P, SUB, NH, VW], F32)
        pb = [ctx.enter_context(nc.psum_tensor(f"F_pb{i}", [P, CH], F32)) for i in range(8)]
        c_in, got, eps_set = sem("F_c_in", 0), sem("F_got", 0), sem("F_eps")
        var_done, sd_done, n_done, x_copied = sem("F_var"), sem("F_sd"), sem("F_n"), sem("F_xc")
        t_done, xt_done, l_done, lat_done = sem("F_t"), sem("F_xt"), sem("F_l"), sem("F_lat")
        r_mm, r_read, r_done, hi_done, lo_done = sem("F_rmm"), sem("F_rr"), sem("F_r"), sem("F_hi"), sem("F_lo")
        v_mm, v_done, stored, dch, fence = sem("F_vmm"), sem("F_v"), sem("F_st"), sem("F_dch"), sem("F_fence")
        sem.start()
        block = ctx.enter_context(nc.Block())

        def chunks(eng, body):
            with eng.Fori(0, B) as b:
                with eng.Fori(0, CPB) as c:
                    body(b * CPB + c, b, c)

        @block.gpsimd
        def _(pool):
            pool.memset(eps[:], EPS).then_inc(eps_set, 1)
            pool.memset(v[:], 1.0).then_inc(eps_set, 1)
            for b in range(B):
                for q in range(QT):
                    for k in range(TOPK):
                        pool.indirect_dma_start(Y[:, b * QT + q, k], None, eout,
                                                bass.IndirectOffsetOnAxis(slot_g[:, b, k, q:q + 1], 0),
                                                bounds_check=E_ * ROWS - 1, oob_is_err=False).then_inc(got, 16)

        @block.tensor
        def _(pe):
            pe.wait_ge(c_in, 16 * 9)

            def body(n, b, c):
                pe.wait_ge(n_done, n + 2)
                for kc in range(KC):
                    for s in range(SUB):
                        last = pe.transpose(pb[kc][:, s * P:(s + 1) * P], xn[:, s, kc * P:(kc + 1) * P], idf[:])
                last.then_inc(t_done, 1)
                pe.wait_ge(xt_done, n + 2)
                pe.wait_ge(v_done, n + 1)
                for kc in range(KC):
                    last = pe.matmul(pb[2][0:LAT], wd[:, kc], xnT[:, kc], start=kc == 0, stop=kc == KC - 1)
                last.then_inc(l_done, 1)
                for j in range(RJ):
                    pe.wait_ge(r_read, n * RJ + j + 2)
                    m = j % KC
                    if j == KC:
                        pe.wait_ge(lat_done, n + 2)
                    for i, name in enumerate(("q", "qs") if j < KC else ("k", "ks")):
                        bank = pb[3 + 2 * (j % 2) + i]
                        if j < KC:
                            for kc in range(KC):
                                last = pe.matmul(bank[:], wt[name][:, kc, m * P:(m + 1) * P], xnT[:, kc],
                                                 start=kc == 0, stop=kc == KC - 1)
                        else:
                            last = pe.matmul(bank[:], wkt[name][:, m * P:(m + 1) * P], lat[:], start=True, stop=True)
                    last.then_inc(r_mm, 1)
                for s in range(SUB):
                    last = pe.matmul(pb[(7, 2)[s // 2]][:, s % 2 * D:(s % 2 + 1) * D], lat[:, s * P:(s + 1) * P],
                                     wkt["v"][:], start=True, stop=True)
                last.then_inc(v_mm, 1)
            chunks(pe, body)

        @block.scalar
        def _(act):
            act.wait_ge(eps_set, 3)

            def body(n, b, c):
                act.wait_ge(var_done, n + 2)
                act.activation(sd[:], mv[:, :, 1], ACT.Sqrt, bias=eps[:]).then_inc(sd_done, 1)
                act.wait_ge(n_done, n + 2)
                act.activation(X[:, ds(n * SUB, SUB), :], xn[:], ACT.Copy).then_inc(x_copied, 1)
                act.wait_ge(t_done, n + 2)
                act.wait_ge(v_mm, n + 1)
                for kc in range(KC):
                    last = act.activation(xnT[:, kc], pb[kc][:], ACT.Copy)
                last.then_inc(xt_done, 1)
                act.wait_ge(l_done, n + 2)
                act.activation(lat[:], pb[2][0:LAT], ACT.Copy).then_inc(lat_done, 1)
                act.wait_ge(stored, n * (16 * STORES) + 1)
                for j in range(RJ):
                    act.wait_ge(r_done, n * RJ + j + 2)
                    act.activation(hi[:, j], r[:, j % 2], ACT.Copy).then_inc(hi_done, 1)
                act.wait_ge(v_mm, n + 2)
                for s in range(SUB):
                    last = act.activation(v[:, s, :, 0:HD], pb[(7, 2)[s // 2]][:, s % 2 * D:(s % 2 + 1) * D].rearrange(
                        "p (h e) -> p h e", e=HD), ACT.Copy)
                last.then_inc(v_done, 1)
            chunks(act, body)

        @block.vector
        def _(dve):
            ch = Chain(dve, dch, 2 * SUB + 2 + SUB - 1 + RJ - 1)
            dve.wait_ge(c_in, 16 * 9)
            dve.wait_ge(got, 16 * NT * TOPK)
            dve.sem_inc(r_read, 2)

            def body(n, b, c):
                ch.start(n)
                for s in range(SUB):
                    tile = n * SUB + s
                    t0 = Y[:, ds(tile, 1), 0, :].rearrange("p o c -> p (o c)")
                    ch.link(dve.scalar_tensor_tensor(y[:, s], t0, prob[:, 0, ds(tile, 1)],
                                                     X[:, ds(tile, 1), :].rearrange("p o c -> p (o c)"),
                                                     ALU.mult, ALU.add))
                for s in range(SUB):
                    tile = n * SUB + s
                    t0 = Y[:, ds(tile, 1), 1, :].rearrange("p o c -> p (o c)")
                    ch.link(dve.scalar_tensor_tensor(y[:, s], t0, prob[:, 1, ds(tile, 1)], y[:, s],
                                                     ALU.mult, ALU.add))
                for s in range(SUB):
                    last = dve.bn_stats(st[:, s], y[:, s])
                ch.link(last)
                dve.sem_inc(fence, 1)
                for s in range(SUB):
                    last = dve.bn_aggr(mv[:, s], st[:, s])
                last.then_inc(var_done, 1)
                dve.wait_ge(sd_done, n + 2)
                ch.link(dve.reciprocal(rs[:], sd[:]))
                dve.wait_ge(x_copied, n + 1)
                dve.wait_ge(t_done, n + 1)
                for s in range(SUB):
                    last = dve.tensor_scalar(xn[:, s], y[:, s], mv[:, s, 0:1], rs[:, s:s + 1], ALU.subtract, ALU.mult)
                    if s == SUB - 1:
                        last.then_inc(n_done, 1)
                    else:
                        ch.link(last)
                for j in range(RJ):
                    dve.wait_ge(r_mm, n * RJ + j + 2)
                    main, swap = pb[3 + 2 * (j % 2)], pb[4 + 2 * (j % 2)]
                    dve.tensor_tensor(t1[:], main[:], co[:, ds(c * CH, CH)], ALU.mult)
                    last = dve.tensor_tensor(t2[:], swap[:], si[:, ds(c * CH, CH)], ALU.mult)
                    last.then_inc(r_read, 1)
                    dve.wait_ge(r_read, n * RJ + j + 4)
                    dve.tensor_tensor(r[:, j % 2], t1[:], t2[:], ALU.add).then_inc(r_done, 1)
                    dve.wait_ge(hi_done, n * RJ + j + 2)
                    last = dve.tensor_tensor(lo[:, j], r[:, j % 2], hi[:, j].bitcast(F32), ALU.subtract)
                    if j == RJ - 1:
                        last.then_inc(lo_done, 1)
                    else:
                        ch.link(last)
                ch.end()
            chunks(dve, body)
            dve.wait_ge(x_copied, TOK // CH + 1)

        @block.sync
        def _(sp):
            sp.dma_start(idf[:], ident).then_inc(c_in, 16)
            for n, src in (("q", wq), ("qs", wqs)):
                sp.dma_start(wt[n][:], src.rearrange("(kc p) n -> p kc n", p=P)).then_inc(c_in, 16)
            sp.dma_start(wd[:], wdown.rearrange("(kc p) n -> p kc n", p=P)).then_inc(c_in, 16)
            for n, src in (("k", wk), ("ks", wks), ("v", wv)):
                sp.dma_start(wkt[n][:], src).then_inc(c_in, 16)
            sp.dma_start(co[:], cos).then_inc(c_in, 16)
            sp.dma_start(si[:], sin).then_inc(c_in, 16)
            vs_v = vs.rearrange("(bb g t) e -> bb t g e", bb=B, g=NG)

            def body(n, b, c):
                sp.wait_ge(lo_done, n + 2)
                for j in range(RJ):
                    for dst, src in (((qh, hi), (ql, lo)) if j < KC else ((kh, hi), (kl, lo))):
                        sp.dma_start(dst[ds(b * D + j % KC * P, P), ds(c * CH, CH)], src[:, j].bitcast(F32)
                                     ).then_inc(stored, 16)
                sp.wait_ge(v_done, n + 2)
                for s in range(SUB):
                    sp.dma_start(vs_v[ds(b, 1), ds(c * CH + s * P, P)].rearrange("o t g e -> (o t) g e"),
                                 v[:, s]).then_inc(stored, 16)
            chunks(sp, body)
            sp.wait_ge(stored, 16 * STORES * (TOK // CH) + 1)


LH, LD = 8, 64
INNER = LH * LD
WIN = S // P
VE = LD + 1
HIDF = int(D * 4 * 2 / 3)
FT = -(-HIDF // P)
FLAST = HIDF - (FT - 1) * P
PADS = S + 1
PADW = S + P
PAIRS = INNER // P


def tiles(eng, body):
    with eng.Fori(0, B) as b:
        with eng.Fori(0, WIN // 2) as pair:
            for u in range(2):
                body(b * WIN + pair * 2 + u, b, pair * 2 + u, b * (WIN // 2) + pair, u)


def local_projections(nc, sem, tag, xp, wqkv, tab, scales, ident, qT, kT, ve):
    W2 = 2 * INNER
    NB = 2 * LH
    with ExitStack() as ctx:
        sb = lambda n, s, t: ctx.enter_context(nc.sbuf_tensor(tag + n, s, t))
        w = sb("w", [P, KC, 3 * INNER], F32)
        h = sb("h", [P, 2, D], F32)
        hT = sb("hT", [P, 2, KC, P], F32)
        tb = sb("tb", [P, 4, WIN, LD], F32)
        sc = sb("sc", [P, 2, LD], F32)
        A = sb("A", [P, 2, WIN, LD], F32)
        R = sb("R", [P, 2, WIN, LD], F32)
        sq = sb("sq", [P, 2, W2], F32)
        ss = sb("ss", [P, 2, NB], F32)
        nr = sb("nr", [P, 2, NB], F32)
        rn = sb("rn", [P, 2, NB], F32)
        qn = sb("qn", [P, 2, 2, LH, LD], F32)
        t1 = sb("t1", [P, 2, 2, LH, LD], F32)
        t2 = sb("t2", [P, 2, 2, LH, LD], F32)
        v = sb("v", [P, 2, LH, VE], F32)
        tT = sb("tT", [P, 2, 2, PAIRS, P], F32)
        idf = sb("idf", [P, P], F32)
        pqk = [ctx.enter_context(nc.psum_tensor(f"{tag}pqk{u}", [P, 2, CH], F32)) for u in range(2)]
        pv = [ctx.enter_context(nc.psum_tensor(f"{tag}pv{u}", [P, CH], F32)) for u in range(2)]
        ph = [ctx.enter_context(nc.psum_tensor(f"{tag}ph{u}", [P, CH], F32)) for u in range(2)]
        c_in, h_in, v_set = sem(tag + "c_in", 0), [sem(f"{tag}h_in{u}", 0) for u in range(2)], sem(tag + "vs")
        t_done, ht_done, qk_mm, v_mm = sem(tag + "t"), sem(tag + "ht"), sem(tag + "qkmm"), sem(tag + "vmm")
        sq_done, ss_done, nr_done, qn_done = sem(tag + "sq"), sem(tag + "ss"), sem(tag + "nr"), sem(tag + "qn")
        t2_done, r_done, qt_done, ev_done = sem(tag + "t2"), sem(tag + "r"), sem(tag + "qt"), sem(tag + "ev")
        v_done, stored, dch = sem(tag + "v"), [sem(f"{tag}st{u}") for u in range(2)], sem(tag + "dch")
        pch, tabs = sem(tag + "pch"), sem(tag + "tabs")
        sem.start()
        block = ctx.enter_context(nc.Block())
        NST = 3

        def pairs(eng, body):
            with eng.Fori(0, B) as b:
                with eng.Fori(0, WIN // 2) as pair:
                    body(b * (WIN // 2) + pair, b, pair)

        @block.sync
        def _(sp):
            sp.dma_start(w[:], wqkv.rearrange("(kc p) n -> p kc n", p=P)).then_inc(c_in, 16)
            sp.dma_start(tb[:], tab.rearrange("(k w p) d -> p k w d", p=P, w=WIN)).then_inc(c_in, 16)
            sp.dma_start(sc[:].rearrange("p k d -> p (k d)"), scales.to_broadcast([P, 2 * LD])).then_inc(c_in, 16)
            sp.dma_start(idf[:], ident).then_inc(c_in, 16)

            def body(m, b, pair):
                for u in range(2):
                    sp.wait_ge(t_done, m * 2 + u + 1)
                    row = b * PADS + pair * (2 * P) + u * P
                    sp.dma_start(h[:, u, 0:P], xp[ds(row + 1, P), 0:P]).then_inc(h_in[u], 16)
                    sp.dma_start(h[:, u, P:D], xp[ds(row, P), P:D]).then_inc(h_in[u], 16)
                for u in range(2):
                    sp.wait_ge(ev_done, m * 2 + u + 2)
                    col = P + pair * (2 * P) + u * P
                    sp.dma_start(qT[ds(b * INNER, INNER), ds(pair * (2 * P) + u * P, P)].rearrange(
                        "(g p) t -> p g t", p=P), tT[:, u, 0]).then_inc(stored[u], 16)
                    sp.dma_start(kT[ds(b * INNER, INNER), ds(col, P)].rearrange("(g p) t -> p g t", p=P), tT[:, u, 1]
                                 ).then_inc(stored[u], 16)
                    sp.dma_start(ve[ds(b * PADW + col, P), :], v[:, u].rearrange("p h e -> p (h e)")
                                 ).then_inc(stored[u], 16)
            pairs(sp, body)
            for u in range(2):
                sp.wait_ge(stored[u], 16 * NST * (NT // 2) + 1)

        @block.tensor
        def _(pe):
            pe.wait_ge(c_in, 64)

            def body(m, b, pair):
                for u in range(2):
                    pe.wait_ge(h_in[u], m * 32 + 32)
                    pe.wait_ge(ht_done, m * 2 + u + 1)
                    for kc in range(KC):
                        last = pe.transpose(ph[u][:, kc * P:(kc + 1) * P], h[:, u, kc * P:(kc + 1) * P], idf[:])
                    last.then_inc(t_done, 1)
                for u in range(2):
                    pe.wait_ge(ht_done, m * 2 + u + 2)
                    pe.wait_ge(ev_done, m * 2 + 1)
                    for j in range(3):
                        for kc in range(KC):
                            last = pe.matmul(pqk[u][:, j] if j < 2 else pv[u][:], hT[:, u, kc],
                                             w[:, kc, j * INNER:(j + 1) * INNER], start=kc == 0, stop=kc == KC - 1)
                        if j == 1:
                            last.then_inc(qk_mm, 1)
                    last.then_inc(v_mm, 1)
                for u in range(2):
                    pe.wait_ge(r_done, m * 2 + u + 2)
                    for j in range(2):
                        for g in range(PAIRS):
                            last = pe.transpose(pqk[u][:, j, g * P:(g + 1) * P],
                                                t1[:, u, j].rearrange("p h e -> p (h e)")[:, g * P:(g + 1) * P], idf[:])
                    last.then_inc(qt_done, 1)
            pairs(pe, body)

        @block.scalar
        def _(act):
            act.wait_ge(v_set, 2)

            def body(m, b, pair):
                for u in range(2):
                    act.wait_ge(t_done, m * 2 + u + 2)
                    act.activation(hT[:, u].rearrange("p k t -> p (k t)"), ph[u][:, 0:D], ACT.Copy).then_inc(ht_done, 1)
                for u in range(2):
                    act.wait_ge(qk_mm, m * 2 + u + 2)
                    act.activation(sq[:, u], pqk[u][:].rearrange("p j c -> p (j c)"), ACT.Square).then_inc(sq_done, 1)
                    act.wait_ge(ss_done, m * 2 + u + 2)
                    act.activation(nr[:, u], ss[:, u], ACT.Sqrt).then_inc(nr_done, 1)
                    act.wait_ge(v_mm, m * 2 + u + 2)
                    act.wait_ge(stored[u], m * (16 * NST) + 1)
                    act.activation(v[:, u, :, 0:LD], pv[u][:].rearrange("p (h e) -> p h e", e=LD), ACT.Copy
                                   ).then_inc(v_done, 1)
                for u in range(2):
                    act.wait_ge(qt_done, m * 2 + u + 2)
                    act.activation(tT[:, u].rearrange("p j g t -> p j (g t)"), pqk[u][:], ACT.Copy).then_inc(ev_done, 1)
            pairs(act, body)

        @block.gpsimd
        def _(pool):
            pool.wait_ge(tabs, 2)

            def body(m, b, pair):
                for u in range(2):
                    pool.wait_ge(qn_done, m * 2 + u + 2)
                    H = LD // 2
                    for a, z in ((0, H), (H, 0)):
                        last = pool.tensor_tensor(
                            t2[:, u, :, :, a:a + H], qn[:, u, :, :, z:z + H],
                            R[:, :, ds(pair * 2 + u, 1), a:a + H].to_broadcast([P, 2, LH, H]), ALU.mult)
                    last.then_inc(t2_done, 1)
            pairs(pool, body)

        @block.vector
        def _(dve):
            H = LD // 2
            dve.wait_ge(c_in, 64)
            dve.memset(v[:], 1.0).then_inc(v_set, 1)
            for j in range(2):
                dve.tensor_tensor(A[:, j], tb[:, 2 * j], sc[:, j:j + 1].to_broadcast([P, WIN, LD]), ALU.mult)
                for a, z in ((0, H), (H, 0)):
                    last = dve.tensor_tensor(R[:, j, :, a:a + H], tb[:, 2 * j + 1, :, a:a + H],
                                             sc[:, j:j + 1, z:z + H].to_broadcast([P, WIN, H]), ALU.mult)
            last.then_inc(tabs, 1)
            dve.wait_ge(tabs, 2)
            ch = Chain(dve, dch, 6)

            def body(m, b, pair):
                ch.start(m)
                for u in range(2):
                    dve.wait_ge(sq_done, m * 2 + u + 2)
                    dve.tensor_reduce(ss[:, u], sq[:, u].rearrange("p (n e) -> p n e", e=LD), AX, ALU.add
                                      ).then_inc(ss_done, 1)
                    dve.wait_ge(nr_done, m * 2 + u + 2)
                    ch.link(dve.tensor_scalar(nr[:, u], nr[:, u], 1e-12, None, ALU.max))
                    ch.link(dve.reciprocal(rn[:, u], nr[:, u]))
                    dve.wait_ge(t2_done, m * 2 + u + 1)
                    dve.tensor_tensor(qn[:, u].rearrange("p j h e -> p (j h) e"),
                                      pqk[u][:].rearrange("p j (h e) -> p (j h) e", e=LD),
                                      rn[:, u].unsqueeze(2).to_broadcast([P, NB, LD]), ALU.mult).then_inc(qn_done, 1)
                    dve.wait_ge(qn_done, m * 2 + u + 2)
                    dve.wait_ge(qt_done, m * 2 + 1)
                    ch.link(dve.tensor_tensor(t1[:, u], qn[:, u],
                                              A[:, :, ds(pair * 2 + u, 1), :].to_broadcast([P, 2, LH, LD]), ALU.mult))
                    dve.wait_ge(t2_done, m * 2 + u + 2)
                    dve.tensor_tensor(t1[:, u], t1[:, u], t2[:, u], ALU.add).then_inc(r_done, 1)
            pairs(dve, body)


def local_attention(nc, sem, tag, qT, kT, ve, wo, masks, ident_bf, ident, X, xp):
    def pos(h):
        return h % 2 * (LH // 2) + h // 2

    HB = LH // 2
    BANK = [0, 1, 1, 0]
    with ExitStack() as ctx:
        sb = lambda n, s, t: ctx.enter_context(nc.sbuf_tensor(tag + n, s, t))
        q = sb("q", [P, 2, PAIRS, P], F32)
        k = sb("k", [P, 2, PAIRS, 2 * P], F32)
        v = sb("v", [P, 2, 2, LH * VE], F32)
        pr = sb("pr", [P, 2, LH, 2 * P], F32)
        pT = sb("pT", [P, 4, 2, 2, P], F32)
        mx = sb("mx", [P, 2, LH], F32)
        nm = sb("nm", [P, 2, LH], F32)
        rc = sb("rc", [P, LH], F32)
        cx = sb("cx", [P, LH, LD], F32)
        cT = sb("cT", [P, PAIRS, P], F32)
        xn = sb("xn", [P, 2, D], F32)
        w = sb("w", [P, PAIRS, D], F32)
        mk = sb("mk", [P, NT, 2 * P], BF16)
        idb = sb("idb", [P, P], BF16)
        idf = sb("idf", [P, P], F32)
        pS = ctx.enter_context(nc.psum_tensor(tag + "pS", [P, LH, 2 * P], F32))
        pP = [ctx.enter_context(nc.psum_tensor(f"{tag}pP{i}", [P, CH], F32)) for i in range(2)]
        pO = [ctx.enter_context(nc.psum_tensor(f"{tag}pO{i}", [P, CH], F32)) for i in range(2)]
        c_in, used = sem(tag + "c_in", 0), sem(tag + "used")
        in_, v_in = [sem(f"{tag}in{u}", 0) for u in range(2)], [sem(f"{tag}vin{u}", 0) for u in range(2)]
        s_done, m_done, nm_done, e_done = sem(tag + "s"), sem(tag + "m"), sem(tag + "nm"), sem(tag + "e")
        t_done, te_done, o_mm, cx_done = sem(tag + "t"), [sem(f"{tag}te{i}") for i in range(2)], sem(tag + "omm"), sem(tag + "cx")
        ct_mm, ct_done, w_mm, x_done = sem(tag + "ctm"), sem(tag + "ct"), sem(tag + "wmm"), sem(tag + "x")
        fence = sem(tag + "fence")
        x_out, xc, dch = [sem(f"{tag}xo{u}") for u in range(2)], sem(tag + "xc"), sem(tag + "dch")
        sem.start()
        block = ctx.enter_context(nc.Block())

        def skewed(eng, first, body, finish):
            first()
            body(0, 0, 0, True, False)
            body(1, 0, 1, True, True)
            with eng.Fori(1, NT // 2 - 1) as m:
                for u in range(2):
                    body(m * 2 + u, m, u, True, True)
            body(NT - 2, NT // 2 - 1, 0, True, True)
            body(NT - 1, NT // 2 - 1, 1, False, True)
            finish(NT, NT // 2, 0)

        @block.gpsimd
        def _(pool):
            for dst, src in ((w[:], wo.rearrange("(g p) n -> p g n", p=P)), (idb[:], ident_bf), (idf[:], ident),
                             (mk[:], masks.rearrange("(w p) k -> p w k", p=P))):
                pool.dma_start(dst, src).then_inc(c_in, 16)

            def body(n, b, win, m, u):
                wait_apart(pool, s_done, n, fence)
                pool.dma_start(q[:, u], qT[ds(b * INNER, INNER), ds(win * P, P)].rearrange("(g p) t -> p g t", p=P)
                               ).then_inc(in_[u], 16)
                pool.dma_start(k[:, u], kT[ds(b * INNER, INNER), ds(win * P, 2 * P)].rearrange(
                    "(g p) t -> p g t", p=P)).then_inc(in_[u], 16)
                wait_apart(pool, used, n + 1, fence)
                pool.dma_start(v[:, u], ve[ds(b * PADW + win * P, 2 * P), :].rearrange("(s p) e -> p s e", p=P)
                               ).then_inc(v_in[u], 16)
            tiles(pool, body)

        @block.tensor
        def _(pe):
            pe.sem_inc(used, 2)
            pe.sem_inc(s_done, 1)
            pe.wait_ge(c_in, 64)

            def scores(n, u, m):
                pe.wait_ge(in_[u], m * 32 + 32)
                pe.wait_ge(e_done, n + 1)
                for i in range(4):
                    pe.matmul(pS[:, 2 * i:2 * i + 2, :], idb[:], mk[:, ds(n, 1), :].to_broadcast([P, 2, 2 * P]),
                              start=True, stop=False, skip_group_check=True)
                for h in sorted(range(LH), key=pos):
                    a = h % 2 * LD
                    last = pe.matmul(pS[:, pos(h), :], q[a:a + LD, u, h // 2], k[a:a + LD, u, h // 2],
                                     start=False, stop=True, skip_group_check=True)
                last.then_inc(s_done, 1)

            def turn(r, n, u):
                for i in range(2):
                    for s in range(2):
                        last = pe.transpose(pP[BANK[r]][:, (2 * i + s) * P:(2 * i + s + 1) * P],
                                            pr[:, u, 2 * r + i, s * P:(s + 1) * P], idf[:])
                last.then_inc(t_done, 1)

            def weigh(r, u):
                for i in range(2):
                    h = next(h for h in range(LH) if pos(h) == 2 * r + i)
                    for s in range(2):
                        last = pe.matmul(pO[h // HB][:, h % HB * VE:(h % HB + 1) * VE], pT[:, r, i, s],
                                         v[:, u, s, h * VE:(h + 1) * VE], start=s == 0, stop=s == 1)
                return last

            def turn_outputs(n):
                pe.wait_ge(cx_done, n + 1)
                for g in range(PAIRS):
                    last = pe.transpose(pP[0][:, g * P:(g + 1) * P],
                                        cx[:].rearrange("p h e -> p (h e)")[:, g * P:(g + 1) * P], idf[:])
                last.then_inc(ct_mm, 1)

            def project(n):
                for g in range(PAIRS):
                    last = pe.matmul(pO[0][:, 0:D], cT[:, g], w[:, g], start=g == 0, stop=g == PAIRS - 1)
                last.then_inc(w_mm, 1)

            def body(n, m, u, nxt, prev):
                pe.wait_ge(e_done, n + 2)
                pe.wait_ge(te_done[0], n * 2 + 1)
                turn(0, n, u)
                pe.wait_ge(te_done[1], n * 2 + 1)
                turn(1, n, u)
                if nxt:
                    scores(n + 1, 1 - u, m + u)
                pe.wait_ge(te_done[0], n * 2 + 2)
                if prev:
                    turn_outputs(n)
                pe.wait_ge(te_done[1], n * 2 + 2)
                turn(2, n, u)
                if prev:
                    pe.wait_ge(ct_done, n + 1)
                turn(3, n, u)
                if prev:
                    project(n)
                pe.wait_ge(v_in[u], m * 16 + 16)
                weigh(1, u)
                pe.wait_ge(te_done[0], n * 2 + 3)
                weigh(3, u)
                if prev:
                    pe.wait_ge(x_done, n + 1)
                weigh(0, u)
                pe.wait_ge(te_done[1], n * 2 + 3)
                weigh(2, u).then_inc(o_mm, 1)
                pe.drain().then_inc(used, 1)

            def finish(n, m, u):
                turn_outputs(n)
                pe.wait_ge(ct_done, n + 1)
                project(n)
            skewed(pe, lambda: scores(0, 0, 0), body, finish)

        @block.scalar
        def _(act):
            def exps(n, u):
                act.wait_ge(nm_done, n + 2)
                for p_ in range(LH):
                    last = act.activation(pr[:, u, p_], pS[:, p_, :], ACT.Exp, bias=nm[:, u, p_:p_ + 1], scale=8.0)
                last.then_inc(e_done, 1)

            def evict(r, done):
                act.wait_ge(t_done, done)
                act.activation(pT[:, r].rearrange("p i s t -> p (i s t)"), pP[0][:], ACT.Copy).then_inc(te_done[0], 1)

            def outputs(n):
                act.wait_ge(ct_mm, n + 1)
                act.activation(cT[:].rearrange("p g t -> p (g t)"), pP[0][:], ACT.Copy).then_inc(ct_done, 1)

            def result(n, u):
                act.wait_ge(x_done, n + 1)
                act.activation(X[:, ds(n - 1, 1), :], xn[:, 1 - u:2 - u], ACT.Copy).then_inc(xc, 1)

            def body(n, m, u, nxt, prev):
                evict(0, n * 4 + 2)
                if prev:
                    outputs(n)
                evict(3, n * 4 + 5)
                if nxt:
                    exps(n + 1, 1 - u)
                if prev:
                    result(n, u)

            def finish(n, m, u):
                outputs(n)
                result(n, u)
            skewed(act, lambda: exps(0, 0), body, finish)

        @block.vector
        def _(dve):
            ch = Chain(dve, dch, 1)

            def maxima(n, u):
                dve.wait_ge(s_done, n + 3)
                dve.tensor_reduce(mx[:, u], pS[:], AX, ALU.max).then_inc(m_done, 1)
                dve.wait_ge(m_done, n + 2)
                dve.tensor_scalar(nm[:, u], mx[:, u], -8.0, None, ALU.mult).then_inc(nm_done, 1)

            def evict(r, done):
                dve.wait_ge(t_done, done)
                dve.tensor_copy(pT[:, r].rearrange("p i s t -> p (i s t)"), pP[1][:]).then_inc(te_done[1], 1)

            def result(n, m, u):
                dve.wait_ge(w_mm, n + 1)
                dve.wait_ge(x_out[1 - u], (m - 1) * 16 + 1 if u == 0 else m * 16 + 1)
                dve.wait_ge(xc, n)
                dve.tensor_tensor(xn[:, 1 - u:2 - u], pO[0][:, 0:D].unsqueeze(1), X[:, ds(n - 1, 1), :], ALU.add
                                  ).then_inc(x_done, 1)

            def body(n, m, u, nxt, prev):
                ch.start(n)
                evict(1, n * 4 + 3)
                if nxt:
                    maxima(n + 1, 1 - u)
                evict(2, n * 4 + 4)
                if prev:
                    result(n, m, u)
                dve.wait_ge(o_mm, n + 2)
                o = [pO[i][:, 0:HB * VE].rearrange("p (h e) -> p h e", e=VE) for i in range(2)]
                for i in range(2):
                    last = dve.reciprocal(rc[:, i * HB:(i + 1) * HB], o[i][:, :, LD])
                ch.link(last)
                for i in range(2):
                    last = dve.tensor_tensor(cx[:, i * HB:(i + 1) * HB], o[i][:, :, 0:LD],
                                             rc[:, i * HB:(i + 1) * HB].unsqueeze(2).to_broadcast([P, HB, LD]),
                                             ALU.mult)
                last.then_inc(cx_done, 1)
            skewed(dve, lambda: maxima(0, 0), body, result)
            dve.wait_ge(xc, NT + 1)

        @block.sync
        def _(sp):
            def body(n, b, win, m, u):
                sp.wait_ge(x_done, n + 2)
                sp.dma_start(xp[ds(b * PADS + win * P + 1, P), :], xn[:, u]).then_inc(x_out[u], 16)
            tiles(sp, body)
            for u in range(2):
                sp.wait_ge(x_out[u], 16 * (NT // 2) + 1)


def gated_unit(nc, sem, tag, xp, lng, lnb, w1, b1a, b1g, w2, b2, ident, X, xp_out, xp_first, out):
    NCK = TOK // CH
    final = out is not None
    with ExitStack() as ctx:
        sb = lambda n, s, t: ctx.enter_context(nc.sbuf_tensor(tag + n, s, t))
        W1 = sb("W1", [P, KC, 2 * HIDF], F32)
        W2 = sb("W2", [P, FT, D], F32)
        g_ = sb("g_", [P, KC], F32)
        b_ = sb("b_", [P, KC], F32)
        ba = sb("ba", [P, FT], F32)
        bg = sb("bg", [P, FT], F32)
        bb = sb("bb", [P, D], F32)
        h = sb("h", [P, 2, SUB, D], F32)
        hn = sb("hn", [P, SUB, D], F32)
        hT = sb("hT", [P, 2, KC, CH], F32)
        gl = sb("gl", [P, 2, CH], F32)
        hid = sb("hid", [P, FT, CH], F32)
        y = sb("y", [P, SUB, D], F32)
        y2 = sb("y2", [P, 2, SUB, D], F32)
        x0 = sb("x0", [P, 2, SUB, D], F32)
        st = sb("st", [P, SUB, 6], F32)
        mv = sb("mv", [P, SUB, 2], F32)
        sd = sb("sd", [P, SUB], F32)
        rs = sb("rs", [P, SUB], F32)
        st2 = sb("st2", [P, SUB, 6], F32)
        mv2 = sb("mv2", [P, SUB, 2], F32)
        sd2 = sb("sd2", [P, SUB], F32)
        rs2 = sb("rs2", [P, SUB], F32)
        eps = sb("eps", [P, 1], F32)
        idf = sb("idf", [P, P], F32)
        pT = [ctx.enter_context(nc.psum_tensor(f"{tag}pT{i}", [P, CH], F32)) for i in range(2)]
        pA = [ctx.enter_context(nc.psum_tensor(f"{tag}pA{i}", [P, CH], F32)) for i in range(2)]
        pG = [ctx.enter_context(nc.psum_tensor(f"{tag}pG{i}", [P, CH], F32)) for i in range(2)]
        pO = [ctx.enter_context(nc.psum_tensor(f"{tag}pO{i}", [P, CH], F32)) for i in range(2)]
        c_in, h_in = sem(tag + "c_in", 0), [sem(f"{tag}h_in{u}", 0) for u in range(2)]
        var, sdd, n_done, t_done = sem(tag + "var"), sem(tag + "sdd"), sem(tag + "n"), sem(tag + "t")
        xt_done, ag_mm, gl_done, hid_done = sem(tag + "xt"), sem(tag + "ag"), sem(tag + "gl"), sem(tag + "hid")
        o_mm, y_done, x_done, xc = sem(tag + "omm"), sem(tag + "y"), sem(tag + "x"), sem(tag + "xc")
        var2, sdd2, eps_set = sem(tag + "var2"), sem(tag + "sdd2"), sem(tag + "eps")
        fence = sem(tag + "fence")
        dch, och, x_out = sem(tag + "dch"), sem(tag + "och"), [sem(f"{tag}xo{u}") for u in range(2)]
        sem.start()
        block = ctx.enter_context(nc.Block())
        x0_in, x_free = [sem(f"{tag}x0{u}", 0) for u in range(2)], sem(tag + "xf")
        NC_IN = 9

        def skewed(eng, first, body):
            first(0)
            with eng.Fori(0, NCK // 2 - 1) as m:
                for u in range(2):
                    body(m * 2 + u, m, u, True)
            body(NCK - 2, NCK // 2 - 1, 0, True)
            body(NCK - 1, NCK // 2 - 1, 1, False)

        def chunks(eng, body):
            with eng.Fori(0, B) as b:
                with eng.Fori(0, CPB // 2) as pair:
                    for u in range(2):
                        body(b * CPB + pair * 2 + u, b, pair * 2 + u, b * (CPB // 2) + pair, u)

        def rows(j):
            return P if j < FT - 1 else FLAST

        @block.gpsimd
        def _(pool):
            pool.memset(eps[:], EPS).then_inc(eps_set, 1)
            for dst, src in ((W1[:], w1.rearrange("(kc p) n -> p kc n", p=P)),
                             (W2[:, 0:FT - 1], w2[0:(FT - 1) * P, :].rearrange("(k p) n -> p k n", p=P)),
                             (W2[0:FLAST, FT - 1], w2[(FT - 1) * P:HIDF, :]), (g_[:], lng), (b_[:], lnb),
                             (ba[:], b1a), (bg[:], b1g), (bb[:], b2.to_broadcast([P, D])), (idf[:], ident)):
                pool.dma_start(dst, src).then_inc(c_in, 16)

            def body(n, b, c, m, u):
                wait_apart(pool, n_done, n, fence)
                row = b * PADS + c * CH
                pool.dma_start(h[:, u, :, 0:P], xp[ds(row + 1, CH), 0:P].rearrange("(s p) c -> p s c", p=P)
                               ).then_inc(h_in[u], 16)
                pool.dma_start(h[:, u, :, P:D], xp[ds(row, CH), P:D].rearrange("(s p) c -> p s c", p=P)
                               ).then_inc(h_in[u], 16)
                if final:
                    wait_apart(pool, x_free, n + 1, fence)
                    pool.dma_start(x0[:, u], xp_first[ds(row + 1, CH), :].rearrange("(s p) c -> p s c", p=P)
                                   ).then_inc(x0_in[u], 16)
            chunks(pool, body)

        @block.tensor
        def _(pe):
            pe.wait_ge(c_in, 16 * NC_IN)

            def turn(n):
                pe.wait_ge(n_done, n + 3)
                pe.wait_ge(xt_done, n + 1)
                for kc in range(KC):
                    for s in range(SUB):
                        last = pe.transpose(pT[kc][:, s * P:(s + 1) * P], hn[:, s, kc * P:(kc + 1) * P], idf[:])
                last.then_inc(t_done, 1)

            def body(n, m, u, nxt):
                pe.wait_ge(xt_done, n + 2)
                for j in range(FT):
                    pe.wait_ge(hid_done, n * FT + j + 2)
                    r = rows(j)
                    for bank, off in ((pG, HIDF), (pA, 0)):
                        for kc in range(KC):
                            last = pe.matmul(bank[j % 2][0:r, :], W1[:, kc, off + j * P:off + j * P + r], hT[:, u, kc],
                                             start=kc == 0, stop=kc == KC - 1)
                    last.then_inc(ag_mm, 1)
                if nxt:
                    turn(n + 1)
                pe.wait_ge(hid_done, (n + 1) * FT + 3)
                pe.wait_ge(y_done, n + 1)
                for s in range(SUB):
                    for j in range(FT):
                        r = rows(j)
                        last = pe.matmul(pO[s // 2][:, s % 2 * D:(s % 2 + 1) * D], hid[0:r, j, s * P:(s + 1) * P],
                                         W2[0:r, j], start=j == 0, stop=j == FT - 1)
                last.then_inc(o_mm, 1)
            skewed(pe, turn, body)

        @block.scalar
        def _(act):
            act.wait_ge(c_in, 16 * NC_IN)
            act.wait_ge(eps_set, 2)

            def norm(n, u):
                act.wait_ge(var, n + 2)
                act.activation(sd[:], mv[:, :, 1], ACT.Sqrt, bias=eps[:]).then_inc(sdd, 1)
                act.wait_ge(t_done, n + 2)
                for kc in range(KC):
                    last = act.activation(hT[:, u, kc], pT[kc][:], ACT.Identity, bias=b_[:, kc:kc + 1],
                                          scale=g_[:, kc:kc + 1])
                last.then_inc(xt_done, 1)

            def body(n, m, u, nxt):
                for j in range(FT):
                    r = rows(j)
                    act.wait_ge(ag_mm, n * FT + j + 2)
                    act.wait_ge(hid_done, n * FT + j + 2)
                    act.activation(gl[0:r, j % 2], pG[j % 2][0:r, :], ACT.Gelu, bias=bg[0:r, j:j + 1]
                                   ).then_inc(gl_done, 1)
                if nxt:
                    norm(n + 1, 1 - u)
                if final:
                    act.wait_ge(var2, n + 2)
                    act.activation(sd2[:], mv2[:, :, 1], ACT.Sqrt, bias=eps[:]).then_inc(sdd2, 1)
                else:
                    act.wait_ge(x_done, n + 2)
                    act.activation(X[:, ds(n * SUB, SUB), :], y2[:, u], ACT.Copy).then_inc(xc, 1)
            skewed(act, lambda n: norm(0, 0), body)

        @block.vector
        def _(dve):
            NL, OL = 2, (4 if final else 0)
            cn, co = Chain(dve, dch, NL), Chain(dve, och, OL)
            dve.wait_ge(c_in, 16 * NC_IN)
            dve.sem_inc(n_done, 1)
            if final:
                dve.sem_inc(x_free, 2)
            dve.sem_inc(hid_done, 2)

            def norm(n, m, u):
                cn.start(n)
                dve.wait_ge(h_in[u], m * 32 + 32)
                for s in range(SUB):
                    last = dve.bn_stats(st[:, s], h[:, u, s])
                cn.link(last)
                dve.sem_inc(fence, 1)
                for s in range(SUB):
                    last = dve.bn_aggr(mv[:, s], st[:, s])
                last.then_inc(var, 1)
                dve.wait_ge(sdd, n + 2)
                cn.link(dve.reciprocal(rs[:], sd[:]))
                dve.wait_ge(t_done, n + 1)
                for s in range(SUB):
                    last = dve.tensor_scalar(hn[:, s], h[:, u, s], mv[:, s, 0:1], rs[:, s:s + 1], ALU.subtract, ALU.mult)
                last.then_inc(n_done, 1)
                cn.end()

            def body(n, m, u, nxt):
                for j in range(FT):
                    r = rows(j)
                    dve.wait_ge(gl_done, n * FT + j + 2)
                    if j == 0:
                        dve.wait_ge(o_mm, n + 1)
                    dve.scalar_tensor_tensor(hid[0:r, j], pA[j % 2][0:r, :], ba[0:r, j:j + 1], gl[0:r, j % 2],
                                             ALU.add, ALU.mult).then_inc(hid_done, 1)
                if nxt:
                    norm(n + 1, m + u, 1 - u)
                co.start(n)
                dve.wait_ge(o_mm, n + 2)
                for k in range(2):
                    last = dve.tensor_tensor(y[:, 2 * k:2 * k + 2], pO[k][:].rearrange("p (s c) -> p s c", c=D),
                                             bb[:].unsqueeze(1).to_broadcast([P, 2, D]), ALU.add)
                last.then_inc(y_done, 1)
                dve.wait_ge(y_done, n + 2)
                dve.wait_ge(x_out[u], m * 16 + 1)
                if final:
                    co.link(dve.tensor_tensor(y[:], y[:], X[:, ds(n * SUB, SUB), :], ALU.add))
                    dve.wait_ge(x0_in[u], m * 16 + 16)
                    co.link(dve.tensor_tensor(y[:], y[:], x0[:, u], ALU.add))
                    for s in range(SUB):
                        last = dve.bn_stats(st2[:, s], y[:, s])
                    co.link(last)
                    dve.sem_inc(fence, 1)
                    for s in range(SUB):
                        last = dve.bn_aggr(mv2[:, s], st2[:, s])
                    last.then_inc(var2, 1)
                    dve.wait_ge(sdd2, n + 2)
                    co.link(dve.reciprocal(rs2[:], sd2[:]))
                    for s in range(SUB):
                        last = dve.tensor_scalar(y2[:, u, s], y[:, s], mv2[:, s, 0:1], rs2[:, s:s + 1], ALU.subtract,
                                                 ALU.mult)
                    last.then_inc(x_done, 1)
                    dve.drain().then_inc(x_free, 1)
                else:
                    dve.wait_ge(xc, n + 1)
                    dve.tensor_tensor(y2[:, u], y[:], X[:, ds(n * SUB, SUB), :], ALU.add).then_inc(x_done, 1)
                    co.end()
            skewed(dve, lambda n: norm(0, 0, 0), body)
            if not final:
                dve.wait_ge(xc, NCK + 1)

        @block.sync
        def _(sp):
            def body(n, b, c, m, u):
                sp.wait_ge(x_done, n + 2)
                if final:
                    dst = out[ds(n * CH, CH), :]
                else:
                    dst = xp_out[ds(b * PADS + c * CH + 1, CH), :]
                sp.dma_start(dst.rearrange("(s p) c -> p s c", p=P), y2[:, u]).then_inc(x_out[u], 16)
            chunks(sp, body)
            for u in range(2):
                sp.wait_ge(x_out[u], 16 * (NCK // 2) + 1)


def clear_buffers(nc, sem, ein, xps, kT, ve):
    WIDTH = E_ * ROWS * D // P
    CUT = 8
    with ExitStack() as ctx:
        z = ctx.enter_context(nc.sbuf_tensor("Z_z", [P, WIDTH // CUT], F32))
        zeroed, cleared = sem("Z_zeroed"), sem("Z_cleared")
        sem.start()
        block = ctx.enter_context(nc.Block())

        @block.vector
        def _(dve):
            dve.memset(z[:], 0.0).then_inc(zeroed, 1)

        @block.sync
        def _(sp):
            sp.wait_ge(zeroed, 2)
            flat = ein.rearrange("r c -> (r c)").rearrange("(p w) -> p w", p=P)
            n = 0
            for i in range(CUT):
                sp.dma_start(flat[:, i * (WIDTH // CUT):(i + 1) * (WIDTH // CUT)], z[:]).then_inc(cleared, 16)
                n += 1
            for b in range(B):
                for xp in xps:
                    sp.dma_start(xp[b * PADS:b * PADS + 1, :], z[0:1, 0:D]).then_inc(cleared, 16)
                    n += 1
                sp.dma_start(ve[b * PADW:b * PADW + P, :], z[:, 0:LH * VE]).then_inc(cleared, 16)
                sp.dma_start(kT[b * INNER:(b + 1) * INNER, 0:P].rearrange("(g p) t -> p g t", p=P),
                             z[:, 0:PAIRS * P].rearrange("p (g t) -> p g t", g=PAIRS)).then_inc(cleared, 16)
                n += 2
            sp.wait_ge(cleared, 16 * n + 1)


def build(nc, d, out):
    with ExitStack() as ctx:
        sem = Semaphores(nc)
        keep = lambda n, s, t=F32: ctx.enter_context(nc.sbuf_tensor(n, s, t))
        scratch = lambda n, s: nc.dram_tensor(n, s, F32).ap()
        inverse = scratch("inverse", (B * NH, S))
        X = keep("X", [P, NT, D])
        LG = keep("LG", [P, NT, E_])
        slot_s = keep("slot_s", [P, B, TOPK, S // P], U32)
        slot_g = keep("slot_g", [P, B, TOPK, S // P], U32)
        prob = keep("prob", [P, TOPK, NT])
        ein, eout = scratch("ein", (E_ * ROWS, D)), scratch("eout", (E_ * ROWS, D))
        xp = [scratch(f"xp{i}", (B * PADS, D)) for i in range(3)]
        lqT, lkT = scratch("lqT", (B * INNER, S)), scratch("lkT", (B * INNER, PADW))
        lve = scratch("lve", (B * PADW, LH * VE))
        m_rows = scratch("m_rows", (2, GRP * S))
        ot = scratch("ot", (NIT * P, S))

        clear_buffers(nc, sem, ein, xp, lkT, lve)
        qh, ql = scratch("qh0", (B * D, S)), scratch("ql0", (B * D, S))
        kh, kl = scratch("kh0", (B * NKV * HD, S)), scratch("kl0", (B * NKV * HD, S))
        vs = scratch("vs0", (NIT * S, VW))
        layer0_projections(nc, sem, d["xT"], d["a0_wqT"], d["a0_wkT"], d["a0_wvT"], qh, ql, kh, kl, vs)
        attention(nc, sem, "B_", 1, qh, ql, kh, kl, vs, d["causal"], d["causalT"], d["ident_bf"], d["ident"], m_rows, ot)
        attention_output(nc, sem, "C_", ot, d["a0_woT"], d["x"], X, d["ident"], (d["router_w"], d["router_b"], LG), None,
                         inverse)
        sem.clear()
        route(nc, sem, LG, d["tri"], d["iota8"], d["ones"], slot_s, slot_g, prob)
        experts(nc, sem, X, slot_s, ein, eout, d["w_fc"], d["b_fc"], d["w_gate"], d["b_gate"], d["w_proj"], d["b_proj"],
                d["ident"])
        qh1, ql1 = scratch("qh1", (B * D, S)), scratch("ql1", (B * D, S))
        kh1, kl1 = scratch("kh1", (B * D, S)), scratch("kl1", (B * D, S))
        vs1 = scratch("vs1", (NIT * S, GRP * VW))
        combine_and_project(nc, sem, X, eout, slot_g, prob, d["rope_cos"], d["rope_sin"], d["a1_wq"], d["a1_wqs"],
                            d["a1_wd"], d["a1_wk"], d["a1_wks"], d["a1_wv"], d["ident"], qh1, ql1, kh1, kl1, vs1)
        sem.clear()
        attention(nc, sem, "G_", GRP, qh1, ql1, kh1, kl1, vs1, d["paged"], d["pagedT"], d["ident_bf"], d["ident"],
                  m_rows, ot)
        attention_output(nc, sem, "H_", ot, d["a1_wo"], None, X, d["ident"], None, xp[0], inverse)
        for l in range(2):
            sem.clear()
            local_projections(nc, sem, f"I{l}_", xp[0] if l == 0 else xp[2], d[f"l{l}_wqkv"], d["xpos"],
                              d[f"l{l}_scales"], d["ident"], lqT, lkT, lve)
            local_attention(nc, sem, f"J{l}_", lqT, lkT, lve, d[f"l{l}_wo"], d["windows"], d["ident_bf"], d["ident"],
                            X, xp[1])
            gated_unit(nc, sem, f"K{l}_", xp[1], d[f"l{l}_lng"], d[f"l{l}_lnb"], d[f"l{l}_w1"], d[f"l{l}_b1a"],
                       d[f"l{l}_b1g"], d[f"l{l}_w2"], d[f"l{l}_b2"], d["ident"], X, xp[2] if l == 0 else None,
                       xp[0], out if l else None)


def shape_constants():
    c = {}
    i = np.arange(P)
    c["ident"] = np.eye(P, dtype=np.float32)
    c["ones"] = np.ones((P, P), np.float32)
    c["tri"] = (i[:, None] <= i[None, :]).astype(np.float32)
    c["iota8"] = np.tile(np.arange(E_, dtype=np.float32), (P, 1))
    page = i // PAGE
    bf = mybir.dt.np(BF16)
    c["ident_bf"] = np.eye(P).astype(bf)
    causal = np.where(i[None, :] > i[:, None], NEG, 0.0)
    paged = np.where(page[None, :] > page[:, None], NEG, 0.0)
    for name, m in (("causal", causal), ("paged", paged)):
        c[name], c[name + "T"] = m.astype(bf), np.ascontiguousarray(m.T).astype(bf)
    before = np.where(i[None, :] < i[:, None], NEG, 0.0)
    c["windows"] = np.concatenate([np.concatenate([before if t % WIN else np.full((P, P), NEG), causal], 1)
                                   for t in range(NT)]).astype(bf)
    inv = 1.0 / 10000.0 ** (np.arange(0, HD, 2, dtype=np.float32) / HD)
    ang = np.outer(np.arange(S, dtype=np.float32), inv)
    pair = i % HD // 2
    c["rope_cos"] = np.ascontiguousarray(np.cos(ang).T[pair]).astype(np.float32)
    sign = np.where(i % 2 == 0, -1.0, 1.0)[:, None]
    c["rope_sin"] = (np.sin(ang).T[pair] * sign).astype(np.float32)
    half = np.arange(0, LD, 2, dtype=np.float32)
    freq = np.arange(S, dtype=np.float32)[:, None] * (1.0 / 10000.0 ** (half / LD)).astype(np.float32)[None, :]
    freq = np.concatenate([freq, freq], -1)
    base = (half + np.float32(0.4 * LD)) / np.float32(1.4 * LD)
    power = (np.arange(S, dtype=np.float32) - S // 2) / np.float32(P // 2)
    scale = base[None, :] ** power[:, None]
    scale = np.concatenate([scale, scale], -1)
    sign = np.where(np.arange(LD) < LD // 2, -1.0, 1.0)
    cos, sin = np.cos(freq), np.sin(freq) * sign
    c["xpos"] = np.concatenate([cos * scale, sin * scale, cos / scale, sin / scale]).astype(np.float32)
    return c


def laid_out(v):
    a = {k: np.asarray(x) for k, x in v.items()}
    x = a["L0_attn_x"].reshape(TOK, D)
    d = {"x": x, "xT": x.T}
    for n in ("wq", "wk", "wv", "wo"):
        d[f"a0_{n}T"] = a[f"L0_attn_{n}"].T
    cols = lambda w: w.reshape(-1, P).T
    d["router_w"] = a["L0_ffn_router_w"]
    d["router_b"] = np.broadcast_to(a["L0_ffn_router_b"], (P, E_))
    d["w_fc"] = a["L0_ffn_w_c_fc"].reshape(E_ * D, HID_E)
    d["w_gate"] = a["L0_ffn_w_gate"].reshape(E_ * D, HID_E)
    d["w_proj"] = a["L0_ffn_w_c_proj"].reshape(E_ * HID_E, D)
    for n in ("fc", "gate"):
        b = a["L0_ffn_b_c_fc" if n == "fc" else "L0_ffn_b_gate"]
        d[f"b_{n}"] = b.reshape(E_, HT, P).transpose(0, 2, 1).reshape(E_ * P, HT)
    d["b_proj"] = a["L0_ffn_b_c_proj"].reshape(E_, D)
    swap = np.arange(D) ^ 1
    d["a1_wq"], d["a1_wqs"] = a["L1_attn_wq"], a["L1_attn_wq"][:, swap]
    d["a1_wk"], d["a1_wks"] = a["L1_attn_wk_up"], a["L1_attn_wk_up"][:, swap]
    d["a1_wd"], d["a1_wv"], d["a1_wo"] = a["L1_attn_w_down"], a["L1_attn_wv_up"], a["L1_attn_wo"]
    for l in range(2):
        g = lambda n: a["L1_ffn_" + n][l]
        d[f"l{l}_wqkv"], d[f"l{l}_wo"], d[f"l{l}_w1"], d[f"l{l}_w2"] = g("wqkv"), g("wo"), g("w1"), g("w2")
        d[f"l{l}_scales"] = np.concatenate([g("q_scale"), g("k_scale")]).reshape(1, 2 * LD)
        d[f"l{l}_lng"], d[f"l{l}_lnb"] = cols(g("ln_g")), cols(g("ln_b"))
        b1 = np.zeros((2, FT * P), np.float32)
        b1[:, :HIDF] = g("b1").reshape(2, HIDF)
        d[f"l{l}_b1a"], d[f"l{l}_b1g"] = cols(b1[0]), cols(b1[1])
        d[f"l{l}_b2"] = g("b2").reshape(1, D)
    return d


def kernel(**inputs):
    import concourse.bacc as bacc
    from concourse.bass_utils import run_bass_kernel_spmd

    nc = bacc.Bacc("TRN2", target_bir_lowering=False, num_devices=1)
    arrays = {f"in_{k}": np.ascontiguousarray(v) for k, v in {**laid_out(inputs), **shape_constants()}.items()}
    d = {k[3:]: nc.dram_tensor(k, v.shape, mybir.dt.from_np(v.dtype), kind="ExternalInput").ap()
         for k, v in arrays.items()}
    out = nc.dram_tensor("out_0", (TOK, D), F32, kind="ExternalOutput").ap()
    build(nc, d, out)
    r = run_bass_kernel_spmd(nc, [arrays], core_ids=[0])
    return r.results[0]["out_0"].reshape(B, S, D)
```

```python
from contextlib import ExitStack

import numpy as np
import concourse.bass as bass
from concourse import mybir

F32 = mybir.dt.float32
F32R = mybir.dt.float32r
BF16 = mybir.dt.bfloat16
U32 = mybir.dt.uint32
ALU = mybir.AluOpType
ACT = mybir.ActivationFunctionType
AX = mybir.AxisListType.X
ds = bass.ds

P = 128
B, S, D = 2, 2048, 256
TOK = B * S
NT = TOK // P
KC = D // P
CH = 512
CPB = S // CH
SUB = CH // P
NH, HD = 16, 16
GRP = 4
NG = NH // GRP
NIT = B * NG
NKV = 4
VW = 2 * HD
PAGE = 64
NEG = -1e30
EPS = 1e-5


class Semaphores:

    def __init__(self, nc):
        self.nc, self.taken, self.new = nc, [], []

    def __call__(self, name, first=1):
        s = self.nc.alloc_semaphore(name)
        self.new.append((s, first))
        return s

    def start(self):
        for s, first in self.new:
            if first:
                self.nc.gpsimd.sem_inc(s, first)
            self.taken.append(s)
        self.nc.all_engine_barrier()
        self.new = []

    def clear(self):
        self.nc.all_engine_barrier()
        self.nc.clear_and_free_semaphores(self.taken)
        self.nc.all_engine_barrier()
        self.taken = []


def wait_apart(eng, semaphore, value, fence):
    eng.wait_ge(semaphore, value + 1)
    eng.sem_inc(fence, 1)


def layer0_projections(nc, sem, xT, wqT, wkT, wvT, qh, ql, kh, kl, vs):
    NKD = NKV * HD
    STORES = 2 * KC + 2 + SUB
    with ExitStack() as ctx:
        sb = lambda n, s, t: ctx.enter_context(nc.sbuf_tensor("A_" + n, s, t))
        x = sb("x", [P, 2, KC, CH], F32)
        wq = sb("wq", [P, KC, D], F32)
        wk = sb("wk", [P, KC, NKD], F32)
        wv = sb("wv", [P, KC, NKD], F32)
        qhi = sb("qhi", [P, 2, KC, CH], F32R)
        qlo = sb("qlo", [P, 2, KC, CH], F32R)
        khi = sb("khi", [NKD, 2, CH], F32R)
        klo = sb("klo", [NKD, 2, CH], F32R)
        v = sb("v", [P, 2, SUB, NKV, VW], F32)
        bank = [ctx.enter_context(nc.psum_tensor(f"A_b{i}", [P, CH], F32)) for i in range(8)]
        w_in, x_in = sem("A_w_in", 0), [sem(f"A_x_in{u}", 0) for u in range(2)]
        x_used, banks_used = sem("A_x_used"), sem("A_banks_used")
        stored = [sem(f"A_stored{u}") for u in range(2)]
        fence = sem("A_fence")
        mm_done, hi_done, lo_done, ones_set = sem("A_mm"), sem("A_hi"), sem("A_lo"), sem("A_ones")
        sem.start()
        block = ctx.enter_context(nc.Block())
        xT_v = xT.rearrange("(kc p) t -> p kc t", p=P)

        @block.gpsimd
        def _(pool):
            for w, src in ((wq, wqT), (wk, wkT), (wv, wvT)):
                pool.dma_start(w[:], src.rearrange("(kc p) n -> p kc n", p=P)).then_inc(w_in, 16)
            with pool.Fori(0, TOK // CH // 2) as pair:
                for u in range(2):
                    wait_apart(pool, x_used, pair * 2 + u + 1, fence)
                    pool.dma_start(x[:, u], xT_v[:, :, ds(pair * (2 * CH) + u * CH, CH)]).then_inc(x_in[u], 16)

        @block.tensor
        def _(pe):
            pe.sem_inc(x_used, 2)
            pe.wait_ge(w_in, 48)
            with pe.Fori(0, TOK // CH // 2) as pair:
                for u in range(2):
                    n = pair * 2 + u
                    pe.wait_ge(x_in[u], pair * 16 + 16)
                    pe.wait_ge(banks_used, n + 2)
                    for m in range(KC):
                        for c in range(KC):
                            pe.matmul(bank[4 * u + m][:], wq[:, c, m * P:(m + 1) * P], x[:, u, c],
                                      start=c == 0, stop=c == KC - 1)
                    for c in range(KC):
                        pe.matmul(bank[4 * u + 2][0:NKD], wk[:, c], x[:, u, c], start=c == 0, stop=c == KC - 1)
                    for s in range(SUB):
                        for c in range(KC):
                            last = pe.matmul(bank[4 * u + 3][:, s * NKD:(s + 1) * NKD], x[:, u, c, s * P:(s + 1) * P],
                                             wv[:, c], start=c == 0, stop=c == KC - 1)
                    last.then_inc(mm_done, 1)
                    pe.drain().then_inc(x_used, 1)

        @block.scalar
        def _(act):
            act.wait_ge(ones_set, 2)
            with act.Fori(0, TOK // CH // 2) as pair:
                for u in range(2):
                    n = pair * 2 + u
                    act.wait_ge(mm_done, n + 2)
                    act.wait_ge(stored[u], pair * (16 * STORES) + 1)
                    for s in range(SUB):
                        act.activation(v[:, u, s, :, 0:HD],
                                       bank[4 * u + 3][:, s * NKD:(s + 1) * NKD].rearrange("p (g e) -> p g e", e=HD),
                                       ACT.Copy)
                    act.activation(khi[:, u], bank[4 * u + 2][0:NKD], ACT.Copy)
                    for m in range(KC):
                        last = act.activation(qhi[:, u, m], bank[4 * u + m][:], ACT.Copy)
                    last.then_inc(hi_done, 1)

        @block.vector
        def _(dve):
            dve.sem_inc(banks_used, 2)
            dve.memset(v[:], 1.0).then_inc(ones_set, 1)
            with dve.Fori(0, TOK // CH // 2) as pair:
                for u in range(2):
                    n = pair * 2 + u
                    dve.wait_ge(hi_done, n + 2)
                    dve.tensor_tensor(klo[:, u], bank[4 * u + 2][0:NKD], khi[:, u].bitcast(F32), ALU.subtract)
                    for m in range(KC):
                        last = dve.tensor_tensor(qlo[:, u, m], bank[4 * u + m][:], qhi[:, u, m].bitcast(F32),
                                                 ALU.subtract)
                    last.then_inc(lo_done, 1)
                    dve.drain().then_inc(banks_used, 1)

        @block.sync
        def _(sp):
            with sp.Fori(0, B) as b:
                with sp.Fori(0, CPB // 2) as pair:
                    for u in range(2):
                        n = b * CPB + pair * 2 + u
                        col = pair * (2 * CH) + u * CH
                        sp.wait_ge(lo_done, n + 2)
                        for m in range(KC):
                            for dst, src in ((qh, qhi), (ql, qlo)):
                                sp.dma_start(dst[ds(b * D + m * P, P), ds(col, CH)], src[:, u, m].bitcast(F32)).then_inc(stored[u], 16)
                        for dst, src in ((kh, khi), (kl, klo)):
                            sp.dma_start(dst[ds(b * NKD, NKD), ds(col, CH)], src[:, u].bitcast(F32)).then_inc(stored[u], 16)
                        vs_v = vs.rearrange("(bb g t) e -> bb t g e", bb=B, g=NG)
                        for s in range(SUB):
                            sp.dma_start(vs_v[ds(b, 1), ds(col + s * P, P)].rearrange("o t g e -> (o t) g e"),
                                         v[:, u, s]).then_inc(stored[u], 16)
            for u in range(2):
                sp.wait_ge(stored[u], 16 * STORES * (TOK // CH // 2) + 1)


def attention(nc, sem, tag, nk, page, qh, ql, kh, kl, vs, mask_qk, ident_bf, ident, m_rows, ot):
    R = 4 * HD
    MR = 96
    NQ = S // P
    SC = 1.0 / HD ** 0.5

    pieces = []
    for qb in range(NQ):
        full, rest = divmod((qb + 1) * P, CH)
        for kc in range(full):
            pieces += [(qb, kc, CH, [h]) for h in range(GRP)]
        if rest:
            per = CH // rest
            pieces += [(qb, full, rest, list(range(h, h + per))) for h in range(0, GRP, per)]
    NP = len(pieces)
    steps = [(qc, kb) for qc in range(NQ * P // CH) for kb in range(SUB * (qc + 1))]
    NS = len(steps)
    cut = [NP * i // NS for i in range(NS + 1)]

    with ExitStack() as ctx:
        sb = lambda n, s, t: ctx.enter_context(nc.sbuf_tensor(tag + n, s, t))
        qs = [sb(f"qs{i}", [P, GRP, S], F32R) for i in range(2)]
        ks = [sb(f"ks{i}", [P, nk, S], F32R) for i in range(2)]
        v = [sb(f"v{i}", [P, NQ, nk, VW], F32) for i in range(2)]
        p = sb("p", [P, 2, GRP, CH], F32)
        o = sb("o", [P, 2, CH], F32)
        mpart = sb("mpart", [P, GRP, NQ, 4], F32)
        m = sb("m", [P, P], F32)
        mhi = sb("mhi", [GRP * NQ, P], F32R)
        mlo = sb("mlo", [GRP * NQ, P], F32R)
        mqk = sb("mqk", [P, P], BF16)
        idb = sb("idb", [P, P], BF16)
        idf = sb("idf", [P, P], F32)
        psc = ctx.enter_context(nc.psum_tensor(tag + "psc", [P, GRP, CH], F32))
        po = [ctx.enter_context(nc.psum_tensor(f"{tag}po{i}", [P, CH], F32)) for i in range(2)]
        pm = [ctx.enter_context(nc.psum_tensor(f"{tag}pm{i}", [P, CH], F32)) for i in range(2)]
        c_in, ready = sem(tag + "c_in", 0), sem(tag + "ready")
        q_in, ld_free = [sem(f"{tag}q_in{i}", 0) for i in range(2)], sem(tag + "ld_free")
        s_max, max_done = sem(tag + "s_max"), sem(tag + "max_done")
        m_all, mt_done = sem(tag + "m_all"), sem(tag + "mt_done")
        mh_done, ml_done = sem(tag + "mh_done"), sem(tag + "ml_done")
        m_out, m_in, fence = sem(tag + "m_out"), sem(tag + "m_in"), sem(tag + "fence")
        s_done, pv_done = sem(tag + "s_done"), sem(tag + "pv_done")
        e_done = [sem(f"{tag}e_done{i}") for i in range(2)]
        cleared = sem(tag + "cleared")
        o_done, o_out = sem(tag + "o_done"), [sem(f"{tag}o_out{i}") for i in range(2)]
        sem.start()
        block = ctx.enter_context(nc.Block())

        def masked(t):
            return sum(kb >= SUB * qc for qc, kb in steps[:t])

        LOADS = 8 + 1
        NC4 = S // CH

        @block.gpsimd
        def _(pool):
            for dst, src in ((mqk, mask_qk), (idb, ident_bf)):
                pool.dma_start(dst[:], src).then_inc(c_in, 16)
            pool.dma_start(idf[:], ident).then_inc(c_in, 16)

            def load(i, s):
                for r, (a, c) in enumerate(((qh, kh), (qh, kl), (ql, kh), (ql, kl))):
                    pool.dma_start(qs[s][r * HD:(r + 1) * HD, :, :].bitcast(F32),
                                   a[ds(i * (GRP * HD), GRP * HD), :].rearrange("(h e) t -> e h t", e=HD)
                                   ).then_inc(q_in[s], 16)
                    pool.dma_start(ks[s][r * HD:(r + 1) * HD, :, :].bitcast(F32),
                                   c[ds(i * (nk * HD), nk * HD), :].rearrange("(h e) t -> e h t", e=HD)
                                   ).then_inc(q_in[s], 16)
                pool.dma_start(v[s][:], vs[ds(i * S, S), :].rearrange("(kb p) (h e) -> p kb h e", p=P, e=VW)
                               ).then_inc(q_in[s], 16)

            def clear(i):
                for t, (qc, kb) in enumerate(steps):
                    if kb < SUB * qc:
                        continue
                    off = (kb - SUB * qc) * P
                    for pr in range(2):
                        wait_apart(pool, e_done[pr], i * NS + t + 1, fence)
                    if page == 1:
                        tile = p[:, t % 2, :, off:off + P]
                        pool.affine_select(out=tile, in_=tile, pattern=[[0, GRP], [1, P]], compare_op=ALU.is_ge,
                                           fill=0.0, base=0, channel_multiplier=-1).then_inc(cleared, 1)
                    else:
                        for k in range(page, P, page):
                            last = pool.memset(p[k:k + page, t % 2, :, off:off + k], 0.0)
                        last.then_inc(cleared, 1)

            load(0, 0)
            load(1, 1)
            with pool.Fori(0, NIT // 2 - 1) as pair:
                for s in range(2):
                    clear(pair * 2 + s)
                    wait_apart(pool, ld_free, pair * 2 + s + 1, fence)
                    load(pair * 2 + s + 2, s)
            clear(NIT - 2)
            clear(NIT - 1)

        @block.sync
        def _(sp):
            def m_step(i, s):
                sp.wait_ge(ml_done, i + 2)
                sp.dma_start(m_rows[0:1].rearrange("o (a t) -> (o a) t", t=P), mhi[:].bitcast(F32)).then_inc(m_out, 16)
                sp.dma_start(m_rows[1:2].rearrange("o (a t) -> (o a) t", t=P), mlo[:].bitcast(F32)).then_inc(m_out, 16)
                sp.wait_ge(m_out, (i + 1) * 32 + 1)
                sp.dma_start(qs[s][MR:MR + 2, :, :].bitcast(F32).rearrange("r h t -> r (h t)"), m_rows).then_inc(m_in, 16)

            def outs(i):
                for c in range(NC4):
                    sp.wait_ge(o_done, i * NC4 + c + 3)
                    sp.dma_start(ot[ds(i * P, P), c * CH:(c + 1) * CH], o[:, c % 2]).then_inc(o_out[c % 2], 16)

            m_step(0, 0)
            with sp.Fori(0, NIT // 2 - 1) as pair:
                for s in range(2):
                    outs(pair * 2 + s)
                    m_step(pair * 2 + s + 1, (s + 1) % 2)
            outs(NIT - 2)
            m_step(NIT - 1, 1)
            outs(NIT - 1)
            for c in range(2):
                sp.wait_ge(o_out[c], 16 * (NC4 // 2 * NIT) + 1)

        @block.tensor
        def _(pe):
            def maxima(i, s, a, z):
                for j in range(a, z):
                    qb, kc, w, heads = pieces[j]
                    t = pm[j % 2]
                    pe.wait_ge(max_done, i * NP + j + 2)
                    diag = kc * CH + w == (qb + 1) * P
                    for n, h in enumerate(heads):
                        last = pe.matmul(t[:, n * w:(n + 1) * w], qs[s][0:MR, h, qb * P:(qb + 1) * P],
                                         ks[s][0:MR, h % nk, kc * CH:kc * CH + w], start=True, stop=True)
                    if diag:
                        c = len(heads)
                        last = pe.matmul(t[:, 0:c * w].rearrange("p (h k) -> p h k", k=w)[:, :, w - P:w], idb[:],
                                         mqk[:].unsqueeze(1).to_broadcast([P, c, P]), start=False, stop=True,
                                         skip_group_check=True)
                    last.then_inc(s_max, 1)

            def turn(i):
                pe.wait_ge(m_all, i + 2)
                pe.transpose(pm[0][:, 0:P], m[:], idf[:]).then_inc(mt_done, 1)

            def weigh(i, s, t):
                qc, kb = steps[t]
                off = max(0, kb - SUB * qc) * P
                if kb >= SUB * qc:
                    pe.wait_ge(cleared, i * NQ + masked(t) + 2)
                for pr in range(2):
                    pe.wait_ge(e_done[pr], i * NS + t + 2)
                if kb == 0:
                    pe.wait_ge(o_done, i * NC4 + qc + 1)
                for h in range(GRP):
                    last = pe.matmul(po[qc % 2][VW * h:VW * (h + 1), off:CH], v[s][:, kb, h % nk],
                                     p[:, t % 2, h, off:CH], start=kb == 0, stop=kb == SUB * (qc + 1) - 1,
                                     skip_group_check=True)
                last.then_inc(pv_done, 1)

            def step(i, s, nxt):
                pe.wait_ge(m_in, (i + 1) * 16 + 1)
                for t, (qc, kb) in enumerate(steps):
                    diag = kb - SUB * qc
                    off = max(0, diag) * P
                    a, z = (cut[t], cut[t + 1]) if nxt else (0, 0)
                    spread = [a, min(a + 1, z), min(a + 2, z), z]
                    for pr in range(2):
                        pe.wait_ge(e_done[pr], i * NS + t + 1)
                        for h in (2 * pr, 2 * pr + 1):
                            last = pe.matmul(psc[:, h, off:CH], ks[s][:, h % nk, kb * P:(kb + 1) * P],
                                             qs[s][:, h, qc * CH + off:(qc + 1) * CH],
                                             start=True, stop=True)
                        last.then_inc(s_done, 1)
                        maxima(i + 1, 1 - s, spread[pr], spread[pr + 1])
                    if t:
                        weigh(i, s, t - 1)
                    maxima(i + 1, 1 - s, spread[2], spread[3])
                weigh(i, s, NS - 1)
                pe.drain().then_inc(ld_free, 1)
                if nxt:
                    turn(i + 1)

            pe.wait_ge(c_in, 48)
            pe.wait_ge(ready, 2)
            pe.wait_ge(q_in[0], 16 * LOADS)
            maxima(0, 0, 0, NP)
            turn(0)
            with pe.Fori(0, NIT // 2 - 1) as pair:
                for s in range(2):
                    pe.wait_ge(q_in[1 - s], (pair + s + 1) * (16 * LOADS))
                    step(pair * 2 + s, s, True)
            pe.wait_ge(q_in[1], NIT // 2 * 16 * LOADS)
            step(NIT - 2, 0, True)
            step(NIT - 1, 1, False)

        @block.scalar
        def _(act):
            def m_hi(i):
                act.wait_ge(mt_done, i + 2)
                act.wait_ge(m_in, i * 16 + 1)
                act.activation(mhi[:], pm[0][0:GRP * NQ, 0:P], ACT.Copy, scale=-1.0).then_inc(mh_done, 1)

            def step(i):
                for t, (qc, kb) in enumerate(steps):
                    off = max(0, kb - SUB * qc) * P
                    for pr in range(2):
                        act.wait_ge(s_done, (i * NS + t) * 2 + pr + 2)
                        act.wait_ge(pv_done, i * NS + t + 2)
                        act.activation(p[:, t % 2, 2 * pr:2 * pr + 2, off:CH], psc[:, 2 * pr:2 * pr + 2, off:CH],
                                       ACT.Exp, scale=SC).then_inc(e_done[pr], 1)

            m_hi(0)
            with act.Fori(0, NIT // 2 - 1) as pair:
                for s in range(2):
                    step(pair * 2 + s)
                    m_hi(pair * 2 + s + 1)
            step(NIT - 2)
            m_hi(NIT - 1)
            step(NIT - 1)

        @block.vector
        def _(dve):
            def maxima(i, a, z):
                for j in range(a, z):
                    qb, kc, w, heads = pieces[j]
                    dve.wait_ge(s_max, i * NP + j + 2)
                    dve.tensor_reduce(mpart[:, heads[0]:heads[-1] + 1, qb, kc],
                                      pm[j % 2][:, 0:len(heads) * w].rearrange("p (h k) -> p h k", k=w),
                                      AX, ALU.max).then_inc(max_done, 1)

            def fold(i):
                dve.wait_ge(max_done, (i + 1) * NP + 3)
                dve.wait_ge(mt_done, i + 1)
                dve.tensor_reduce(m[:, 0:GRP * NQ], mpart[:].rearrange("p h q k -> p (h q) k"), AX, ALU.max).then_inc(m_all, 1)

            def m_lo(i):
                dve.wait_ge(mh_done, i + 2)
                dve.scalar_tensor_tensor(mlo[:], pm[0][0:GRP * NQ, 0:P], -1.0, mhi[:].bitcast(F32),
                                         ALU.mult, ALU.subtract).then_inc(ml_done, 1)

            def copy_out(i, qc):
                dve.wait_ge(pv_done, i * NS + 2 + sum(SUB * (c + 1) for c in range(qc + 1)) + 1)
                dve.wait_ge(o_out[qc % 2], i * (NC4 // 2 * 16) + qc // 2 * 16 + 1)
                dve.tensor_copy(o[:, qc % 2], po[qc % 2][:]).then_inc(o_done, 1)

            def step(i, nxt):
                for t, (qc, kb) in enumerate(steps):
                    if nxt:
                        maxima(i + 1, cut[t], cut[t + 1])
                    if kb == 0 and qc:
                        copy_out(i, qc - 1)
                copy_out(i, NC4 - 1)
                if nxt:
                    fold(i + 1)
                    m_lo(i + 1)

            dve.sem_inc(max_done, 2)
            dve.sem_inc(o_done, 1)
            dve.sem_inc(pv_done, 2)
            dve.memset(mpart[:], -3e38)
            dve.memset(m[:], 0.0)
            for s in range(2):
                dve.memset(qs[s][R:P].bitcast(F32), 0.0)
                last = dve.memset(ks[s][R:P].bitcast(F32), 1.0)
            last.then_inc(ready, 1)
            maxima(0, 0, NP)
            fold(0)
            m_lo(0)
            with dve.Fori(0, NIT // 2 - 1) as pair:
                for s in range(2):
                    step(pair * 2 + s, True)
            step(NIT - 2, True)
            step(NIT - 1, False)


E_, HID_E = 8, 1024
TOPK = 2
CAP = int(1.2 * TOPK * S // E_)
ROWS = B * CAP


class Chain:

    def __init__(self, eng, semaphore, per):
        self.eng, self.sem, self.per, self.n, self.base = eng, semaphore, per, 0, 0

    def start(self, i):
        self.base, self.n = i * self.per, 0

    def link(self, ins):
        self.n += 1
        ins.then_inc(self.sem, 1)
        self.eng.wait_ge(self.sem, self.base + self.n + 1)

    def end(self):
        assert self.n == self.per, self.n


def attention_output(nc, sem, tag, ot, woT, x_src, X, ident, router, xp, inverse):
    with ExitStack() as ctx:
        sb = lambda n, s, t: ctx.enter_context(nc.sbuf_tensor(tag + n, s, t))
        num = sb("num", [P, 2, KC, CH], F32)
        den = sb("den", [P, 2, KC, CH], F32)
        sums = sb("sums", [P, CH], F32)
        inv = sb("inv", [P, CH], F32)
        cx = sb("cx", [P, 2, KC, CH], F32)
        wo = sb("wo", [P, KC, D], F32)
        y = sb("y", [P, SUB, D], F32)
        xn = sb("xn", [P, SUB, D], F32)
        xnT = sb("xnT", [P, KC, CH], F32)
        st = sb("st", [P, SUB, 6], F32)
        mv = sb("mv", [P, SUB, 2], F32)
        sd = sb("sd", [P, SUB], F32)
        rs = sb("rs", [P, SUB], F32)
        eps = sb("eps", [P, 1], F32)
        idf = sb("idf", [P, P], F32)
        rw = sb("rw", [P, KC, E_], F32)
        rb = sb("rb", [P, E_], F32)
        pb = [ctx.enter_context(nc.psum_tensor(f"{tag}pb{i}", [P, CH], F32)) for i in range(5)]
        w_in, a_in = sem(tag + "w_in", 0), [sem(f"{tag}a_in{u}", 0) for u in range(2)]
        c_ready, mm_done = sem(tag + "c_ready"), sem(tag + "mm_done")
        var_done, sd_done, n_done = sem(tag + "var"), sem(tag + "sd"), sem(tag + "n_done")
        t_done, xt_done, lg_done = sem(tag + "t"), sem(tag + "xt"), sem(tag + "lg")
        x_copied, st_done, dch, fence = sem(tag + "xc"), sem(tag + "st"), sem(tag + "dch"), sem(tag + "fence")
        lg_kept = sem(tag + "lgk")
        eps_set, sums_in, inv_done, inv_out = sem(tag + "eps"), sem(tag + "si", 0), sem(tag + "id"), sem(tag + "io")
        sem.start()
        block = ctx.enter_context(nc.Block())
        wcount = 2 + (2 if router else 0) + (1 if x_src is not None else 0)

        def chunks(eng, body):
            with eng.Fori(0, B) as b:
                with eng.Fori(0, CPB // 2) as pair:
                    for u in range(2):
                        body(b * CPB + pair * 2 + u, b, pair, u)

        def skewed(eng, first, second, swapped=False):
            def both(n, *nxt):
                if swapped:
                    second(n)
                first(n + 1, *nxt)
                if not swapped:
                    second(n)

            last = CPB // 2 - 1
            first(0, 0, 0, 0)
            for b in range(B):
                with eng.Fori(0, last) as pair:
                    for u in range(2):
                        both(b * CPB + pair * 2 + u, b, pair + u, 1 - u)
                n = b * CPB + last * 2
                both(n, b, last, 1)
                if b < B - 1:
                    both(n + 1, b + 1, 0, 0)
            second(NT // SUB - 1)

        @block.gpsimd
        def _(pool):
            pool.dma_start(wo[:], woT.rearrange("(kc p) n -> p kc n", p=P)).then_inc(w_in, 16)
            pool.dma_start(idf[:], ident).then_inc(w_in, 16)
            pool.memset(eps[:], EPS).then_inc(eps_set, 1)
            if router:
                pool.dma_start(rw[:], router[0].rearrange("(kc p) n -> p kc n", p=P)).then_inc(w_in, 16)
                pool.dma_start(rb[:], router[1]).then_inc(w_in, 16)
            if x_src is not None:
                pool.dma_start(X[:], x_src.rearrange("(t p) c -> p t c", p=P)).then_inc(w_in, 16)

            pool.sem_inc(c_ready, 1)

            def body(n, b, pair, u):
                wait_apart(pool, a_in[u], b * (CPB // 2 * 64) + pair * 64 + 63, fence)
                wait_apart(pool, mm_done, n, fence)
                pool.tensor_tensor(cx[:, u], num[:, u], den[:, u], ALU.mult).then_inc(c_ready, 1)
            chunks(pool, body)

        @block.tensor
        def _(pe):
            pe.wait_ge(w_in, wcount * 16)

            def body(n, b, pair, u):
                pe.wait_ge(c_ready, n + 3)
                pe.wait_ge(var_done, n + 1)
                for s in range(SUB):
                    for c in range(KC):
                        last = pe.matmul(pb[s // 2][:, s % 2 * D:(s % 2 + 1) * D], cx[:, u, c, s * P:(s + 1) * P],
                                         wo[:, c], start=c == 0, stop=c == KC - 1)
                last.then_inc(mm_done, 1)

            def logits(n):
                if router:
                    pe.wait_ge(n_done, n + 2)
                    for c in range(KC):
                        for s in range(SUB):
                            last = pe.transpose(pb[2 + c][:, s * P:(s + 1) * P], xn[:, s, c * P:(c + 1) * P], idf[:])
                    last.then_inc(t_done, 1)
                    pe.wait_ge(xt_done, n + 2)
                    pe.wait_ge(lg_kept, n + 1)
                    for s in range(SUB):
                        for c in range(KC):
                            last = pe.matmul(pb[4][:, s * E_:(s + 1) * E_], xnT[:, c, s * P:(s + 1) * P], rw[:, c],
                                             start=c == 0, stop=c == KC - 1)
                    last.then_inc(lg_done, 1)
            skewed(pe, body, logits)

        @block.scalar
        def _(act):
            act.wait_ge(eps_set, 2)

            def body(n, b, pair, u):
                act.wait_ge(var_done, n + 2)
                act.activation(sd[:], mv[:, :, 1], ACT.Sqrt, bias=eps[:]).then_inc(sd_done, 1)
                act.wait_ge(n_done, n + 2)
                if xp is not None:
                    for s in range(SUB):
                        act.dma_start(xp[ds(b * (S + 1) + pair * (2 * CH) + u * CH + s * P + 1, P), :], xn[:, s]
                                      ).then_inc(st_done, 16)
                act.activation(X[:, ds(n * SUB, SUB), :], xn[:], ACT.Copy).then_inc(x_copied, 1)

            def turned(n):
                if router:
                    act.wait_ge(t_done, n + 2)
                    for c in range(KC):
                        last = act.activation(xnT[:, c], pb[2 + c][:], ACT.Copy)
                    last.then_inc(xt_done, 1)
            skewed(act, body, turned, swapped=True)

        @block.vector
        def _(dve):
            ch = Chain(dve, dch, 4 + SUB - 1)
            dve.wait_ge(sums_in, 16)
            dve.reciprocal(inv[:], sums[:]).then_inc(inv_done, 1)
            dve.wait_ge(w_in, wcount * 16)
            def body(n, b, pair, u):
                ch.start(n)
                dve.wait_ge(mm_done, n + 2)
                for k in range(2):
                    last = dve.tensor_tensor(y[:, 2 * k:2 * k + 2], pb[k][:].rearrange("p (s c) -> p s c", c=D),
                                             X[:, ds(n * SUB + 2 * k, 2), :], ALU.add)
                    ch.link(last)
                for s in range(SUB):
                    last = dve.bn_stats(st[:, s], y[:, s])
                ch.link(last)
                dve.sem_inc(fence, 1)
                for s in range(SUB):
                    last = dve.bn_aggr(mv[:, s], st[:, s])
                last.then_inc(var_done, 1)
                dve.wait_ge(sd_done, n + 2)
                ch.link(dve.reciprocal(rs[:], sd[:]))
                dve.wait_ge(x_copied, n + 1)
                if router:
                    dve.wait_ge(t_done, n + 1)
                if xp is not None:
                    dve.wait_ge(st_done, n * (16 * SUB) + 1)
                for s in range(SUB):
                    last = dve.tensor_scalar(xn[:, s], y[:, s], mv[:, s, 0:1], rs[:, s:s + 1], ALU.subtract, ALU.mult)
                    if s == SUB - 1:
                        last.then_inc(n_done, 1)
                    else:
                        ch.link(last)
                ch.end()

            def keep_logits(n):
                if router:
                    dve.wait_ge(lg_done, n + 2)
                    dve.tensor_tensor(router[2][:, ds(n * SUB, SUB), :],
                                      pb[4][:, 0:SUB * E_].rearrange("p (s e) -> p s e", e=E_),
                                      rb[:].unsqueeze(1).to_broadcast([P, SUB, E_]), ALU.add).then_inc(lg_kept, 1)
            skewed(dve, body, keep_logits)
            dve.wait_ge(x_copied, TOK // CH + 1)

        @block.sync
        def _(sp):
            def body(n, b, pair, u):
                sp.wait_ge(c_ready, n + 1)
                for m in range(KC):
                    cols = ds(pair * (2 * CH) + u * CH, CH)
                    o = ot[ds(b * (NH * VW) + m * (NH * VW // KC), NH * VW // KC), cols].rearrange(
                        "(h r) t -> h r t", r=VW)
                    sp.dma_start(num[:, u, m], o[:, 0:HD]).then_inc(a_in[u], 16)
                    sp.dma_start(den[:, u, m], inverse[ds(b * NH + m * (NH // KC), NH // KC), cols].unsqueeze(1)
                                 .to_broadcast([NH // KC, HD, CH])).then_inc(a_in[u], 16)

            heads = ot.rearrange("(g r) t -> g r t", r=VW)[:, HD]
            sp.dma_start(sums[:], heads.rearrange("g (q t) -> g q t", t=CH)).then_inc(sums_in, 16)
            sp.wait_ge(inv_done, 2)
            sp.dma_start(inverse.rearrange("g (q t) -> g q t", t=CH), inv[:]).then_inc(inv_out, 16)
            sp.wait_ge(inv_out, 17)
            chunks(sp, body)
            if xp is not None:
                sp.wait_ge(st_done, 16 * SUB * (TOK // CH) + 1)


def route(nc, sem, LG, tri, iota8, ones, slot_s, slot_g, prob):
    NK = TOPK
    QT = S // P
    SEQ = NK * QT
    with ExitStack() as ctx:
        sb = lambda n, s, t: ctx.enter_context(nc.sbuf_tensor("D_" + n, s, t))
        m8 = sb("m8", [P, NT, 8], F32)
        i8 = sb("i8", [P, NT, 8], U32)
        ixf = sb("ixf", [P, NK, NT], F32)
        oh = sb("oh", [P, B, NK, QT, E_], F32)
        trs = sb("trs", [P, P], F32)
        on = sb("on", [P, P], F32)
        io = sb("io", [P, E_], F32)
        ca = sb("ca", [P, B, SEQ, E_], F32)
        cb = sb("cb", [P, B, SEQ, E_], F32)
        pos = sb("pos", [P, B, SEQ, E_], F32)
        pf = sb("pf", [P, B, NK, QT], F32)
        base = sb("base", [P, B, NK, QT], F32)
        of = sb("of", [P, B, NK, QT], F32)
        g = sb("g", [P, B, NK, QT], F32)
        dif = sb("dif", [P, NT], F32)
        e2 = sb("e2", [P, NT], F32)
        den = sb("den", [P, NT], F32)
        pc = ctx.enter_context(nc.psum_tensor("D_pc", [P, CH], F32))
        pt = ctx.enter_context(nc.psum_tensor("D_pt", [P, CH], F32))
        c_in, dch, oh_done, cum_done = sem("D_c_in", 0), sem("D_dch"), sem("D_oh"), sem("D_cum")
        dif_done, e2_done = sem("D_dif"), sem("D_e2")
        sem.start()
        block = ctx.enter_context(nc.Block())

        @block.sync
        def _(sp):
            for dst, src in ((trs, tri), (on, ones), (io, iota8)):
                sp.dma_start(dst[:], src).then_inc(c_in, 16)

        @block.tensor
        def _(pe):
            pe.wait_ge(c_in, 48)
            pe.wait_ge(oh_done, 2)
            flat = oh[:].rearrange("p b k t e -> p (b k t e)")
            pe.matmul(pc[:], trs[:], flat, start=True, stop=True)
            pe.matmul(pt[:], on[:], flat, start=True, stop=True).then_inc(cum_done, 1)

        @block.scalar
        def _(act):
            act.wait_ge(dif_done, 2)
            act.activation(e2[:], dif[:], ACT.Exp).then_inc(e2_done, 1)

        @block.vector
        def _(dve):
            n = [0]

            def link(ins):
                n[0] += 1
                ins.then_inc(dch, 1)
                dve.wait_ge(dch, n[0] + 1)

            dve.wait_ge(c_in, 48)
            for t in range(NT):
                last = dve.max(m8[:, t], LG[:, t])
            link(last)
            for t in range(NT):
                last = dve.max_index(i8[:, t], m8[:, t], LG[:, t])
            link(last)
            dve.tensor_tensor(dif[:], m8[:, :, 1], m8[:, :, 0], ALU.subtract).then_inc(dif_done, 1)
            for k in range(NK):
                last = dve.tensor_copy(ixf[:, k], i8[:, :, k])
            link(last)
            for b in range(B):
                for k in range(NK):
                    last = dve.tensor_tensor(
                        oh[:, b, k], io[:].unsqueeze(1).to_broadcast([P, QT, E_]),
                        ixf[:, k, b * QT:(b + 1) * QT].unsqueeze(2).to_broadcast([P, QT, E_]), ALU.is_equal)
            last.then_inc(oh_done, 1)
            dve.wait_ge(cum_done, 2)
            tot = pt[:].rearrange("p (b s e) -> p b s e", b=B, e=E_)
            link(dve.memset(ca[:, :, 0:1], 0.0))
            link(dve.tensor_copy(ca[:, :, 1:SEQ], tot[:, :, 0:SEQ - 1]))
            a, c, step = ca, cb, 1
            while step < SEQ:
                dve.tensor_copy(c[:, :, 0:step], a[:, :, 0:step])
                link(dve.tensor_tensor(c[:, :, step:SEQ], a[:, :, step:SEQ], a[:, :, 0:SEQ - step], ALU.add))
                a, c, step = c, a, step * 2
            link(dve.tensor_tensor(pos[:], pc[:].rearrange("p (b s e) -> p b s e", b=B, e=E_), a[:], ALU.add))
            link(dve.tensor_tensor(c[:], pos[:], oh[:].rearrange("p b k t e -> p b (k t) e"), ALU.mult))
            link(dve.tensor_reduce(pf[:].rearrange("p b k t -> p b (k t)"), c[:], AX, ALU.add))
            for b in range(B):
                for k in range(NK):
                    last = dve.tensor_scalar(base[:, b, k], ixf[:, k, b * QT:(b + 1) * QT], float(ROWS),
                                             float(b * CAP - 1), ALU.mult, ALU.add)
            link(last)
            link(dve.tensor_scalar(of[:], pf[:], float(CAP), float(E_ * ROWS), ALU.is_gt, ALU.mult))
            link(dve.tensor_scalar(g[:], pf[:], float(CAP), None, ALU.min))
            link(dve.tensor_tensor(of[:], of[:], pf[:], ALU.add))
            dve.tensor_tensor(slot_s[:], of[:], base[:], ALU.add)
            dve.tensor_tensor(slot_g[:], g[:], base[:], ALU.add)
            dve.wait_ge(e2_done, 2)
            link(dve.tensor_scalar(den[:], e2[:], 1.0, None, ALU.add))
            link(dve.reciprocal(prob[:, 0], den[:]))
            link(dve.tensor_tensor(prob[:, 1], e2[:], prob[:, 0], ALU.mult))


HT = HID_E // P
XT = -(-ROWS // P)
LAST = ROWS - (XT - 1) * P


def experts(nc, sem, X, slot_s, ein, eout, wfc, bfc, wgate, bgate, wproj, bproj, ident):
    chunks = [(t, min(SUB, XT - t)) for t in range(0, XT, SUB)]
    NCH = len(chunks)
    WG = 4
    WC = HID_E // WG
    PARTS = ((0, 0), (0, 1), (1, 0))

    def width(t, k):
        return min(ROWS, (t + k) * P) - t * P

    with ExitStack() as ctx:
        sb = lambda n, s, t: ctx.enter_context(nc.sbuf_tensor("E_" + n, s, t))
        wfg = sb("wfg", [P, 2, KC, HID_E], F32)
        wp = sb("wp", [P, HT, D], F32)
        wfg_p = [sb(f"wfg{i}", [P, 2, KC, HID_E], F32R) for i in range(2)]
        wp_p = [sb(f"wp{i}", [P, HT, D], F32R) for i in range(2)]
        bf = sb("bf", [P, 2, HT], F32)
        bg = sb("bg", [P, 2, HT], F32)
        bp = sb("bp", [P, 2, D], F32)
        xin = sb("xin", [P, 2, XT, D], F32)
        xT = [sb(f"xT{i}", [P, KC, CH], F32R) for i in range(2)]
        hs = sb("hs", [P, 2, CH], F32)
        z = sb("z", [P, 2, CH], F32)
        sl = sb("sl", [P, 2, CH], F32)
        a = [sb(f"a{i}", [P, HT, CH], F32R) for i in range(2)]
        ob = sb("ob", [P, SUB, D], F32)
        idf = sb("idf", [P, P], F32)
        pT = [ctx.enter_context(nc.psum_tensor(f"E_pT{i}", [P, CH], F32)) for i in range(2)]
        pH = [ctx.enter_context(nc.psum_tensor(f"E_pH{i}", [P, CH], F32)) for i in range(2)]
        pG = [ctx.enter_context(nc.psum_tensor(f"E_pG{i}", [P, CH], F32)) for i in range(2)]
        pO = [ctx.enter_context(nc.psum_tensor(f"E_pO{i}", [P, CH], F32)) for i in range(2)]
        c_in, sent = sem("E_c_in", 0), sem("E_sent", 0)
        w_in, x_in = [sem(f"E_w_in{i}", 0) for i in range(2)], [sem(f"E_x_in{i}", 0) for i in range(2)]
        whi_done, wlo_done, phi_done, plo_done = sem("E_whi"), sem("E_wlo"), sem("E_phi"), sem("E_plo")
        t_done, xhi_done, xt_done, hg_done, hs_done = sem("E_t"), sem("E_xhi"), sem("E_xt"), sem("E_hg"), sem("E_hs")
        z_done, s_done, a_done, o_mm, o_done = sem("E_z"), sem("E_s"), sem("E_a"), sem("E_omm"), sem("E_od")
        o_out, fence = sem("E_out"), sem("E_fence")
        sem.start()
        block = ctx.enter_context(nc.Block())
        W_LOADS, X_LOADS = 6, 2

        @block.gpsimd
        def _(pool):
            def load_weights(e, s):
                for dst, src, kc in ((wfg[:, 0], wfc, KC), (wfg[:, 1], wgate, KC), (wp[:], wproj, HT)):
                    pool.dma_start(dst, src[ds(e * kc * P, kc * P), :].rearrange("(k p) n -> p k n", p=P)
                                   ).then_inc(w_in[s], 16)
                pool.dma_start(bf[:, s], bfc[ds(e * P, P), :]).then_inc(w_in[s], 16)
                pool.dma_start(bg[:, s], bgate[ds(e * P, P), :]).then_inc(w_in[s], 16)
                pool.dma_start(bp[:, s], bproj[ds(e, 1), :].to_broadcast([P, D])).then_inc(w_in[s], 16)

            def load_rows(e, s):
                rows = e * ROWS
                pool.dma_start(xin[:, s, 0:XT - 1], ein[ds(rows, (XT - 1) * P), :].rearrange("(t p) c -> p t c", p=P)
                               ).then_inc(x_in[s], 16)
                pool.dma_start(xin[0:LAST, s, XT - 1], ein[ds(rows + (XT - 1) * P, LAST), :]).then_inc(x_in[s], 16)

            load_weights(0, 0)
            for b in range(B):
                for k in range(TOPK):
                    for q in range(S // P):
                        pool.indirect_dma_start(ein, bass.IndirectOffsetOnAxis(slot_s[:, b, k, q:q + 1], 0),
                                                X[:, b * (S // P) + q], None, bounds_check=E_ * ROWS - 1,
                                                oob_is_err=False).then_inc(sent, 16)
            pool.wait_ge(sent, 16 * B * TOPK * (S // P))
            load_rows(0, 0)

            def following(e, s):
                wait_apart(pool, plo_done, e * WG, fence)
                load_rows(e, s)
                load_weights(e, s)
            with pool.Fori(0, E_ // 2 - 1) as pair:
                following(pair * 2 + 1, 1)
                following(pair * 2 + 2, 0)
            following(E_ - 1, 1)

        def every(eng, first, body):
            def two(pair, last):
                for s in range(2):
                    for c in range(NCH):
                        nxt = (pair, s, c + 1) if c < NCH - 1 else (pair, 1, 0) if s == 0 else (pair + 1, 0, 0)
                        body(pair, s, c, None if last and s == 1 and c == NCH - 1 else nxt)
            first(0, 0, 0)
            with eng.Fori(0, E_ // 2 - 1) as pair:
                two(pair, False)
            two(E_ // 2 - 1, True)

        def number(pair, s, c):
            return pair * (2 * NCH) + s * NCH + c

        @block.tensor
        def _(pe):
            pe.wait_ge(c_in, 16)

            def turn(pair, s, c):
                t, k = chunks[c]
                if c == 0:
                    pe.wait_ge(x_in[s], pair * (16 * X_LOADS) + 16 * X_LOADS)
                pe.wait_ge(xt_done, number(pair, s, c) + 1)
                for h in range(KC):
                    for j in range(k):
                        r = min(P, ROWS - (t + j) * P)
                        last = pe.transpose(pT[h][:, j * P:j * P + r], xin[0:r, s, t + j, h * P:(h + 1) * P],
                                            idf[0:r, 0:r])
                last.then_inc(t_done, 1)

            def body(pair, s, c, nxt):
                q, (t, k) = number(pair, s, c), chunks[c]
                w = width(t, k)
                pe.wait_ge(xt_done, q + 2)
                for ht in range(HT):
                    if c == 0 and ht * P % WC == 0:
                        pe.wait_ge(wlo_done, (pair * 2 + s) * WG + ht * P // WC + 2)
                    pe.wait_ge(z_done, q * HT + ht + 2)
                    for i, bank in enumerate((pH, pG)):
                        for kc in range(KC):
                            for j, (pw, px) in enumerate(PARTS):
                                last = pe.matmul(bank[ht % 2][:, 0:w], wfg_p[pw][:, i, kc, ht * P:(ht + 1) * P],
                                                 xT[px][:, kc, 0:w], start=kc + j == 0, stop=kc == KC - 1 and j == 2)
                    last.then_inc(hg_done, 1)
                if nxt:
                    turn(*nxt)
                if c == 0:
                    pe.wait_ge(plo_done, (pair * 2 + s) * WG + WG + 1)
                pe.wait_ge(a_done, (q + 1) * HT + 3)
                pe.wait_ge(o_done, q + 1)
                for j in range(k):
                    r = min(P, ROWS - (t + j) * P)
                    for ht in range(HT):
                        for i, (pa, pw) in enumerate(PARTS):
                            last = pe.matmul(pO[j // 2][0:r, j % 2 * D:(j % 2 + 1) * D],
                                             a[pa][:, ht, j * P:j * P + r], wp_p[pw][:, ht],
                                             start=ht + i == 0, stop=ht == HT - 1 and i == 2)
                last.then_inc(o_mm, 1)
            every(pe, turn, body)

        @block.scalar
        def _(act):
            def rows_hi(pair, s, c):
                q, w = number(pair, s, c), width(*chunks[c])
                act.wait_ge(t_done, q + 2)
                act.wait_ge(hg_done, q * HT + 1)
                for h in range(KC):
                    last = act.activation(xT[0][:, h, 0:w], pT[h][:, 0:w], ACT.Copy)
                last.then_inc(xhi_done, 1)

            def silu(q, ht, w):
                act.wait_ge(z_done, q * HT + ht + 4)
                act.wait_ge(a_done, q * HT + ht + 2)
                act.activation(a[0][:, ht, 0:w], z[:, ht % 2, 0:w], ACT.Silu)
                act.activation(sl[:, ht % 2, 0:w], z[:, ht % 2, 0:w], ACT.Silu).then_inc(s_done, 1)

            def body(pair, s, c, nxt):
                q, w = number(pair, s, c), width(*chunks[c])
                if c == 0:
                    act.wait_ge(w_in[s], pair * (16 * W_LOADS) + 16 * W_LOADS)
                    act.wait_ge(hg_done, q * HT + 1)
                    for g in range(WG):
                        cols = slice(g * WC, (g + 1) * WC)
                        act.activation(wfg_p[0][:, :, :, cols], wfg[:, :, :, cols], ACT.Copy).then_inc(whi_done, 1)
                for ht in range(HT):
                    act.wait_ge(hg_done, q * HT + ht + 2)
                    act.activation(hs[:, ht % 2, 0:w], pH[ht % 2][:, 0:w], ACT.Identity, bias=bf[:, s, ht:ht + 1]
                                   ).then_inc(hs_done, 1)
                    if ht == 0:
                        act.wait_ge(o_mm, q + 1)
                    else:
                        silu(q, ht - 1, w)
                    if c == 0 and ht < WG:
                        part = slice(ht * (HT // WG), (ht + 1) * (HT // WG))
                        act.activation(wp_p[0][:, part], wp[:, part], ACT.Copy).then_inc(phi_done, 1)
                silu(q, HT - 1, w)
                if nxt:
                    rows_hi(*nxt)
            every(act, rows_hi, body)

        @block.vector
        def _(dve):
            for s in (z_done, a_done, s_done):
                dve.sem_inc(s, 2)

            def rows_lo(pair, s, c):
                q, w = number(pair, s, c), width(*chunks[c])
                dve.wait_ge(xhi_done, q + 2)
                for h in range(KC):
                    last = dve.tensor_tensor(xT[1][:, h, 0:w], pT[h][:, 0:w], xT[0][:, h, 0:w].bitcast(F32),
                                             ALU.subtract)
                last.then_inc(xt_done, 1)

            def low(q, ht, w):
                dve.wait_ge(s_done, q * HT + ht + 4)
                dve.tensor_tensor(a[1][:, ht, 0:w], sl[:, ht % 2, 0:w], a[0][:, ht, 0:w].bitcast(F32), ALU.subtract
                                  ).then_inc(a_done, 1)

            def body(pair, s, c, nxt):
                q, (t, k) = number(pair, s, c), chunks[c]
                e, w = pair * 2 + s, width(t, k)
                if c == 0:
                    for g in range(WG):
                        cols = slice(g * WC, (g + 1) * WC)
                        dve.wait_ge(whi_done, e * WG + g + 2)
                        dve.tensor_tensor(wfg_p[1][:, :, :, cols], wfg[:, :, :, cols],
                                          wfg_p[0][:, :, :, cols].bitcast(F32), ALU.subtract).then_inc(wlo_done, 1)
                for ht in range(HT):
                    dve.wait_ge(hs_done, q * HT + ht + 2)
                    dve.wait_ge(s_done, q * HT + ht + 2)
                    dve.scalar_tensor_tensor(z[:, ht % 2, 0:w], pG[ht % 2][:, 0:w], bg[:, s, ht:ht + 1],
                                             hs[:, ht % 2, 0:w], ALU.add, ALU.mult).then_inc(z_done, 1)
                    if ht:
                        low(q, ht - 1, w)
                    if c == 0 and ht < WG:
                        part = slice(ht * (HT // WG), (ht + 1) * (HT // WG))
                        dve.wait_ge(phi_done, e * WG + ht + 2)
                        dve.tensor_tensor(wp_p[1][:, part], wp[:, part], wp_p[0][:, part].bitcast(F32), ALU.subtract
                                          ).then_inc(plo_done, 1)
                low(q, HT - 1, w)
                if nxt:
                    rows_lo(*nxt)
                dve.wait_ge(o_mm, q + 2)
                dve.wait_ge(o_out, e * (16 * (NCH + 1)) + 16 * c + 1)
                for j in range(k):
                    r = min(P, ROWS - (t + j) * P)
                    last = dve.tensor_tensor(ob[0:r, j], pO[j // 2][0:r, j % 2 * D:(j % 2 + 1) * D], bp[0:r, s], ALU.add)
                last.then_inc(o_done, 1)
            every(dve, rows_lo, body)

        @block.sync
        def _(sp):
            sp.dma_start(idf[:], ident).then_inc(c_in, 16)

            with sp.Fori(0, E_) as e:
                for c, (t, k) in enumerate(chunks):
                    w = width(t, k)
                    sp.wait_ge(o_done, e * NCH + c + 2)
                    rows = e * ROWS + t * P
                    whole = k if w == k * P else k - 1
                    sp.dma_start(eout[ds(rows, whole * P), :].rearrange("(t p) c -> p t c", p=P), ob[:, 0:whole]
                                 ).then_inc(o_out, 16)
                    if whole < k:
                        sp.dma_start(eout[ds(rows + whole * P, LAST), :], ob[0:LAST, whole]).then_inc(o_out, 16)
            sp.wait_ge(o_out, 16 * (NCH + 1) * E_ + 1)


def combine_and_project(nc, sem, X, eout, slot_g, prob, cos, sin, wq, wqs, wdown, wk, wks, wv, ident,
                        qh, ql, kh, kl, vs):
    LAT = wdown.shape[1]
    QT = S // P
    RJ = 2 * KC
    STORES = 2 * RJ + SUB
    with ExitStack() as ctx:
        sb = lambda n, s, t: ctx.enter_context(nc.sbuf_tensor("F_" + n, s, t))
        Y = sb("Y", [P, NT, TOPK, D], F32)
        y = sb("y", [P, SUB, D], F32)
        xn = sb("xn", [P, SUB, D], F32)
        xnT = sb("xnT", [P, KC, CH], F32)
        lat = sb("lat", [LAT, CH], F32)
        st = sb("st", [P, SUB, 6], F32)
        mv = sb("mv", [P, SUB, 2], F32)
        sd = sb("sd", [P, SUB], F32)
        rs = sb("rs", [P, SUB], F32)
        eps = sb("eps", [P, 1], F32)
        idf = sb("idf", [P, P], F32)
        wt = {n: sb("w" + n, [P, KC, D], F32) for n in ("q", "qs")}
        wd = sb("wd", [P, KC, LAT], F32)
        wkt = {n: sb("w" + n, [LAT, D], F32) for n in ("k", "ks", "v")}
        co = sb("co", [P, S], F32)
        si = sb("si", [P, S], F32)
        t1 = sb("t1", [P, CH], F32)
        t2 = sb("t2", [P, CH], F32)
        r = sb("r", [P, 2, CH], F32)
        hi = sb("hi", [P, RJ, CH], F32R)
        lo = sb("lo", [P, RJ, CH], F32R)
        v = sb("v", [P, SUB, NH, VW], F32)
        pb = [ctx.enter_context(nc.psum_tensor(f"F_pb{i}", [P, CH], F32)) for i in range(8)]
        c_in, got, eps_set = sem("F_c_in", 0), [sem(f"F_got{b}", 0) for b in range(B)], sem("F_eps")
        var_done, sd_done, n_done, x_copied = sem("F_var"), sem("F_sd"), sem("F_n"), sem("F_xc")
        t_done, xt_done, l_done, lat_done = sem("F_t"), sem("F_xt"), sem("F_l"), sem("F_lat")
        r_mm, r_read, r_done, hi_done, lo_done = sem("F_rmm"), sem("F_rr"), sem("F_r"), sem("F_hi"), sem("F_lo")
        v_mm, v_done, stored, fence = sem("F_vmm"), sem("F_v"), sem("F_st"), sem("F_fence")
        nch, jch = sem("F_nch"), sem("F_jch")
        sem.start()
        block = ctx.enter_context(nc.Block())

        def skewed(eng, first, body):
            first(0)
            for b in range(B):
                with eng.Fori(0, CPB - 1) as c:
                    body(b * CPB + c, b, c, b * CPB + c + 1)
                n = b * CPB + CPB - 1
                body(n, b, CPB - 1, n + 1 if b < B - 1 else None)

        def chunks(eng, body):
            with eng.Fori(0, B) as b:
                with eng.Fori(0, CPB) as c:
                    body(b * CPB + c, b, c)

        @block.gpsimd
        def _(pool):
            pool.memset(eps[:], EPS).then_inc(eps_set, 1)
            pool.memset(v[:], 1.0).then_inc(eps_set, 1)
            for b in range(B):
                for q in range(QT):
                    for k in range(TOPK):
                        pool.indirect_dma_start(Y[:, b * QT + q, k], None, eout,
                                                bass.IndirectOffsetOnAxis(slot_g[:, b, k, q:q + 1], 0),
                                                bounds_check=E_ * ROWS - 1, oob_is_err=False).then_inc(got[b], 16)

        @block.tensor
        def _(pe):
            pe.wait_ge(c_in, 16 * 9)

            def turn(n):
                pe.wait_ge(n_done, n + 2)
                pe.wait_ge(xt_done, n + 1)
                for kc in range(KC):
                    for s in range(SUB):
                        last = pe.transpose(pb[kc][:, s * P:(s + 1) * P], xn[:, s, kc * P:(kc + 1) * P], idf[:])
                last.then_inc(t_done, 1)

            def body(n, b, c, nxt):
                pe.wait_ge(xt_done, n + 2)
                pe.wait_ge(v_done, n + 1)
                for kc in range(KC):
                    last = pe.matmul(pb[2][0:LAT], wd[:, kc], xnT[:, kc], start=kc == 0, stop=kc == KC - 1)
                last.then_inc(l_done, 1)
                for j in range(RJ):
                    pe.wait_ge(r_read, n * RJ + j + 2)
                    m = j % KC
                    if j == KC:
                        pe.wait_ge(lat_done, n + 2)
                    for i, name in enumerate(("q", "qs") if j < KC else ("k", "ks")):
                        bank = pb[3 + 2 * (j % 2) + i]
                        if j < KC:
                            for kc in range(KC):
                                last = pe.matmul(bank[:], wt[name][:, kc, m * P:(m + 1) * P], xnT[:, kc],
                                                 start=kc == 0, stop=kc == KC - 1)
                        else:
                            last = pe.matmul(bank[:], wkt[name][:, m * P:(m + 1) * P], lat[:], start=True, stop=True)
                    last.then_inc(r_mm, 1)
                if nxt is not None:
                    turn(nxt)
                for s in range(SUB):
                    last = pe.matmul(pb[(7, 2)[s // 2]][:, s % 2 * D:(s % 2 + 1) * D], lat[:, s * P:(s + 1) * P],
                                     wkt["v"][:], start=True, stop=True)
                last.then_inc(v_mm, 1)
            skewed(pe, turn, body)

        @block.scalar
        def _(act):
            act.wait_ge(eps_set, 3)

            def deviation(n):
                act.wait_ge(var_done, n + 2)
                act.activation(sd[:], mv[:, :, 1], ACT.Sqrt, bias=eps[:]).then_inc(sd_done, 1)
                act.wait_ge(n_done, n + 2)
                act.activation(X[:, ds(n * SUB, SUB), :],
                               xn[:], ACT.Copy).then_inc(x_copied, 1)

            def turned(n):
                act.wait_ge(t_done, n + 2)
                act.wait_ge(r_mm, n * RJ + 1)
                for kc in range(KC):
                    last = act.activation(xnT[:, kc], pb[kc][:], ACT.Copy)
                last.then_inc(xt_done, 1)

            def first(n):
                deviation(n)
                turned(n)

            def body(n, b, c, nxt):
                act.wait_ge(l_done, n + 2)
                act.wait_ge(v_mm, n + 1)
                act.activation(lat[:], pb[2][0:LAT], ACT.Copy).then_inc(lat_done, 1)
                if nxt is not None:
                    deviation(nxt)
                act.wait_ge(stored, n * (16 * STORES) + 1)
                for j in range(RJ):
                    act.wait_ge(r_done, n * RJ + j + 2)
                    act.activation(hi[:, j], r[:, j % 2], ACT.Copy).then_inc(hi_done, 1)
                if nxt is not None:
                    turned(nxt)
                act.wait_ge(v_mm, n + 2)
                for s in range(SUB):
                    last = act.activation(v[:, s, :, 0:HD], pb[(7, 2)[s // 2]][:, s % 2 * D:(s % 2 + 1) * D].rearrange(
                        "p (h e) -> p h e", e=HD), ACT.Copy)
                last.then_inc(v_done, 1)
            skewed(act, first, body)

        @block.vector
        def _(dve):
            ch, cj = Chain(dve, nch, 2 * SUB + 2 + SUB - 1), Chain(dve, jch, RJ)
            dve.wait_ge(c_in, 16 * 9)
            dve.sem_inc(r_read, 2)

            def first(n):
                if isinstance(n, int) and n % CPB == 0:
                    dve.wait_ge(got[n // CPB], 16 * QT * TOPK)
                ch.start(n)
                for s in range(SUB):
                    tile = n * SUB + s
                    t0 = Y[:, ds(tile, 1), 0, :].rearrange("p o c -> p (o c)")
                    ch.link(dve.scalar_tensor_tensor(y[:, s], t0, prob[:, 0, ds(tile, 1)],
                                                     X[:, ds(tile, 1), :].rearrange("p o c -> p (o c)"),
                                                     ALU.mult, ALU.add))
                for s in range(SUB):
                    tile = n * SUB + s
                    t0 = Y[:, ds(tile, 1), 1, :].rearrange("p o c -> p (o c)")
                    ch.link(dve.scalar_tensor_tensor(y[:, s], t0, prob[:, 1, ds(tile, 1)], y[:, s],
                                                     ALU.mult, ALU.add))
                for s in range(SUB):
                    last = dve.bn_stats(st[:, s], y[:, s])
                ch.link(last)
                dve.sem_inc(fence, 1)
                for s in range(SUB):
                    last = dve.bn_aggr(mv[:, s], st[:, s])
                last.then_inc(var_done, 1)
                dve.wait_ge(sd_done, n + 2)
                ch.link(dve.reciprocal(rs[:], sd[:]))
                dve.wait_ge(x_copied, n + 1)
                dve.wait_ge(t_done, n + 1)
                for s in range(SUB):
                    last = dve.tensor_scalar(xn[:, s], y[:, s], mv[:, s, 0:1], rs[:, s:s + 1], ALU.subtract, ALU.mult)
                    if s == SUB - 1:
                        last.then_inc(n_done, 1)
                    else:
                        ch.link(last)
                ch.end()

            def body(n, b, c, nxt):
                if nxt is not None:
                    first(nxt)
                cj.start(n)
                for j in range(RJ):
                    dve.wait_ge(r_mm, n * RJ + j + 2)
                    main, swap = pb[3 + 2 * (j % 2)], pb[4 + 2 * (j % 2)]
                    dve.tensor_tensor(t1[:], main[:], co[:, ds(c * CH, CH)], ALU.mult)
                    last = dve.tensor_tensor(t2[:], swap[:], si[:, ds(c * CH, CH)], ALU.mult)
                    last.then_inc(r_read, 1)
                    dve.wait_ge(r_read, n * RJ + j + 4)
                    dve.tensor_tensor(r[:, j % 2], t1[:], t2[:], ALU.add).then_inc(r_done, 1)
                    dve.wait_ge(hi_done, n * RJ + j + 2)
                    last = dve.tensor_tensor(lo[:, j], r[:, j % 2], hi[:, j].bitcast(F32), ALU.subtract)
                    cj.link(last)
                dve.sem_inc(lo_done, 1)
                cj.end()
            skewed(dve, first, body)
            dve.wait_ge(x_copied, TOK // CH + 1)

        @block.sync
        def _(sp):
            sp.dma_start(idf[:], ident).then_inc(c_in, 16)
            for n, src in (("q", wq), ("qs", wqs)):
                sp.dma_start(wt[n][:], src.rearrange("(kc p) n -> p kc n", p=P)).then_inc(c_in, 16)
            sp.dma_start(wd[:], wdown.rearrange("(kc p) n -> p kc n", p=P)).then_inc(c_in, 16)
            for n, src in (("k", wk), ("ks", wks), ("v", wv)):
                sp.dma_start(wkt[n][:], src).then_inc(c_in, 16)
            sp.dma_start(co[:], cos).then_inc(c_in, 16)
            sp.dma_start(si[:], sin).then_inc(c_in, 16)
            vs_v = vs.rearrange("(bb g t) e -> bb t g e", bb=B, g=NG)

            def body(n, b, c):
                sp.wait_ge(lo_done, n + 2)
                for j in range(RJ):
                    for dst, src in (((qh, hi), (ql, lo)) if j < KC else ((kh, hi), (kl, lo))):
                        sp.dma_start(dst[ds(b * D + j % KC * P, P), ds(c * CH, CH)], src[:, j].bitcast(F32)
                                     ).then_inc(stored, 16)
                sp.wait_ge(v_done, n + 2)
                for s in range(SUB):
                    sp.dma_start(vs_v[ds(b, 1), ds(c * CH + s * P, P)].rearrange("o t g e -> (o t) g e"),
                                 v[:, s]).then_inc(stored, 16)
            chunks(sp, body)
            sp.wait_ge(stored, 16 * STORES * (TOK // CH) + 1)


LH, LD = 8, 64
INNER = LH * LD
WIN = S // P
VE = LD + 1
HIDF = int(D * 4 * 2 / 3)
FT = -(-HIDF // P)
FLAST = HIDF - (FT - 1) * P
PADS = S + 1
PADW = S + P
PAIRS = INNER // P


def tiles(eng, body):
    with eng.Fori(0, B) as b:
        with eng.Fori(0, WIN // 2) as pair:
            for u in range(2):
                body(b * WIN + pair * 2 + u, b, pair * 2 + u, b * (WIN // 2) + pair, u)


def local_projections(nc, sem, tag, xp, wqkv, tab, scales, ident, qT, kT, ve):
    W2 = 2 * INNER
    NB = 2 * LH
    H = LD // 2
    with ExitStack() as ctx:
        sb = lambda n, s, t: ctx.enter_context(nc.sbuf_tensor(tag + n, s, t))
        w = sb("w", [P, KC, 3 * INNER], F32)
        whi = sb("whi", [P, KC, 3 * INNER], F32R)
        wlo = sb("wlo", [P, KC, 3 * INNER], F32R)
        h = sb("h", [P, 2, D], F32)
        hhi = sb("hhi", [P, 2, KC, P], F32R)
        hlo = sb("hlo", [P, 2, KC, P], F32R)
        tb = sb("tb", [P, 4, WIN, LD], F32)
        sc = sb("sc", [P, 2, LD], F32)
        A = sb("A", [P, 2, WIN, LD], F32)
        R = sb("R", [P, 2, WIN, LD], F32)
        sq = sb("sq", [P, W2], F32)
        ss = sb("ss", [P, 2, NB], F32)
        nr = sb("nr", [P, 2, NB], F32)
        rn = sb("rn", [P, 2, NB], F32)
        qn = sb("qn", [P, 2, 2, LH, LD], F32)
        t1 = sb("t1", [P, 2, 2, LH, LD], F32)
        t2 = sb("t2", [P, 2, 2, LH, LD], F32)
        v = sb("v", [P, 2, LH, VE], F32)
        tT = sb("tT", [P, 2, 2, PAIRS, P], F32)
        idf = sb("idf", [P, P], F32)
        pqk = [ctx.enter_context(nc.psum_tensor(f"{tag}pqk{u}", [P, 2, CH], F32)) for u in range(2)]
        pt = ctx.enter_context(nc.psum_tensor(f"{tag}pt", [P, 2, CH], F32))
        pv = ctx.enter_context(nc.psum_tensor(f"{tag}pv", [P, CH], F32))
        ph = ctx.enter_context(nc.psum_tensor(f"{tag}ph", [P, CH], F32))
        c_in, h_in, v_set = sem(tag + "c_in", 0), [sem(f"{tag}h_in{u}", 0) for u in range(2)], sem(tag + "vs")
        t_done, hi_done, ht_done = sem(tag + "t"), sem(tag + "hi"), sem(tag + "ht")
        whi_done, wlo_done, qk_mm, v_mm = sem(tag + "whi"), sem(tag + "wlo"), sem(tag + "qkmm"), sem(tag + "vmm")
        sq_done, ss_done, nr_done, qn_done = sem(tag + "sq"), sem(tag + "ss"), sem(tag + "nr"), sem(tag + "qn")
        t2_done, r_done, qt_done, ev_done = sem(tag + "t2"), sem(tag + "r"), sem(tag + "qt"), sem(tag + "ev")
        v_done, tabs = sem(tag + "v"), sem(tag + "tabs")
        rot, clip, inv = sem(tag + "rot"), sem(tag + "clip"), sem(tag + "inv")
        v_out, qk_out = [sem(f"{tag}vo{u}") for u in range(2)], [sem(f"{tag}qo{u}") for u in range(2)]
        sem.start()
        block = ctx.enter_context(nc.Block())

        def skewed(eng, first, mul, turn):
            M = WIN // 2
            with eng.Fori(0, B) as b:
                first(b, 0, 0, 0)
                mul(b, 0, 0, 0, (b, 1, 0, 1))
                mul(b, 1, 0, 1, (b, 2, 1, 0))
                with eng.Fori(0, M - 2) as m:
                    for u in range(2):
                        mul(b, m * 2 + u + 2, m + 1, u, (b, m * 2 + u + 3, m + 1 + u, 1 - u))
                        turn(b, m * 2 + u, m, u)
                mul(b, WIN - 2, M - 1, 0, (b, WIN - 1, M - 1, 1))
                turn(b, WIN - 4, M - 2, 0)
                mul(b, WIN - 1, M - 1, 1, None)
                turn(b, WIN - 3, M - 2, 1)
                turn(b, WIN - 2, M - 1, 0)
                turn(b, WIN - 1, M - 1, 1)

        def nothing(*a):
            pass

        @block.sync
        def _(sp):
            sp.dma_start(w[:], wqkv.rearrange("(kc p) n -> p kc n", p=P)).then_inc(c_in, 16)
            sp.dma_start(tb[:], tab.rearrange("(k w p) d -> p k w d", p=P, w=WIN)).then_inc(c_in, 16)
            sp.dma_start(sc[:].rearrange("p k d -> p (k d)"), scales.to_broadcast([P, 2 * LD])).then_inc(c_in, 16)
            sp.dma_start(idf[:], ident).then_inc(c_in, 16)

            def first(b, w_, m, u):
                sp.wait_ge(t_done, b * WIN + w_ + 1)
                row = b * PADS + w_ * P
                sp.dma_start(h[:, u, 0:P], xp[ds(row + 1, P), 0:P]).then_inc(h_in[u], 16)
                sp.dma_start(h[:, u, P:D], xp[ds(row, P), P:D]).then_inc(h_in[u], 16)

            def mul(b, w_, m, u, nxt):
                if nxt:
                    first(*nxt)
                sp.wait_ge(v_done, b * WIN + w_ + 2)
                sp.dma_start(ve[ds(b * PADW + w_ * P + P, P), :], v[:, u].rearrange("p h e -> p (h e)")
                             ).then_inc(v_out[u], 16)

            def turn(b, w_, m, u):
                sp.wait_ge(ev_done, b * WIN + w_ + 2)
                for dst, j, col in ((qT, 0, w_ * P), (kT, 1, w_ * P + P)):
                    sp.dma_start(dst[ds(b * INNER, INNER), ds(col, P)].rearrange("(g p) t -> p g t", p=P), tT[:, u, j]
                                 ).then_inc(qk_out[u], 16)
            skewed(sp, first, mul, turn)
            for u in range(2):
                sp.wait_ge(v_out[u], 16 * (NT // 2) + 1)
                sp.wait_ge(qk_out[u], 32 * (NT // 2) + 1)

        @block.tensor
        def _(pe):
            for s in (t_done, v_mm, qt_done):
                pe.sem_inc(s, 1)
            pe.wait_ge(c_in, 64)
            pe.wait_ge(wlo_done, 2)

            def first(b, w_, m, u):
                pe.wait_ge(h_in[u], b * (WIN // 2 * 32) + m * 32 + 32)
                pe.wait_ge(ht_done, b * WIN + w_ + 1)
                for kc in range(KC):
                    last = pe.transpose(ph[:, kc * P:(kc + 1) * P], h[:, u, kc * P:(kc + 1) * P], idf[:])
                last.then_inc(t_done, 1)

            def mul(b, w_, m, u, nxt):
                n = b * WIN + w_
                pe.wait_ge(ht_done, n + 2)
                pe.wait_ge(qn_done, n + 1)
                pe.wait_ge(v_done, n + 1)
                for j in range(3):
                    for kc in range(KC):
                        for i, (x_, y_) in enumerate(((hhi, whi), (hhi, wlo), (hlo, whi))):
                            last = pe.matmul(pqk[u][:, j] if j < 2 else pv[:], x_[:, u, kc],
                                             y_[:, kc, j * INNER:(j + 1) * INNER], start=kc + i == 0,
                                             stop=kc == KC - 1 and i == 2)
                    if j == 1:
                        last.then_inc(qk_mm, 1)
                last.then_inc(v_mm, 1)
                if nxt:
                    first(*nxt)

            def turn(b, w_, m, u):
                n = b * WIN + w_
                pe.wait_ge(r_done, n + 2)
                pe.wait_ge(ev_done, n + 1)
                for j in range(2):
                    for g in range(PAIRS):
                        last = pe.transpose(pt[:, j, g * P:(g + 1) * P],
                                            t1[:, u, j].rearrange("p h e -> p (h e)")[:, g * P:(g + 1) * P], idf[:])
                last.then_inc(qt_done, 1)
            skewed(pe, first, mul, turn)

        @block.scalar
        def _(act):
            act.wait_ge(v_set, 2)
            act.wait_ge(c_in, 64)
            act.activation(whi[:], w[:], ACT.Copy).then_inc(whi_done, 1)

            def first(b, w_, m, u):
                n = b * WIN + w_
                act.wait_ge(t_done, n + 3)
                act.wait_ge(v_mm, n + 1)
                act.activation(hhi[:, u].rearrange("p k t -> p (k t)"), ph[:, 0:D], ACT.Copy).then_inc(hi_done, 1)

            def mul(b, w_, m, u, nxt):
                n = b * WIN + w_
                act.wait_ge(qk_mm, n + 2)
                act.wait_ge(ss_done, n + 1)
                act.activation(sq[:], pqk[u][:].rearrange("p j c -> p (j c)"), ACT.Square).then_inc(sq_done, 1)
                if nxt:
                    first(*nxt)
                act.wait_ge(v_mm, n + 3)
                act.wait_ge(v_out[u], b * (WIN // 2 * 16) + m * 16 + 1)
                act.activation(v[:, u, :, 0:LD], pv[:].rearrange("p (h e) -> p h e", e=LD), ACT.Copy
                               ).then_inc(v_done, 1)
                act.wait_ge(ss_done, n + 2)
                act.activation(nr[:, u], ss[:, u], ACT.Sqrt).then_inc(nr_done, 1)

            def turn(b, w_, m, u):
                act.wait_ge(qt_done, b * WIN + w_ + 3)
                act.wait_ge(qk_out[u], b * (WIN // 2 * 32) + m * 32 + 1)
                act.activation(tT[:, u].rearrange("p j g t -> p j (g t)"), pt[:], ACT.Copy).then_inc(ev_done, 1)
            skewed(act, first, mul, turn)

        @block.gpsimd
        def _(pool):
            pool.wait_ge(tabs, 2)

            def mul(b, w_, m, u, nxt):
                pool.wait_ge(qn_done, b * WIN + w_ + 3)
                for a, z in ((0, H), (H, 0)):
                    last = pool.tensor_tensor(
                        t2[:, u, :, :, a:a + H], qn[:, u, :, :, z:z + H],
                        R[:, :, ds(w_, 1), a:a + H].to_broadcast([P, 2, LH, H]), ALU.mult)
                last.then_inc(t2_done, 1)
            skewed(pool, nothing, mul, nothing)

        @block.vector
        def _(dve):
            dve.wait_ge(c_in, 64)
            dve.sem_inc(qn_done, 1)
            dve.memset(v[:], 1.0).then_inc(v_set, 1)
            for j in range(2):
                dve.tensor_tensor(A[:, j], tb[:, 2 * j], sc[:, j:j + 1].to_broadcast([P, WIN, LD]), ALU.mult)
                for a, z in ((0, H), (H, 0)):
                    last = dve.tensor_tensor(R[:, j, :, a:a + H], tb[:, 2 * j + 1, :, a:a + H],
                                             sc[:, j:j + 1, z:z + H].to_broadcast([P, WIN, H]), ALU.mult)
            last.then_inc(tabs, 1)
            dve.wait_ge(whi_done, 2)
            dve.tensor_tensor(wlo[:], w[:], whi[:].bitcast(F32), ALU.subtract).then_inc(wlo_done, 1)
            dve.wait_ge(tabs, 2)

            def first(b, w_, m, u):
                n = b * WIN + w_
                dve.wait_ge(hi_done, n + 2)
                dve.tensor_tensor(hlo[:, u].rearrange("p k t -> p (k t)"), ph[:, 0:D],
                                  hhi[:, u].rearrange("p k t -> p (k t)").bitcast(F32), ALU.subtract
                                  ).then_inc(ht_done, 1)

            def rotate(b, w_, u):
                n = b * WIN + w_
                dve.wait_ge(qn_done, n + 3)
                dve.wait_ge(qt_done, n + 1)
                link(dve.tensor_tensor(
                    t1[:, u], qn[:, u],
                    A[:, :, ds(w_, 1), :].to_broadcast([P, 2, LH, LD]), ALU.mult), rot, n + 2)
                dve.wait_ge(t2_done, n + 2)
                dve.tensor_tensor(t1[:, u], t1[:, u], t2[:, u], ALU.add).then_inc(r_done, 1)

            def link(ins, s, value):
                ins.then_inc(s, 1)
                dve.wait_ge(s, value)

            def mul(b, w_, m, u, nxt):
                n = b * WIN + w_
                dve.wait_ge(sq_done, n + 2)
                dve.tensor_reduce(ss[:, u], sq[:].rearrange("p (n e) -> p n e", e=LD), AX, ALU.add
                                  ).then_inc(ss_done, 1)
                if nxt:
                    first(*nxt)
                if not (isinstance(w_, int) and w_ == 0):
                    rotate(b, w_ - 1, 1 - u)
                dve.wait_ge(nr_done, n + 2)
                link(dve.tensor_scalar(nr[:, u], nr[:, u], 1e-12, None, ALU.max), clip, n + 2)
                link(dve.reciprocal(rn[:, u], nr[:, u]), inv, n + 2)
                dve.tensor_tensor(qn[:, u].rearrange("p j h e -> p (j h) e"),
                                  pqk[u][:].rearrange("p j (h e) -> p (j h) e", e=LD),
                                  rn[:, u].unsqueeze(2).to_broadcast([P, NB, LD]), ALU.mult).then_inc(qn_done, 1)

            def turn(b, w_, m, u):
                if isinstance(w_, int) and w_ == WIN - 3:
                    rotate(b, WIN - 1, 1)
            skewed(dve, first, mul, turn)


def local_attention(nc, sem, tag, qT, kT, ve, wo, masks, ident_bf, ident, X, xp):
    def pos(h):
        return h % 2 * (LH // 2) + h // 2

    HB = LH // 2
    BANK = [0, 1, 1, 0]
    with ExitStack() as ctx:
        sb = lambda n, s, t: ctx.enter_context(nc.sbuf_tensor(tag + n, s, t))
        q = sb("q", [P, 2, PAIRS, P], F32)
        k = sb("k", [P, 2, PAIRS, 2 * P], F32)
        v = sb("v", [P, 2, 2, LH * VE], F32)
        pr = sb("pr", [P, 2, LH, 2 * P], F32)
        pT = sb("pT", [P, 4, 2, 2, P], F32)
        mx = sb("mx", [P, 2, LH], F32)
        nm = sb("nm", [P, 2, LH], F32)
        rc = sb("rc", [P, LH], F32)
        cx = sb("cx", [P, LH, LD], F32)
        cT = sb("cT", [P, PAIRS, P], F32)
        xn = sb("xn", [P, 2, D], F32)
        w = sb("w", [P, PAIRS, D], F32)
        mk = sb("mk", [P, NT, 2 * P], BF16)
        idb = sb("idb", [P, P], BF16)
        idf = sb("idf", [P, P], F32)
        pS = ctx.enter_context(nc.psum_tensor(tag + "pS", [P, LH, 2 * P], F32))
        pP = [ctx.enter_context(nc.psum_tensor(f"{tag}pP{i}", [P, CH], F32)) for i in range(2)]
        pO = [ctx.enter_context(nc.psum_tensor(f"{tag}pO{i}", [P, CH], F32)) for i in range(2)]
        c_in, used = sem(tag + "c_in", 0), sem(tag + "used")
        in_, v_in = [sem(f"{tag}in{u}", 0) for u in range(2)], [sem(f"{tag}vin{u}", 0) for u in range(2)]
        s_done, m_done, nm_done, e_done = sem(tag + "s"), sem(tag + "m"), sem(tag + "nm"), sem(tag + "e")
        t_done, te_done, o_mm, cx_done = sem(tag + "t"), [sem(f"{tag}te{i}") for i in range(2)], sem(tag + "omm"), sem(tag + "cx")
        ct_mm, ct_done, w_mm, x_done = sem(tag + "ctm"), sem(tag + "ct"), sem(tag + "wmm"), sem(tag + "x")
        fence = sem(tag + "fence")
        x_out, xc, dch = [sem(f"{tag}xo{u}") for u in range(2)], sem(tag + "xc"), sem(tag + "dch")
        sem.start()
        block = ctx.enter_context(nc.Block())

        def skewed(eng, first, body, finish):
            first()
            body(0, 0, 0, True, False)
            body(1, 0, 1, True, True)
            with eng.Fori(1, NT // 2 - 1) as m:
                for u in range(2):
                    body(m * 2 + u, m, u, True, True)
            body(NT - 2, NT // 2 - 1, 0, True, True)
            body(NT - 1, NT // 2 - 1, 1, False, True)
            finish(NT, NT // 2, 0)

        @block.gpsimd
        def _(pool):
            for dst, src in ((w[:], wo.rearrange("(g p) n -> p g n", p=P)), (idb[:], ident_bf), (idf[:], ident),
                             (mk[:], masks.rearrange("(w p) k -> p w k", p=P))):
                pool.dma_start(dst, src).then_inc(c_in, 16)

            def body(n, b, win, m, u):
                wait_apart(pool, s_done, n, fence)
                pool.dma_start(q[:, u], qT[ds(b * INNER, INNER), ds(win * P, P)].rearrange("(g p) t -> p g t", p=P)
                               ).then_inc(in_[u], 16)
                pool.dma_start(k[:, u], kT[ds(b * INNER, INNER), ds(win * P, 2 * P)].rearrange(
                    "(g p) t -> p g t", p=P)).then_inc(in_[u], 16)
                wait_apart(pool, used, n + 1, fence)
                pool.dma_start(v[:, u], ve[ds(b * PADW + win * P, 2 * P), :].rearrange("(s p) e -> p s e", p=P)
                               ).then_inc(v_in[u], 16)
            tiles(pool, body)

        @block.tensor
        def _(pe):
            pe.sem_inc(used, 2)
            pe.sem_inc(s_done, 1)
            pe.wait_ge(c_in, 64)

            def scores(n, u, m):
                pe.wait_ge(in_[u], m * 32 + 32)
                pe.wait_ge(e_done, n + 1)
                for i in range(4):
                    pe.matmul(pS[:, 2 * i:2 * i + 2, :], idb[:], mk[:, ds(n, 1), :].to_broadcast([P, 2, 2 * P]),
                              start=True, stop=False, skip_group_check=True)
                for h in sorted(range(LH), key=pos):
                    a = h % 2 * LD
                    last = pe.matmul(pS[:, pos(h), :], q[a:a + LD, u, h // 2], k[a:a + LD, u, h // 2],
                                     start=False, stop=True, skip_group_check=True)
                last.then_inc(s_done, 1)

            def turn(r, n, u):
                for i in range(2):
                    for s in range(2):
                        last = pe.transpose(pP[BANK[r]][:, (2 * i + s) * P:(2 * i + s + 1) * P],
                                            pr[:, u, 2 * r + i, s * P:(s + 1) * P], idf[:])
                last.then_inc(t_done, 1)

            def weigh(r, u):
                for i in range(2):
                    h = next(h for h in range(LH) if pos(h) == 2 * r + i)
                    for s in range(2):
                        last = pe.matmul(pO[h // HB][:, h % HB * VE:(h % HB + 1) * VE], pT[:, r, i, s],
                                         v[:, u, s, h * VE:(h + 1) * VE], start=s == 0, stop=s == 1)
                return last

            def turn_outputs(n):
                pe.wait_ge(cx_done, n + 1)
                for g in range(PAIRS):
                    last = pe.transpose(pP[0][:, g * P:(g + 1) * P],
                                        cx[:].rearrange("p h e -> p (h e)")[:, g * P:(g + 1) * P], idf[:])
                last.then_inc(ct_mm, 1)

            def project(n):
                for g in range(PAIRS):
                    last = pe.matmul(pO[0][:, 0:D], cT[:, g], w[:, g], start=g == 0, stop=g == PAIRS - 1)
                last.then_inc(w_mm, 1)

            def body(n, m, u, nxt, prev):
                pe.wait_ge(e_done, n + 2)
                pe.wait_ge(te_done[0], n * 2 + 1)
                turn(0, n, u)
                pe.wait_ge(te_done[1], n * 2 + 1)
                turn(1, n, u)
                if nxt:
                    scores(n + 1, 1 - u, m + u)
                pe.wait_ge(te_done[0], n * 2 + 2)
                if prev:
                    turn_outputs(n)
                pe.wait_ge(te_done[1], n * 2 + 2)
                turn(2, n, u)
                if prev:
                    pe.wait_ge(ct_done, n + 1)
                turn(3, n, u)
                if prev:
                    project(n)
                pe.wait_ge(v_in[u], m * 16 + 16)
                weigh(1, u)
                pe.wait_ge(te_done[0], n * 2 + 3)
                weigh(3, u)
                if prev:
                    pe.wait_ge(x_done, n + 1)
                weigh(0, u)
                pe.wait_ge(te_done[1], n * 2 + 3)
                weigh(2, u).then_inc(o_mm, 1)
                pe.drain().then_inc(used, 1)

            def finish(n, m, u):
                turn_outputs(n)
                pe.wait_ge(ct_done, n + 1)
                project(n)
            skewed(pe, lambda: scores(0, 0, 0), body, finish)

        @block.scalar
        def _(act):
            def exps(n, u):
                act.wait_ge(nm_done, n + 2)
                for p_ in range(LH):
                    last = act.activation(pr[:, u, p_], pS[:, p_, :], ACT.Exp, bias=nm[:, u, p_:p_ + 1], scale=8.0)
                last.then_inc(e_done, 1)

            def evict(r, done):
                act.wait_ge(t_done, done)
                act.activation(pT[:, r].rearrange("p i s t -> p (i s t)"), pP[0][:], ACT.Copy).then_inc(te_done[0], 1)

            def outputs(n):
                act.wait_ge(ct_mm, n + 1)
                act.activation(cT[:].rearrange("p g t -> p (g t)"), pP[0][:], ACT.Copy).then_inc(ct_done, 1)

            def result(n, u):
                act.wait_ge(x_done, n + 1)
                act.activation(X[:, ds(n - 1, 1), :], xn[:, 1 - u:2 - u], ACT.Copy).then_inc(xc, 1)

            def body(n, m, u, nxt, prev):
                evict(0, n * 4 + 2)
                if prev:
                    outputs(n)
                evict(3, n * 4 + 5)
                if nxt:
                    exps(n + 1, 1 - u)
                if prev:
                    result(n, u)

            def finish(n, m, u):
                outputs(n)
                result(n, u)
            skewed(act, lambda: exps(0, 0), body, finish)

        @block.vector
        def _(dve):
            ch = Chain(dve, dch, 1)

            def maxima(n, u):
                dve.wait_ge(s_done, n + 3)
                dve.tensor_reduce(mx[:, u], pS[:], AX, ALU.max).then_inc(m_done, 1)
                dve.wait_ge(m_done, n + 2)
                dve.tensor_scalar(nm[:, u], mx[:, u], -8.0, None, ALU.mult).then_inc(nm_done, 1)

            def evict(r, done):
                dve.wait_ge(t_done, done)
                dve.tensor_copy(pT[:, r].rearrange("p i s t -> p (i s t)"), pP[1][:]).then_inc(te_done[1], 1)

            def result(n, m, u):
                dve.wait_ge(w_mm, n + 1)
                dve.wait_ge(x_out[1 - u], (m - 1) * 16 + 1 if u == 0 else m * 16 + 1)
                dve.wait_ge(xc, n)
                dve.tensor_tensor(xn[:, 1 - u:2 - u], pO[0][:, 0:D].unsqueeze(1), X[:, ds(n - 1, 1), :], ALU.add
                                  ).then_inc(x_done, 1)

            def body(n, m, u, nxt, prev):
                ch.start(n)
                evict(1, n * 4 + 3)
                if nxt:
                    maxima(n + 1, 1 - u)
                evict(2, n * 4 + 4)
                if prev:
                    result(n, m, u)
                dve.wait_ge(o_mm, n + 2)
                o = [pO[i][:, 0:HB * VE].rearrange("p (h e) -> p h e", e=VE) for i in range(2)]
                for i in range(2):
                    last = dve.reciprocal(rc[:, i * HB:(i + 1) * HB], o[i][:, :, LD])
                ch.link(last)
                for i in range(2):
                    last = dve.tensor_tensor(cx[:, i * HB:(i + 1) * HB], o[i][:, :, 0:LD],
                                             rc[:, i * HB:(i + 1) * HB].unsqueeze(2).to_broadcast([P, HB, LD]),
                                             ALU.mult)
                last.then_inc(cx_done, 1)
            skewed(dve, lambda: maxima(0, 0), body, result)
            dve.wait_ge(xc, NT + 1)

        @block.sync
        def _(sp):
            def body(n, b, win, m, u):
                sp.wait_ge(x_done, n + 2)
                sp.dma_start(xp[ds(b * PADS + win * P + 1, P), :], xn[:, u]).then_inc(x_out[u], 16)
            tiles(sp, body)
            for u in range(2):
                sp.wait_ge(x_out[u], 16 * (NT // 2) + 1)


def gated_unit(nc, sem, tag, xp, lng, lnb, w1, b1a, b1g, w2, b2, ident, X, xp_out, xp_first, out):
    NCK = TOK // CH
    final = out is not None
    with ExitStack() as ctx:
        sb = lambda n, s, t: ctx.enter_context(nc.sbuf_tensor(tag + n, s, t))
        W1 = sb("W1", [P, KC, 2 * HIDF], F32)
        W2 = sb("W2", [P, FT, D], F32)
        W1p = [sb(f"W1p{i}", [P, KC, 2 * HIDF], F32R) for i in range(2)]
        W2p = [sb(f"W2p{i}", [P, FT, D], F32R) for i in range(2)]
        g_ = sb("g_", [P, KC], F32)
        b_ = sb("b_", [P, KC], F32)
        ba = sb("ba", [P, FT], F32)
        bg = sb("bg", [P, FT], F32)
        bb = sb("bb", [P, D], F32)
        h = sb("h", [P, 2, SUB, D], F32)
        hn = sb("hn", [P, SUB, D], F32)
        hTf = sb("hTf", [P, KC, CH], F32)
        hT = [sb(f"hT{i}", [P, KC, CH], F32R) for i in range(2)]
        gl = sb("gl", [P, 2, CH], F32)
        hidf = sb("hidf", [P, 2, CH], F32)
        hid = [sb(f"hid{i}", [P, FT, CH], F32R) for i in range(2)]
        y = sb("y", [P, SUB, D], F32)
        y2 = sb("y2", [P, 2, SUB, D], F32)
        x0 = sb("x0", [P, 2, SUB, D], F32)
        st = sb("st", [P, SUB, 6], F32)
        mv = sb("mv", [P, SUB, 2], F32)
        sd = sb("sd", [P, SUB], F32)
        rs = sb("rs", [P, SUB], F32)
        st2 = sb("st2", [P, SUB, 6], F32)
        mv2 = sb("mv2", [P, SUB, 2], F32)
        sd2 = sb("sd2", [P, SUB], F32)
        rs2 = sb("rs2", [P, SUB], F32)
        eps = sb("eps", [P, 1], F32)
        idf = sb("idf", [P, P], F32)
        pT = [ctx.enter_context(nc.psum_tensor(f"{tag}pT{i}", [P, CH], F32)) for i in range(2)]
        pA = [ctx.enter_context(nc.psum_tensor(f"{tag}pA{i}", [P, CH], F32)) for i in range(2)]
        pG = [ctx.enter_context(nc.psum_tensor(f"{tag}pG{i}", [P, CH], F32)) for i in range(2)]
        pO = [ctx.enter_context(nc.psum_tensor(f"{tag}pO{i}", [P, CH], F32)) for i in range(2)]
        c_in, h_in = sem(tag + "c_in", 0), [sem(f"{tag}h_in{u}", 0) for u in range(2)]
        var, sdd, n_done, t_done = sem(tag + "var"), sem(tag + "sdd"), sem(tag + "n"), sem(tag + "t")
        xt_done, ag_mm, gl_done, hid_done = sem(tag + "xt"), sem(tag + "ag"), sem(tag + "gl"), sem(tag + "hid")
        o_mm, y_done, x_done, xc = sem(tag + "omm"), sem(tag + "y"), sem(tag + "x"), sem(tag + "xc")
        var2, sdd2, eps_set = sem(tag + "var2"), sem(tag + "sdd2"), sem(tag + "eps")
        fence, w_hi, w_lo, ht_hi = sem(tag + "fence"), sem(tag + "whi"), sem(tag + "wlo"), sem(tag + "hthi")
        hi_done, lo_done = sem(tag + "hi"), sem(tag + "lo")
        dch, och, x_out = sem(tag + "dch"), sem(tag + "och"), [sem(f"{tag}xo{u}") for u in range(2)]
        sem.start()
        block = ctx.enter_context(nc.Block())
        x0_in, x_free = [sem(f"{tag}x0{u}", 0) for u in range(2)], sem(tag + "xf")
        NC_IN = 9
        PARTS = ((0, 0), (0, 1), (1, 0))
        W2_PIECES = ((slice(0, P), slice(0, FT - 1)), (slice(0, FLAST), slice(FT - 1, FT)))

        def skewed(eng, first, body):
            first(0)
            with eng.Fori(0, NCK // 2 - 1) as m:
                for u in range(2):
                    body(m * 2 + u, m, u, True)
            body(NCK - 2, NCK // 2 - 1, 0, True)
            body(NCK - 1, NCK // 2 - 1, 1, False)

        def chunks(eng, body):
            with eng.Fori(0, B) as b:
                with eng.Fori(0, CPB // 2) as pair:
                    for u in range(2):
                        body(b * CPB + pair * 2 + u, b, pair * 2 + u, b * (CPB // 2) + pair, u)

        def rows(j):
            return P if j < FT - 1 else FLAST

        @block.gpsimd
        def _(pool):
            pool.memset(eps[:], EPS).then_inc(eps_set, 1)
            for dst, src in ((W1[:], w1.rearrange("(kc p) n -> p kc n", p=P)),
                             (W2[:, 0:FT - 1], w2[0:(FT - 1) * P, :].rearrange("(k p) n -> p k n", p=P)),
                             (W2[0:FLAST, FT - 1], w2[(FT - 1) * P:HIDF, :]), (g_[:], lng), (b_[:], lnb),
                             (ba[:], b1a), (bg[:], b1g), (bb[:], b2.to_broadcast([P, D])), (idf[:], ident)):
                pool.dma_start(dst, src).then_inc(c_in, 16)

            def body(n, b, c, m, u):
                wait_apart(pool, n_done, n, fence)
                row = b * PADS + c * CH
                pool.dma_start(h[:, u, :, 0:P], xp[ds(row + 1, CH), 0:P].rearrange("(s p) c -> p s c", p=P)
                               ).then_inc(h_in[u], 16)
                pool.dma_start(h[:, u, :, P:D], xp[ds(row, CH), P:D].rearrange("(s p) c -> p s c", p=P)
                               ).then_inc(h_in[u], 16)
                if final:
                    wait_apart(pool, x_free, n + 1, fence)
                    pool.dma_start(x0[:, u], xp_first[ds(row + 1, CH), :].rearrange("(s p) c -> p s c", p=P)
                                   ).then_inc(x0_in[u], 16)
            chunks(pool, body)

        @block.tensor
        def _(pe):
            pe.wait_ge(c_in, 16 * NC_IN)
            pe.wait_ge(w_lo, 2)

            def turn(n):
                pe.wait_ge(n_done, n + 3)
                pe.wait_ge(xt_done, n + 1)
                for kc in range(KC):
                    for s in range(SUB):
                        last = pe.transpose(pT[kc][:, s * P:(s + 1) * P], hn[:, s, kc * P:(kc + 1) * P], idf[:])
                last.then_inc(t_done, 1)

            def body(n, m, u, nxt):
                pe.wait_ge(xt_done, n + 2)
                for j in range(FT):
                    pe.wait_ge(hid_done, n * FT + j + 2)
                    r = rows(j)
                    for bank, off in ((pG, HIDF), (pA, 0)):
                        for kc in range(KC):
                            for i, (pw, px) in enumerate(PARTS):
                                last = pe.matmul(bank[j % 2][0:r, :], W1p[pw][:, kc, off + j * P:off + j * P + r],
                                                 hT[px][:, kc], start=kc + i == 0, stop=kc == KC - 1 and i == 2)
                    last.then_inc(ag_mm, 1)
                if nxt:
                    turn(n + 1)
                pe.wait_ge(lo_done, (n + 1) * FT + 3)
                pe.wait_ge(y_done, n + 1)
                for s in range(SUB):
                    for j in range(FT):
                        r = rows(j)
                        for i, (ph, pw) in enumerate(PARTS):
                            last = pe.matmul(pO[s // 2][:, s % 2 * D:(s % 2 + 1) * D],
                                             hid[ph][0:r, j, s * P:(s + 1) * P], W2p[pw][0:r, j],
                                             start=j + i == 0, stop=j == FT - 1 and i == 2)
                last.then_inc(o_mm, 1)
            skewed(pe, turn, body)

        @block.scalar
        def _(act):
            act.wait_ge(c_in, 16 * NC_IN)
            act.wait_ge(eps_set, 2)

            act.activation(W1p[0][:], W1[:], ACT.Copy)
            for p_, f in W2_PIECES:
                last = act.activation(W2p[0][p_, f], W2[p_, f], ACT.Copy)
            last.then_inc(w_hi, 1)

            def deviation(n):
                act.wait_ge(var, n + 2)
                act.activation(sd[:], mv[:, :, 1], ACT.Sqrt, bias=eps[:]).then_inc(sdd, 1)

            def scaled(n):
                act.wait_ge(t_done, n + 2)
                act.wait_ge(ag_mm, n * FT + 1)
                for kc in range(KC):
                    for dst in (hT[0], hTf):
                        last = act.activation(dst[:, kc], pT[kc][:], ACT.Identity, bias=b_[:, kc:kc + 1],
                                              scale=g_[:, kc:kc + 1])
                last.then_inc(ht_hi, 1)

            def high(n, j):
                r = rows(j)
                act.wait_ge(hid_done, n * FT + j + 4)
                act.activation(hid[0][0:r, j], hidf[0:r, j % 2], ACT.Copy).then_inc(hi_done, 1)

            def first():
                deviation(0)
                scaled(0)

            def body(n, m, u, nxt):
                for j in range(FT):
                    r = rows(j)
                    act.wait_ge(ag_mm, n * FT + j + 2)
                    act.wait_ge(hid_done, n * FT + j + 2)
                    act.activation(gl[0:r, j % 2], pG[j % 2][0:r, :], ACT.Gelu, bias=bg[0:r, j:j + 1]
                                   ).then_inc(gl_done, 1)
                    if j == 0:
                        act.wait_ge(o_mm, n + 1)
                    else:
                        high(n, j - 1)
                    if nxt and j == 2:
                        deviation(n + 1)
                high(n, FT - 1)
                if nxt:
                    scaled(n + 1)
                if final:
                    act.wait_ge(var2, n + 2)
                    act.activation(sd2[:], mv2[:, :, 1], ACT.Sqrt, bias=eps[:]).then_inc(sdd2, 1)
                else:
                    act.wait_ge(x_done, n + 2)
                    act.activation(X[:, ds(n * SUB, SUB), :], y2[:, u], ACT.Copy).then_inc(xc, 1)
            skewed(act, lambda n: first(), body)

        @block.vector
        def _(dve):
            NL, OL = 2, (4 if final else 0)
            cn, co = Chain(dve, dch, NL), Chain(dve, och, OL)
            dve.wait_ge(c_in, 16 * NC_IN)
            dve.sem_inc(n_done, 1)
            if final:
                dve.sem_inc(x_free, 2)
            dve.sem_inc(hid_done, 2)

            dve.sem_inc(hi_done, 2)
            dve.sem_inc(lo_done, 2)
            dve.wait_ge(w_hi, 2)
            dve.tensor_tensor(W1p[1][:], W1[:], W1p[0][:].bitcast(F32), ALU.subtract)
            for p_, f in W2_PIECES:
                last = dve.tensor_tensor(W2p[1][p_, f], W2[p_, f], W2p[0][p_, f].bitcast(F32), ALU.subtract)
            last.then_inc(w_lo, 1)

            def stats(n, m, u):
                cn.start(n)
                dve.wait_ge(h_in[u], m * 32 + 32)
                for s in range(SUB):
                    last = dve.bn_stats(st[:, s], h[:, u, s])
                cn.link(last)
                dve.sem_inc(fence, 1)
                for s in range(SUB):
                    last = dve.bn_aggr(mv[:, s], st[:, s])
                last.then_inc(var, 1)

            def norm(n, m, u):
                dve.wait_ge(sdd, n + 2)
                cn.link(dve.reciprocal(rs[:], sd[:]))
                dve.wait_ge(t_done, n + 1)
                for s in range(SUB):
                    last = dve.tensor_scalar(hn[:, s], h[:, u, s], mv[:, s, 0:1], rs[:, s:s + 1], ALU.subtract, ALU.mult)
                last.then_inc(n_done, 1)
                cn.end()

            def turned_low(n):
                dve.wait_ge(ht_hi, n + 2)
                dve.tensor_tensor(hT[1][:], hTf[:], hT[0][:].bitcast(F32), ALU.subtract).then_inc(xt_done, 1)

            def low(n, j):
                r = rows(j)
                dve.wait_ge(hi_done, n * FT + j + 4)
                dve.tensor_tensor(hid[1][0:r, j], hidf[0:r, j % 2], hid[0][0:r, j].bitcast(F32), ALU.subtract
                                  ).then_inc(lo_done, 1)

            def first():
                stats(0, 0, 0)
                norm(0, 0, 0)
                turned_low(0)

            def body(n, m, u, nxt):
                for j in range(FT):
                    r = rows(j)
                    dve.wait_ge(gl_done, n * FT + j + 2)
                    dve.wait_ge(hi_done, n * FT + j + 2)
                    dve.wait_ge(lo_done, n * FT + j + 2)
                    dve.scalar_tensor_tensor(hidf[0:r, j % 2], pA[j % 2][0:r, :], ba[0:r, j:j + 1], gl[0:r, j % 2],
                                             ALU.add, ALU.mult).then_inc(hid_done, 1)
                    if j:
                        low(n, j - 1)
                    if nxt and j == 1:
                        stats(n + 1, m + u, 1 - u)
                    if nxt and j == 3:
                        norm(n + 1, m + u, 1 - u)
                low(n, FT - 1)
                if nxt:
                    turned_low(n + 1)
                co.start(n)
                dve.wait_ge(o_mm, n + 2)
                for k in range(2):
                    last = dve.tensor_tensor(y[:, 2 * k:2 * k + 2], pO[k][:].rearrange("p (s c) -> p s c", c=D),
                                             bb[:].unsqueeze(1).to_broadcast([P, 2, D]), ALU.add)
                last.then_inc(y_done, 1)
                dve.wait_ge(y_done, n + 2)
                dve.wait_ge(x_out[u], m * 16 + 1)
                if final:
                    co.link(dve.tensor_tensor(y[:], y[:], X[:, ds(n * SUB, SUB), :], ALU.add))
                    dve.wait_ge(x0_in[u], m * 16 + 16)
                    co.link(dve.tensor_tensor(y[:], y[:], x0[:, u], ALU.add))
                    for s in range(SUB):
                        last = dve.bn_stats(st2[:, s], y[:, s])
                    co.link(last)
                    dve.sem_inc(fence, 1)
                    for s in range(SUB):
                        last = dve.bn_aggr(mv2[:, s], st2[:, s])
                    last.then_inc(var2, 1)
                    dve.wait_ge(sdd2, n + 2)
                    co.link(dve.reciprocal(rs2[:], sd2[:]))
                    for s in range(SUB):
                        last = dve.tensor_scalar(y2[:, u, s], y[:, s], mv2[:, s, 0:1], rs2[:, s:s + 1], ALU.subtract,
                                                 ALU.mult)
                    last.then_inc(x_done, 1)
                    dve.drain().then_inc(x_free, 1)
                else:
                    dve.wait_ge(xc, n + 1)
                    dve.tensor_tensor(y2[:, u], y[:], X[:, ds(n * SUB, SUB), :], ALU.add).then_inc(x_done, 1)
                    co.end()
            skewed(dve, lambda n: first(), body)
            if not final:
                dve.wait_ge(xc, NCK + 1)

        @block.sync
        def _(sp):
            def body(n, b, c, m, u):
                sp.wait_ge(x_done, n + 2)
                if final:
                    dst = out[ds(n * CH, CH), :]
                else:
                    dst = xp_out[ds(b * PADS + c * CH + 1, CH), :]
                sp.dma_start(dst.rearrange("(s p) c -> p s c", p=P), y2[:, u]).then_inc(x_out[u], 16)
            chunks(sp, body)
            for u in range(2):
                sp.wait_ge(x_out[u], 16 * (NCK // 2) + 1)


def clear_buffers(nc, sem, ein, xps, kT, ve):
    WIDTH = E_ * ROWS * D // P
    CUT = 8
    with ExitStack() as ctx:
        z = ctx.enter_context(nc.sbuf_tensor("Z_z", [P, WIDTH // CUT], F32))
        zeroed, cleared = sem("Z_zeroed"), sem("Z_cleared")
        sem.start()
        block = ctx.enter_context(nc.Block())

        @block.vector
        def _(dve):
            dve.memset(z[:], 0.0).then_inc(zeroed, 1)

        @block.sync
        def _(sp):
            sp.wait_ge(zeroed, 2)
            flat = ein.rearrange("r c -> (r c)").rearrange("(p w) -> p w", p=P)
            n = 0
            for i in range(CUT):
                sp.dma_start(flat[:, i * (WIDTH // CUT):(i + 1) * (WIDTH // CUT)], z[:]).then_inc(cleared, 16)
                n += 1
            for b in range(B):
                for xp in xps:
                    sp.dma_start(xp[b * PADS:b * PADS + 1, :], z[0:1, 0:D]).then_inc(cleared, 16)
                    n += 1
                sp.dma_start(ve[b * PADW:b * PADW + P, :], z[:, 0:LH * VE]).then_inc(cleared, 16)
                sp.dma_start(kT[b * INNER:(b + 1) * INNER, 0:P].rearrange("(g p) t -> p g t", p=P),
                             z[:, 0:PAIRS * P].rearrange("p (g t) -> p g t", g=PAIRS)).then_inc(cleared, 16)
                n += 2
            sp.wait_ge(cleared, 16 * n + 1)


def build(nc, d, out):
    with ExitStack() as ctx:
        sem = Semaphores(nc)
        keep = lambda n, s, t=F32: ctx.enter_context(nc.sbuf_tensor(n, s, t))
        scratch = lambda n, s: nc.dram_tensor(n, s, F32).ap()
        inverse = scratch("inverse", (B * NH, S))
        X = keep("X", [P, NT, D])
        LG = keep("LG", [P, NT, E_])
        slot_s = keep("slot_s", [P, B, TOPK, S // P], U32)
        slot_g = keep("slot_g", [P, B, TOPK, S // P], U32)
        prob = keep("prob", [P, TOPK, NT])
        ein, eout = scratch("ein", (E_ * ROWS, D)), scratch("eout", (E_ * ROWS, D))
        xp = [scratch(f"xp{i}", (B * PADS, D)) for i in range(3)]
        lqT, lkT = scratch("lqT", (B * INNER, S)), scratch("lkT", (B * INNER, PADW))
        lve = scratch("lve", (B * PADW, LH * VE))
        m_rows = scratch("m_rows", (2, GRP * S))
        ot = scratch("ot", (NIT * P, S))

        clear_buffers(nc, sem, ein, xp, lkT, lve)
        qh, ql = scratch("qh0", (B * D, S)), scratch("ql0", (B * D, S))
        kh, kl = scratch("kh0", (B * NKV * HD, S)), scratch("kl0", (B * NKV * HD, S))
        vs = scratch("vs0", (NIT * S, VW))
        layer0_projections(nc, sem, d["xT"], d["a0_wqT"], d["a0_wkT"], d["a0_wvT"], qh, ql, kh, kl, vs)
        attention(nc, sem, "B_", 1, 1, qh, ql, kh, kl, vs, d["causal"], d["ident_bf"], d["ident"], m_rows, ot)
        attention_output(nc, sem, "C_", ot, d["a0_woT"], d["x"], X, d["ident"], (d["router_w"], d["router_b"], LG), None,
                         inverse)
        sem.clear()
        route(nc, sem, LG, d["tri"], d["iota8"], d["ones"], slot_s, slot_g, prob)
        experts(nc, sem, X, slot_s, ein, eout, d["w_fc"], d["b_fc"], d["w_gate"], d["b_gate"], d["w_proj"], d["b_proj"],
                d["ident"])
        qh1, ql1 = scratch("qh1", (B * D, S)), scratch("ql1", (B * D, S))
        kh1, kl1 = scratch("kh1", (B * D, S)), scratch("kl1", (B * D, S))
        vs1 = scratch("vs1", (NIT * S, GRP * VW))
        combine_and_project(nc, sem, X, eout, slot_g, prob, d["rope_cos"], d["rope_sin"], d["a1_wq"], d["a1_wqs"],
                            d["a1_wd"], d["a1_wk"], d["a1_wks"], d["a1_wv"], d["ident"], qh1, ql1, kh1, kl1, vs1)
        sem.clear()
        attention(nc, sem, "G_", GRP, PAGE, qh1, ql1, kh1, kl1, vs1, d["paged"], d["ident_bf"], d["ident"],
                  m_rows, ot)
        attention_output(nc, sem, "H_", ot, d["a1_wo"], None, X, d["ident"], None, xp[0], inverse)
        for l in range(2):
            sem.clear()
            local_projections(nc, sem, f"I{l}_", xp[0] if l == 0 else xp[2], d[f"l{l}_wqkv"], d["xpos"],
                              d[f"l{l}_scales"], d["ident"], lqT, lkT, lve)
            local_attention(nc, sem, f"J{l}_", lqT, lkT, lve, d[f"l{l}_wo"], d["windows"], d["ident_bf"], d["ident"],
                            X, xp[1])
            gated_unit(nc, sem, f"K{l}_", xp[1], d[f"l{l}_lng"], d[f"l{l}_lnb"], d[f"l{l}_w1"], d[f"l{l}_b1a"],
                       d[f"l{l}_b1g"], d[f"l{l}_w2"], d[f"l{l}_b2"], d["ident"], X, xp[2] if l == 0 else None,
                       xp[0], out if l else None)


def shape_constants():
    c = {}
    i = np.arange(P)
    c["ident"] = np.eye(P, dtype=np.float32)
    c["ones"] = np.ones((P, P), np.float32)
    c["tri"] = (i[:, None] <= i[None, :]).astype(np.float32)
    c["iota8"] = np.tile(np.arange(E_, dtype=np.float32), (P, 1))
    page = i // PAGE
    bf = mybir.dt.np(BF16)
    c["ident_bf"] = np.eye(P).astype(bf)
    causal = np.where(i[None, :] > i[:, None], NEG, 0.0)
    paged = np.where(page[None, :] > page[:, None], NEG, 0.0)
    for name, m in (("causal", causal), ("paged", paged)):
        c[name] = m.astype(bf)
    before = np.where(i[None, :] < i[:, None], NEG, 0.0)
    c["windows"] = np.concatenate([np.concatenate([before if t % WIN else np.full((P, P), NEG), causal], 1)
                                   for t in range(NT)]).astype(bf)
    inv = 1.0 / 10000.0 ** (np.arange(0, HD, 2, dtype=np.float32) / HD)
    ang = np.outer(np.arange(S, dtype=np.float32), inv)
    pair = i % HD // 2
    c["rope_cos"] = np.ascontiguousarray(np.cos(ang).T[pair]).astype(np.float32)
    sign = np.where(i % 2 == 0, -1.0, 1.0)[:, None]
    c["rope_sin"] = (np.sin(ang).T[pair] * sign).astype(np.float32)
    half = np.arange(0, LD, 2, dtype=np.float32)
    freq = np.arange(S, dtype=np.float32)[:, None] * (1.0 / 10000.0 ** (half / LD)).astype(np.float32)[None, :]
    freq = np.concatenate([freq, freq], -1)
    base = (half + np.float32(0.4 * LD)) / np.float32(1.4 * LD)
    power = (np.arange(S, dtype=np.float32) - S // 2) / np.float32(P // 2)
    scale = base[None, :] ** power[:, None]
    scale = np.concatenate([scale, scale], -1)
    sign = np.where(np.arange(LD) < LD // 2, -1.0, 1.0)
    cos, sin = np.cos(freq), np.sin(freq) * sign
    c["xpos"] = np.concatenate([cos * scale, sin * scale, cos / scale, sin / scale]).astype(np.float32)
    return c


def laid_out(v):
    a = {k: np.asarray(x) for k, x in v.items()}
    x = a["L0_attn_x"].reshape(TOK, D)
    d = {"x": x, "xT": x.T}
    for n in ("wq", "wk", "wv", "wo"):
        d[f"a0_{n}T"] = a[f"L0_attn_{n}"].T
    cols = lambda w: w.reshape(-1, P).T
    d["router_w"] = a["L0_ffn_router_w"]
    d["router_b"] = np.broadcast_to(a["L0_ffn_router_b"], (P, E_))
    d["w_fc"] = a["L0_ffn_w_c_fc"].reshape(E_ * D, HID_E)
    d["w_gate"] = a["L0_ffn_w_gate"].reshape(E_ * D, HID_E)
    d["w_proj"] = a["L0_ffn_w_c_proj"].reshape(E_ * HID_E, D)
    for n in ("fc", "gate"):
        b = a["L0_ffn_b_c_fc" if n == "fc" else "L0_ffn_b_gate"]
        d[f"b_{n}"] = b.reshape(E_, HT, P).transpose(0, 2, 1).reshape(E_ * P, HT)
    d["b_proj"] = a["L0_ffn_b_c_proj"].reshape(E_, D)
    swap = np.arange(D) ^ 1
    d["a1_wq"], d["a1_wqs"] = a["L1_attn_wq"], a["L1_attn_wq"][:, swap]
    d["a1_wk"], d["a1_wks"] = a["L1_attn_wk_up"], a["L1_attn_wk_up"][:, swap]
    d["a1_wd"], d["a1_wv"], d["a1_wo"] = a["L1_attn_w_down"], a["L1_attn_wv_up"], a["L1_attn_wo"]
    for l in range(2):
        g = lambda n: a["L1_ffn_" + n][l]
        d[f"l{l}_wqkv"], d[f"l{l}_wo"], d[f"l{l}_w1"], d[f"l{l}_w2"] = g("wqkv"), g("wo"), g("w1"), g("w2")
        d[f"l{l}_scales"] = np.concatenate([g("q_scale"), g("k_scale")]).reshape(1, 2 * LD)
        d[f"l{l}_lng"], d[f"l{l}_lnb"] = cols(g("ln_g")), cols(g("ln_b"))
        b1 = np.zeros((2, FT * P), np.float32)
        b1[:, :HIDF] = g("b1").reshape(2, HIDF)
        d[f"l{l}_b1a"], d[f"l{l}_b1g"] = cols(b1[0]), cols(b1[1])
        d[f"l{l}_b2"] = g("b2").reshape(1, D)
    return d


def kernel(**inputs):
    import concourse.bacc as bacc
    from concourse.bass_utils import run_bass_kernel_spmd

    nc = bacc.Bacc("TRN2", target_bir_lowering=False, num_devices=1)
    arrays = {f"in_{k}": np.ascontiguousarray(v) for k, v in {**laid_out(inputs), **shape_constants()}.items()}
    d = {k[3:]: nc.dram_tensor(k, v.shape, mybir.dt.from_np(v.dtype), kind="ExternalInput").ap()
         for k, v in arrays.items()}
    out = nc.dram_tensor("out_0", (TOK, D), F32, kind="ExternalOutput").ap()
    build(nc, d, out)
    r = run_bass_kernel_spmd(nc, [arrays], core_ids=[0])
    return r.results[0]["out_0"].reshape(B, S, D)
```
